# Optimizing a Trainium2 kernel written in Bass

```python
import numpy as np
import jax
import jax.numpy as jnp

def _softmax(x, axis=-1):
    return jax.nn.softmax(x, axis=axis)

def _gelu(x):
    return jax.nn.gelu(x, approximate=True)

def _silu(x):
    return jax.nn.silu(x)

def _sigmoid(x):
    return jax.nn.sigmoid(x)

def _layernorm(x, axis=-1, eps=1e-05):
    m = jnp.mean(x, axis=axis, keepdims=True)
    v = jnp.var(x, axis=axis, keepdims=True)
    return (x - m) / jnp.sqrt(v + eps)

def _scatter_add(tgt, idx, src, axis=0):
    return tgt.at[idx].add(src)

def _segment_sum(src, seg, n):
    return jax.ops.segment_sum(src, seg, n)
kernel_name = 'mk_audio_tower_d2_tok_audfeat512_r4_706cab'

def setup_inputs(seed: int=0):
    np.random.seed(seed)
    _w = jnp.asarray

    def _rec_inputs():
        import jax
        import jax.numpy as jnp
        _rk = jax.random.key(seed)
        x = -3.53888e-05 + 1.00021 * jax.random.normal(jax.random.fold_in(_rk, 1), (32, 125, 23), jnp.float32)
        return x
    x = _rec_inputs()

    def _L0_tok_setup():
        import jax, jax.numpy as jnp
        import numpy as np
        CONTEXT = 5
        DILATION = 1
        BN_EPS = 1e-05

        def _tdnn_forward(x, W, b, gamma, beta):
            B, T, D = x.shape
            L = T - (CONTEXT - 1) * DILATION
            frames = jnp.stack([jax.lax.dynamic_slice_in_dim(x, k * DILATION, L, axis=1) for k in range(CONTEXT)], axis=2)
            patches = frames.reshape(B, L, CONTEXT * D)
            y = jnp.einsum('blf,of->blo', patches, W) + b
            y = jax.nn.relu(y)
            mean = jnp.mean(y, axis=(0, 1))
            var = jnp.var(y, axis=(0, 1))
            y = (y - mean) * jax.lax.rsqrt(var + BN_EPS) * gamma + beta
            return y
        key = jax.random.key(seed)
        k1, k2, k3 = jax.random.split(key, 3)
        B, T, D, O = (64, 1024, 23, 128)
        x = jax.random.normal(k1, (B, T, D), dtype=jnp.float32)
        fan_in = D * CONTEXT
        bound = 1.0 / np.sqrt(fan_in)
        W = jax.random.uniform(k2, (O, fan_in), dtype=jnp.float32, minval=-bound, maxval=bound)
        b = jax.random.uniform(k3, (O,), dtype=jnp.float32, minval=-bound, maxval=bound)
        gamma = jnp.ones((O,), dtype=jnp.float32)
        beta = jnp.zeros((O,), dtype=jnp.float32)
        return {'x': x, 'W': W, 'b': b, 'gamma': gamma, 'beta': beta}
    _L0_tok_all = _L0_tok_setup()
    _L0_tok_in = {k: v for k, v in _L0_tok_all.items() if k in ('W', 'b', 'gamma', 'beta')}
    del _L0_tok_all

    def _L0_attn_setup():
        import jax, jax.numpy as jnp
        import numpy as np
        import math
        C = 128
        B, T = (8, 512)
        STRIDE = 2
        LN_EPS = 1e-05
        EPS = 1e-08

        def _ln(x, g, b):
            mu = jnp.mean(x, axis=-1, keepdims=True)
            var = jnp.mean(jnp.square(x - mu), axis=-1, keepdims=True)
            return (x - mu) * jax.lax.rsqrt(var + LN_EPS) * g + b

        def _lin(x, w, b):
            return jnp.einsum('btc,oc->bto', x, w) + b

        def _forward(x, dw, db, wq_cr, bq_cr, wk_cr, bk_cr, wv_cr, bv_cr, ln_cr_g, ln_cr_b, wq_d, bq_d, wk_d, bk_d, wv_d, bv_d, ln_d_g, ln_d_b, wq_c, bq_c, wk_c, bk_c, wv_c, bv_c, ln_c_g, ln_c_b, temp, gw, gb):
            scale = 1.0 / math.sqrt(C)
            xc = jnp.transpose(x, (0, 2, 1))
            xd = jax.lax.conv_general_dilated(xc, dw, window_strides=(STRIDE,), padding=[(1, 1)], dimension_numbers=('NCH', 'OIH', 'NCH')) + db[None, :, None]
            x_down = jnp.transpose(xd, (0, 2, 1))
            q = _lin(x, wq_cr, bq_cr)
            k = _lin(x_down, wk_cr, bk_cr)
            v = _lin(x_down, wv_cr, bv_cr)
            a = jax.nn.softmax(jnp.einsum('btc,bsc->bts', q, k) * scale, axis=-1)
            out_cross = _ln(jnp.einsum('bts,bsc->btc', a, v), ln_cr_g, ln_cr_b)
            q = _lin(x, wq_d, bq_d)
            k = _lin(x, wk_d, bk_d)
            v = _lin(x, wv_d, bv_d)
            a = jax.nn.softmax(jnp.einsum('btc,bsc->bts', q, k) * scale, axis=-1)
            out_dot = _ln(jnp.einsum('bts,bsc->btc', a, v), ln_d_g, ln_d_b)
            q = _lin(x, wq_c, bq_c)
            k = _lin(x, wk_c, bk_c)
            qn = q / (jnp.linalg.norm(q, axis=2, keepdims=True) + EPS)
            kn = k / (jnp.linalg.norm(k, axis=2, keepdims=True) + EPS)
            t = jnp.maximum(temp, 0.01)
            a = jax.nn.softmax(jnp.einsum('btc,bsc->bts', qn, kn) / t, axis=-1)
            v = _lin(x, wv_c, bv_c)
            out_cos = _ln(jnp.einsum('bts,bsc->btc', a, v), ln_c_g, ln_c_b)
            fused = jnp.concatenate([out_cross, out_dot, out_cos], axis=-1)
            gate = jax.nn.softmax(jnp.einsum('btc,gc->btg', fused, gw) + gb, axis=-1)
            z = gate[..., 0:1] * out_cross + gate[..., 1:2] * out_dot + gate[..., 2:3] * out_cos
            return z
        key = jax.random.key(seed)
        ks = iter(jax.random.split(key, 40))
        s = 0.02
        d = {'x': jax.random.normal(next(ks), (B, T, C), jnp.float32)}
        d['dw'] = jax.random.normal(next(ks), (C, C, 3), jnp.float32) * s
        d['db'] = jnp.zeros((C,), jnp.float32)
        for br in ('cr', 'd', 'c'):
            for p in ('q', 'k', 'v'):
                d[f'w{p}_{br}'] = jax.random.normal(next(ks), (C, C), jnp.float32) * s
                d[f'b{p}_{br}'] = jnp.zeros((C,), jnp.float32)
            d[f'ln_{br}_g'] = jnp.ones((C,), jnp.float32)
            d[f'ln_{br}_b'] = jnp.zeros((C,), jnp.float32)
        d['temp'] = jnp.asarray(0.1, jnp.float32)
        d['gw'] = jax.random.normal(next(ks), (3, 3 * C), jnp.float32) * s
        d['gb'] = jnp.zeros((3,), jnp.float32)
        return d
    _L0_attn_all = _L0_attn_setup()
    _L0_attn_in = {k: v for k, v in _L0_attn_all.items() if k in ('dw', 'db', 'wq_cr', 'bq_cr', 'wk_cr', 'bk_cr', 'wv_cr', 'bv_cr', 'ln_cr_g', 'ln_cr_b', 'wq_d', 'bq_d', 'wk_d', 'bk_d', 'wv_d', 'bv_d', 'ln_d_g', 'ln_d_b', 'wq_c', 'bq_c', 'wk_c', 'bk_c', 'wv_c', 'bv_c', 'ln_c_g', 'ln_c_b', 'temp', 'gw', 'gb')}
    del _L0_attn_all

    def _L0_ffn_setup():
        import jax, jax.numpy as jnp
        import numpy as np
        FP8_MAX = 448.0
        K, N = (128, 128)
        key = jax.random.key(seed)
        kx, kw = jax.random.split(key)
        x = jax.random.normal(kx, (8, 2048, K), dtype=jnp.float32)
        weight = jax.random.normal(kw, (K, N), dtype=jnp.float32) * 0.02
        return {'x': x, 'weight': weight}
    _L0_ffn_all = _L0_ffn_setup()
    _L0_ffn_in = {k: v for k, v in _L0_ffn_all.items() if k in ('weight',)}
    del _L0_ffn_all

    def _L1_attn_setup():
        import jax, jax.numpy as jnp
        import numpy as np
        D_MODEL = 128
        D_STATE = 16
        EXPAND = 2
        CONV = 4
        DEPTH = 5
        D_INNER = EXPAND * D_MODEL
        DT_RANK = D_MODEL // 16
        B = 4
        L = 256

        def _ln(x, g, b, eps=1e-05):
            m = jnp.mean(x, -1, keepdims=True)
            v = jnp.var(x, -1, keepdims=True)
            return (x - m) * jax.lax.rsqrt(v + eps) * g + b

        def _mamba(x, in_w, conv_w, conv_b, xproj_w, dtproj_w, dtproj_b, A_log, D_skip, out_w):
            Bsz, Ls, _ = x.shape
            xz = x @ in_w.T
            xin, z = jnp.split(xz, 2, axis=-1)
            xp = jnp.pad(xin, ((0, 0), (CONV - 1, 0), (0, 0)))
            xc = conv_b + sum((conv_w[:, k] * xp[:, k:k + Ls, :] for k in range(CONV)))
            xc = jax.nn.silu(xc)
            dbl = xc @ xproj_w.T
            dtr = dbl[..., :DT_RANK]
            Bs = dbl[..., DT_RANK:DT_RANK + D_STATE]
            Cs = dbl[..., DT_RANK + D_STATE:]
            dt = jax.nn.softplus(dtr @ dtproj_w.T + dtproj_b)
            A = -jnp.exp(A_log)
            dA = jnp.exp(dt[..., None] * A)
            dBx = dt[..., None] * Bs[:, :, None, :] * xc[..., None]

            def step(h, inp):
                dA_t, dBx_t, C_t = inp
                h = dA_t * h + dBx_t
                return (h, jnp.einsum('bds,bs->bd', h, C_t))
            h0 = jnp.zeros((Bsz, D_INNER, D_STATE), x.dtype)
            xs = (jnp.swapaxes(dA, 0, 1), jnp.swapaxes(dBx, 0, 1), jnp.swapaxes(Cs, 0, 1))
            _, ys = jax.lax.scan(step, h0, xs)
            y = jnp.swapaxes(ys, 0, 1) + D_skip * xc
            y = y * jax.nn.silu(z)
            return y @ out_w.T
        key = jax.random.key(seed)
        ks = jax.random.split(key, 10)

        def w(k, shape, fan_in):
            return jax.random.normal(k, shape, jnp.float32) / np.float32(np.sqrt(fan_in))
        inp = {}
        inp['x'] = jax.random.normal(ks[0], (B, L, D_MODEL), jnp.float32)
        inp['ln1_g'] = jnp.ones((DEPTH, D_MODEL), jnp.float32)
        inp['ln1_b'] = jnp.zeros((DEPTH, D_MODEL), jnp.float32)
        inp['in_w'] = w(ks[1], (DEPTH, 2 * D_INNER, D_MODEL), D_MODEL)
        inp['conv_w'] = w(ks[2], (DEPTH, D_INNER, CONV), CONV)
        inp['conv_b'] = jnp.zeros((DEPTH, D_INNER), jnp.float32)
        inp['xproj_w'] = w(ks[3], (DEPTH, DT_RANK + 2 * D_STATE, D_INNER), D_INNER)
        inp['dtproj_w'] = w(ks[4], (DEPTH, D_INNER, DT_RANK), DT_RANK)
        inp['dtproj_b'] = jnp.full((DEPTH, D_INNER), -4.0, jnp.float32)
        A = jnp.tile(jnp.arange(1, D_STATE + 1, dtype=jnp.float32), (DEPTH, D_INNER, 1))
        inp['A_log'] = jnp.log(A)
        inp['D_skip'] = jnp.ones((DEPTH, D_INNER), jnp.float32)
        inp['out_w'] = w(ks[5], (DEPTH, D_MODEL, D_INNER), D_INNER)
        inp['ln2_g'] = jnp.ones((DEPTH, D_MODEL), jnp.float32)
        inp['ln2_b'] = jnp.zeros((DEPTH, D_MODEL), jnp.float32)
        inp['mlp_w1'] = w(ks[6], (DEPTH, 2 * D_MODEL, D_MODEL), D_MODEL)
        inp['mlp_b1'] = jnp.zeros((DEPTH, 2 * D_MODEL), jnp.float32)
        inp['mlp_w2'] = w(ks[7], (DEPTH, D_MODEL, 2 * D_MODEL), 2 * D_MODEL)
        inp['mlp_b2'] = jnp.zeros((DEPTH, D_MODEL), jnp.float32)
        return inp
    _L1_attn_all = _L1_attn_setup()
    _L1_attn_in = {k: v for k, v in _L1_attn_all.items() if k in ('ln1_g', 'ln1_b', 'in_w', 'conv_w', 'conv_b', 'xproj_w', 'dtproj_w', 'dtproj_b', 'A_log', 'D_skip', 'out_w', 'ln2_g', 'ln2_b', 'mlp_w1', 'mlp_b1', 'mlp_w2', 'mlp_b2')}
    del _L1_attn_all

    def _L1_ffn_setup():
        import jax, jax.numpy as jnp
        import numpy as np
        D, NH, HID, E = (128, 8, 512, 8)
        EPS = 1e-05

        def _layernorm(x, g, b):
            mu = jnp.mean(x, axis=-1, keepdims=True)
            var = jnp.mean(jnp.square(x - mu), axis=-1, keepdims=True)
            return (x - mu) * jax.lax.rsqrt(var + EPS) * g + b
        key = jax.random.key(seed)
        ks = jax.random.split(key, 20)
        s = 0.02
        inp = {'x': jax.random.normal(ks[0], (4, 256, D), jnp.float32), 'Wq': jax.random.normal(ks[1], (D, D), jnp.float32) * s, 'bq': jnp.zeros((D,), jnp.float32), 'Wk': jax.random.normal(ks[2], (D, D), jnp.float32) * s, 'bk': jnp.zeros((D,), jnp.float32), 'Wv': jax.random.normal(ks[3], (D, D), jnp.float32) * s, 'bv': jnp.zeros((D,), jnp.float32), 'Wo': jax.random.normal(ks[4], (D, D), jnp.float32) * s, 'bo': jnp.zeros((D,), jnp.float32), 'g1': jnp.ones((D,), jnp.float32), 'beta1': jnp.zeros((D,), jnp.float32), 'g2': jnp.ones((D,), jnp.float32), 'beta2': jnp.zeros((D,), jnp.float32), 'Wg': jax.random.normal(ks[5], (D, E), jnp.float32) * s, 'bg': jnp.zeros((E,), jnp.float32), 'W1': jax.random.normal(ks[6], (E, D, HID), jnp.float32) * s, 'b1': jnp.zeros((E, HID), jnp.float32), 'W2': jax.random.normal(ks[7], (E, HID, D), jnp.float32) * s, 'b2': jnp.zeros((E, D), jnp.float32)}
        return inp
    _L1_ffn_all = _L1_ffn_setup()
    _L1_ffn_in = {k: v for k, v in _L1_ffn_all.items() if k in ('Wq', 'bq', 'Wk', 'bk', 'Wv', 'bv', 'Wo', 'bo', 'g1', 'beta1', 'g2', 'beta2', 'Wg', 'bg', 'W1', 'b1', 'W2', 'b2')}
    del _L1_ffn_all
    return {'x': x, 'L0_tok_W': _L0_tok_in['W'], 'L0_tok_b': _L0_tok_in['b'], 'L0_tok_gamma': _L0_tok_in['gamma'], 'L0_tok_beta': _L0_tok_in['beta'], 'L0_attn_dw': _L0_attn_in['dw'], 'L0_attn_db': _L0_attn_in['db'], 'L0_attn_wq_cr': _L0_attn_in['wq_cr'], 'L0_attn_bq_cr': _L0_attn_in['bq_cr'], 'L0_attn_wk_cr': _L0_attn_in['wk_cr'], 'L0_attn_bk_cr': _L0_attn_in['bk_cr'], 'L0_attn_wv_cr': _L0_attn_in['wv_cr'], 'L0_attn_bv_cr': _L0_attn_in['bv_cr'], 'L0_attn_ln_cr_g': _L0_attn_in['ln_cr_g'], 'L0_attn_ln_cr_b': _L0_attn_in['ln_cr_b'], 'L0_attn_wq_d': _L0_attn_in['wq_d'], 'L0_attn_bq_d': _L0_attn_in['bq_d'], 'L0_attn_wk_d': _L0_attn_in['wk_d'], 'L0_attn_bk_d': _L0_attn_in['bk_d'], 'L0_attn_wv_d': _L0_attn_in['wv_d'], 'L0_attn_bv_d': _L0_attn_in['bv_d'], 'L0_attn_ln_d_g': _L0_attn_in['ln_d_g'], 'L0_attn_ln_d_b': _L0_attn_in['ln_d_b'], 'L0_attn_wq_c': _L0_attn_in['wq_c'], 'L0_attn_bq_c': _L0_attn_in['bq_c'], 'L0_attn_wk_c': _L0_attn_in['wk_c'], 'L0_attn_bk_c': _L0_attn_in['bk_c'], 'L0_attn_wv_c': _L0_attn_in['wv_c'], 'L0_attn_bv_c': _L0_attn_in['bv_c'], 'L0_attn_ln_c_g': _L0_attn_in['ln_c_g'], 'L0_attn_ln_c_b': _L0_attn_in['ln_c_b'], 'L0_attn_temp': _L0_attn_in['temp'], 'L0_attn_gw': _L0_attn_in['gw'], 'L0_attn_gb': _L0_attn_in['gb'], 'L0_ffn_weight': _L0_ffn_in['weight'], 'L1_attn_ln1_g': _L1_attn_in['ln1_g'], 'L1_attn_ln1_b': _L1_attn_in['ln1_b'], 'L1_attn_in_w': _L1_attn_in['in_w'], 'L1_attn_conv_w': _L1_attn_in['conv_w'], 'L1_attn_conv_b': _L1_attn_in['conv_b'], 'L1_attn_xproj_w': _L1_attn_in['xproj_w'], 'L1_attn_dtproj_w': _L1_attn_in['dtproj_w'], 'L1_attn_dtproj_b': _L1_attn_in['dtproj_b'], 'L1_attn_A_log': _L1_attn_in['A_log'], 'L1_attn_D_skip': _L1_attn_in['D_skip'], 'L1_attn_out_w': _L1_attn_in['out_w'], 'L1_attn_ln2_g': _L1_attn_in['ln2_g'], 'L1_attn_ln2_b': _L1_attn_in['ln2_b'], 'L1_attn_mlp_w1': _L1_attn_in['mlp_w1'], 'L1_attn_mlp_b1': _L1_attn_in['mlp_b1'], 'L1_attn_mlp_w2': _L1_attn_in['mlp_w2'], 'L1_attn_mlp_b2': _L1_attn_in['mlp_b2'], 'L1_ffn_Wq': _L1_ffn_in['Wq'], 'L1_ffn_bq': _L1_ffn_in['bq'], 'L1_ffn_Wk': _L1_ffn_in['Wk'], 'L1_ffn_bk': _L1_ffn_in['bk'], 'L1_ffn_Wv': _L1_ffn_in['Wv'], 'L1_ffn_bv': _L1_ffn_in['bv'], 'L1_ffn_Wo': _L1_ffn_in['Wo'], 'L1_ffn_bo': _L1_ffn_in['bo'], 'L1_ffn_g1': _L1_ffn_in['g1'], 'L1_ffn_beta1': _L1_ffn_in['beta1'], 'L1_ffn_g2': _L1_ffn_in['g2'], 'L1_ffn_beta2': _L1_ffn_in['beta2'], 'L1_ffn_Wg': _L1_ffn_in['Wg'], 'L1_ffn_bg': _L1_ffn_in['bg'], 'L1_ffn_W1': _L1_ffn_in['W1'], 'L1_ffn_b1': _L1_ffn_in['b1'], 'L1_ffn_W2': _L1_ffn_in['W2'], 'L1_ffn_b2': _L1_ffn_in['b2']}

def reference(x, L0_tok_W, L0_tok_b, L0_tok_gamma, L0_tok_beta, L0_attn_dw, L0_attn_db, L0_attn_wq_cr, L0_attn_bq_cr, L0_attn_wk_cr, L0_attn_bk_cr, L0_attn_wv_cr, L0_attn_bv_cr, L0_attn_ln_cr_g, L0_attn_ln_cr_b, L0_attn_wq_d, L0_attn_bq_d, L0_attn_wk_d, L0_attn_bk_d, L0_attn_wv_d, L0_attn_bv_d, L0_attn_ln_d_g, L0_attn_ln_d_b, L0_attn_wq_c, L0_attn_bq_c, L0_attn_wk_c, L0_attn_bk_c, L0_attn_wv_c, L0_attn_bv_c, L0_attn_ln_c_g, L0_attn_ln_c_b, L0_attn_temp, L0_attn_gw, L0_attn_gb, L0_ffn_weight, L1_attn_ln1_g, L1_attn_ln1_b, L1_attn_in_w, L1_attn_conv_w, L1_attn_conv_b, L1_attn_xproj_w, L1_attn_dtproj_w, L1_attn_dtproj_b, L1_attn_A_log, L1_attn_D_skip, L1_attn_out_w, L1_attn_ln2_g, L1_attn_ln2_b, L1_attn_mlp_w1, L1_attn_mlp_b1, L1_attn_mlp_w2, L1_attn_mlp_b2, L1_ffn_Wq, L1_ffn_bq, L1_ffn_Wk, L1_ffn_bk, L1_ffn_Wv, L1_ffn_bv, L1_ffn_Wo, L1_ffn_bo, L1_ffn_g1, L1_ffn_beta1, L1_ffn_g2, L1_ffn_beta2, L1_ffn_Wg, L1_ffn_bg, L1_ffn_W1, L1_ffn_b1, L1_ffn_W2, L1_ffn_b2):
    import jax
    import jax.numpy as jnp

    def _L0_tok_ref(x, W, b, gamma, beta):
        import jax, jax.numpy as jnp
        import numpy as np
        CONTEXT = 5
        DILATION = 1
        BN_EPS = 1e-05

        def _tdnn_forward(x, W, b, gamma, beta):
            B, T, D = x.shape
            L = T - (CONTEXT - 1) * DILATION
            frames = jnp.stack([jax.lax.dynamic_slice_in_dim(x, k * DILATION, L, axis=1) for k in range(CONTEXT)], axis=2)
            patches = frames.reshape(B, L, CONTEXT * D)
            y = jnp.einsum('blf,of->blo', patches, W) + b
            y = jax.nn.relu(y)
            mean = jnp.mean(y, axis=(0, 1))
            var = jnp.var(y, axis=(0, 1))
            y = (y - mean) * jax.lax.rsqrt(var + BN_EPS) * gamma + beta
            return y
        return _tdnn_forward(x, W, b, gamma, beta)

    def _L0_attn_ref(x, dw, db, wq_cr, bq_cr, wk_cr, bk_cr, wv_cr, bv_cr, ln_cr_g, ln_cr_b, wq_d, bq_d, wk_d, bk_d, wv_d, bv_d, ln_d_g, ln_d_b, wq_c, bq_c, wk_c, bk_c, wv_c, bv_c, ln_c_g, ln_c_b, temp, gw, gb):
        import jax, jax.numpy as jnp
        import numpy as np
        import math
        C = 128
        B, T = (8, 512)
        STRIDE = 2
        LN_EPS = 1e-05
        EPS = 1e-08

        def _ln(x, g, b):
            mu = jnp.mean(x, axis=-1, keepdims=True)
            var = jnp.mean(jnp.square(x - mu), axis=-1, keepdims=True)
            return (x - mu) * jax.lax.rsqrt(var + LN_EPS) * g + b

        def _lin(x, w, b):
            return jnp.einsum('btc,oc->bto', x, w) + b

        def _forward(x, dw, db, wq_cr, bq_cr, wk_cr, bk_cr, wv_cr, bv_cr, ln_cr_g, ln_cr_b, wq_d, bq_d, wk_d, bk_d, wv_d, bv_d, ln_d_g, ln_d_b, wq_c, bq_c, wk_c, bk_c, wv_c, bv_c, ln_c_g, ln_c_b, temp, gw, gb):
            scale = 1.0 / math.sqrt(C)
            xc = jnp.transpose(x, (0, 2, 1))
            xd = jax.lax.conv_general_dilated(xc, dw, window_strides=(STRIDE,), padding=[(1, 1)], dimension_numbers=('NCH', 'OIH', 'NCH')) + db[None, :, None]
            x_down = jnp.transpose(xd, (0, 2, 1))
            q = _lin(x, wq_cr, bq_cr)
            k = _lin(x_down, wk_cr, bk_cr)
            v = _lin(x_down, wv_cr, bv_cr)
            a = jax.nn.softmax(jnp.einsum('btc,bsc->bts', q, k) * scale, axis=-1)
            out_cross = _ln(jnp.einsum('bts,bsc->btc', a, v), ln_cr_g, ln_cr_b)
            q = _lin(x, wq_d, bq_d)
            k = _lin(x, wk_d, bk_d)
            v = _lin(x, wv_d, bv_d)
            a = jax.nn.softmax(jnp.einsum('btc,bsc->bts', q, k) * scale, axis=-1)
            out_dot = _ln(jnp.einsum('bts,bsc->btc', a, v), ln_d_g, ln_d_b)
            q = _lin(x, wq_c, bq_c)
            k = _lin(x, wk_c, bk_c)
            qn = q / (jnp.linalg.norm(q, axis=2, keepdims=True) + EPS)
            kn = k / (jnp.linalg.norm(k, axis=2, keepdims=True) + EPS)
            t = jnp.maximum(temp, 0.01)
            a = jax.nn.softmax(jnp.einsum('btc,bsc->bts', qn, kn) / t, axis=-1)
            v = _lin(x, wv_c, bv_c)
            out_cos = _ln(jnp.einsum('bts,bsc->btc', a, v), ln_c_g, ln_c_b)
            fused = jnp.concatenate([out_cross, out_dot, out_cos], axis=-1)
            gate = jax.nn.softmax(jnp.einsum('btc,gc->btg', fused, gw) + gb, axis=-1)
            z = gate[..., 0:1] * out_cross + gate[..., 1:2] * out_dot + gate[..., 2:3] * out_cos
            return z
        return _forward(x, dw, db, wq_cr, bq_cr, wk_cr, bk_cr, wv_cr, bv_cr, ln_cr_g, ln_cr_b, wq_d, bq_d, wk_d, bk_d, wv_d, bv_d, ln_d_g, ln_d_b, wq_c, bq_c, wk_c, bk_c, wv_c, bv_c, ln_c_g, ln_c_b, temp, gw, gb)

    def _L0_ffn_ref(x, weight):
        import jax, jax.numpy as jnp
        import numpy as np
        FP8_MAX = 448.0
        K, N = (128, 128)
        B, S, _ = x.shape
        x2d = x.reshape(-1, K)
        x_amax = jnp.max(jnp.abs(x2d))
        x_scale = FP8_MAX / jnp.maximum(x_amax, 1e-12)
        x_fp8 = jnp.clip(x2d * x_scale, -FP8_MAX, FP8_MAX).astype(jnp.float8_e4m3fn)
        w_amax = jnp.max(jnp.abs(weight))
        w_scale = FP8_MAX / jnp.maximum(w_amax, 1e-12)
        w_fp8 = jnp.clip(weight.T * w_scale, -FP8_MAX, FP8_MAX).astype(jnp.float8_e4m3fn)
        res = jnp.matmul(x_fp8.astype(jnp.float32), w_fp8.astype(jnp.float32).T)
        out = res * (1.0 / x_scale * (1.0 / w_scale))
        return out.reshape(B, S, N).astype(x.dtype)

    def _L1_attn_ref(x, ln1_g, ln1_b, in_w, conv_w, conv_b, xproj_w, dtproj_w, dtproj_b, A_log, D_skip, out_w, ln2_g, ln2_b, mlp_w1, mlp_b1, mlp_w2, mlp_b2):
        import jax, jax.numpy as jnp
        import numpy as np
        D_MODEL = 128
        D_STATE = 16
        EXPAND = 2
        CONV = 4
        DEPTH = 5
        D_INNER = EXPAND * D_MODEL
        DT_RANK = D_MODEL // 16
        B = 4
        L = 256

        def _ln(x, g, b, eps=1e-05):
            m = jnp.mean(x, -1, keepdims=True)
            v = jnp.var(x, -1, keepdims=True)
            return (x - m) * jax.lax.rsqrt(v + eps) * g + b

        def _mamba(x, in_w, conv_w, conv_b, xproj_w, dtproj_w, dtproj_b, A_log, D_skip, out_w):
            Bsz, Ls, _ = x.shape
            xz = x @ in_w.T
            xin, z = jnp.split(xz, 2, axis=-1)
            xp = jnp.pad(xin, ((0, 0), (CONV - 1, 0), (0, 0)))
            xc = conv_b + sum((conv_w[:, k] * xp[:, k:k + Ls, :] for k in range(CONV)))
            xc = jax.nn.silu(xc)
            dbl = xc @ xproj_w.T
            dtr = dbl[..., :DT_RANK]
            Bs = dbl[..., DT_RANK:DT_RANK + D_STATE]
            Cs = dbl[..., DT_RANK + D_STATE:]
            dt = jax.nn.softplus(dtr @ dtproj_w.T + dtproj_b)
            A = -jnp.exp(A_log)
            dA = jnp.exp(dt[..., None] * A)
            dBx = dt[..., None] * Bs[:, :, None, :] * xc[..., None]

            def step(h, inp):
                dA_t, dBx_t, C_t = inp
                h = dA_t * h + dBx_t
                return (h, jnp.einsum('bds,bs->bd', h, C_t))
            h0 = jnp.zeros((Bsz, D_INNER, D_STATE), x.dtype)
            xs = (jnp.swapaxes(dA, 0, 1), jnp.swapaxes(dBx, 0, 1), jnp.swapaxes(Cs, 0, 1))
            _, ys = jax.lax.scan(step, h0, xs)
            y = jnp.swapaxes(ys, 0, 1) + D_skip * xc
            y = y * jax.nn.silu(z)
            return y @ out_w.T
        for d in range(DEPTH):
            x = _mamba(_ln(x, ln1_g[d], ln1_b[d]), in_w[d], conv_w[d], conv_b[d], xproj_w[d], dtproj_w[d], dtproj_b[d], A_log[d], D_skip[d], out_w[d]) + x
            h = _ln(x, ln2_g[d], ln2_b[d])
            h = jax.nn.gelu(h @ mlp_w1[d].T + mlp_b1[d], approximate=False)
            x = h @ mlp_w2[d].T + mlp_b2[d] + x
        return x

    def _L1_ffn_ref(x, Wq, bq, Wk, bk, Wv, bv, Wo, bo, g1, beta1, g2, beta2, Wg, bg, W1, b1, W2, b2):
        import jax, jax.numpy as jnp
        import numpy as np
        D, NH, HID, E = (128, 8, 512, 8)
        EPS = 1e-05

        def _layernorm(x, g, b):
            mu = jnp.mean(x, axis=-1, keepdims=True)
            var = jnp.mean(jnp.square(x - mu), axis=-1, keepdims=True)
            return (x - mu) * jax.lax.rsqrt(var + EPS) * g + b
        B, S, _ = x.shape
        dh = D // NH
        q = (x @ Wq + bq).reshape(B, S, NH, dh)
        k = (x @ Wk + bk).reshape(B, S, NH, dh)
        v = (x @ Wv + bv).reshape(B, S, NH, dh)
        scores = jnp.einsum('bqhd,bkhd->bhqk', q, k) / jnp.sqrt(jnp.float32(dh)).astype(x.dtype)
        attn = jax.nn.softmax(scores, axis=-1)
        ctx = jnp.einsum('bhqk,bkhd->bqhd', attn, v).reshape(B, S, D)
        sa = ctx @ Wo + bo
        x = _layernorm(x + sa, g1, beta1)
        t = x.reshape(-1, D)
        logits = t @ Wg + bg
        idx = jnp.argmax(logits, axis=-1)
        h = jax.nn.gelu(jnp.einsum('td,edh->teh', t, W1) + b1, approximate=False)
        y = jnp.einsum('teh,ehd->ted', h, W2) + b2
        onehot = jax.nn.one_hot(idx, E, dtype=t.dtype)
        moe = jnp.einsum('ted,te->td', y, onehot).reshape(B, S, D)
        return _layernorm(x + moe, g2, beta2)
    h = _L0_tok_ref(x, L0_tok_W, L0_tok_b, L0_tok_gamma, L0_tok_beta)
    h = h + _L0_attn_ref(_layernorm(h, axis=-1), L0_attn_dw, L0_attn_db, L0_attn_wq_cr, L0_attn_bq_cr, L0_attn_wk_cr, L0_attn_bk_cr, L0_attn_wv_cr, L0_attn_bv_cr, L0_attn_ln_cr_g, L0_attn_ln_cr_b, L0_attn_wq_d, L0_attn_bq_d, L0_attn_wk_d, L0_attn_bk_d, L0_attn_wv_d, L0_attn_bv_d, L0_attn_ln_d_g, L0_attn_ln_d_b, L0_attn_wq_c, L0_attn_bq_c, L0_attn_wk_c, L0_attn_bk_c, L0_attn_wv_c, L0_attn_bv_c, L0_attn_ln_c_g, L0_attn_ln_c_b, L0_attn_temp, L0_attn_gw, L0_attn_gb)
    h = h + _L0_ffn_ref(_layernorm(h, axis=-1), L0_ffn_weight)
    h = h + _L1_attn_ref(_layernorm(h, axis=-1), L1_attn_ln1_g, L1_attn_ln1_b, L1_attn_in_w, L1_attn_conv_w, L1_attn_conv_b, L1_attn_xproj_w, L1_attn_dtproj_w, L1_attn_dtproj_b, L1_attn_A_log, L1_attn_D_skip, L1_attn_out_w, L1_attn_ln2_g, L1_attn_ln2_b, L1_attn_mlp_w1, L1_attn_mlp_b1, L1_attn_mlp_w2, L1_attn_mlp_b2)
    h = h + _L1_ffn_ref(_layernorm(h, axis=-1), L1_ffn_Wq, L1_ffn_bq, L1_ffn_Wk, L1_ffn_bk, L1_ffn_Wv, L1_ffn_bv, L1_ffn_Wo, L1_ffn_bo, L1_ffn_g1, L1_ffn_beta1, L1_ffn_g2, L1_ffn_beta2, L1_ffn_Wg, L1_ffn_bg, L1_ffn_W1, L1_ffn_b1, L1_ffn_W2, L1_ffn_b2)
    return h

_drawn_inputs = setup_inputs


def setup_inputs(seed=0):
    import zlib

    import numpy as np

    out = dict(_drawn_inputs(seed))
    spreads = {'L0_tok_gamma': (1.0, 0.2),
     'L0_tok_beta': (0.0, 0.1),
     'L0_attn_db': (0.0, 0.1),
     'L0_attn_bq_cr': (0.0, 0.8),
     'L0_attn_bk_cr': (0.0, 0.8),
     'L0_attn_bv_cr': (0.0, 0.1),
     'L0_attn_ln_cr_g': (1.0, 0.2),
     'L0_attn_ln_cr_b': (0.0, 0.1),
     'L0_attn_bq_d': (0.0, 0.8),
     'L0_attn_bk_d': (0.0, 0.8),
     'L0_attn_bv_d': (0.0, 0.1),
     'L0_attn_ln_d_g': (1.0, 0.2),
     'L0_attn_ln_d_b': (0.0, 0.313),
     'L0_attn_bq_c': (0.0, 0.1),
     'L0_attn_bk_c': (0.0, 0.665),
     'L0_attn_bv_c': (0.0, 0.1),
     'L0_attn_ln_c_g': (1.0, 0.2),
     'L0_attn_ln_c_b': (0.0, 0.1),
     'L0_attn_gb': (0.0, 0.1),
     'L1_attn_ln1_g': (1.0, 0.2),
     'L1_attn_ln1_b': (0.0, 0.1),
     'L1_attn_conv_b': (0.0, 0.1),
     'L1_attn_dtproj_b': (-4.0, 0.2),
     'L1_attn_D_skip': (1.0, 0.2),
     'L1_attn_ln2_g': (1.0, 0.2),
     'L1_attn_ln2_b': (0.0, 0.1),
     'L1_attn_mlp_b1': (0.0, 0.1),
     'L1_attn_mlp_b2': (0.0, 0.1),
     'L1_ffn_bq': (0.0, 0.8),
     'L1_ffn_bk': (0.0, 0.8),
     'L1_ffn_bv': (0.0, 0.8),
     'L1_ffn_bo': (0.0, 0.287),
     'L1_ffn_g1': (1.0, 0.2),
     'L1_ffn_beta1': (0.0, 0.29),
     'L1_ffn_g2': (1.0, 0.2),
     'L1_ffn_beta2': (0.0, 0.31),
     'L1_ffn_bg': (0.0, 0.406),
     'L1_ffn_b1': (0.0, 0.8),
     'L1_ffn_b2': (0.0, 0.311)}
    factors = {'L0_attn_wq_cr': 8.0,
     'L0_attn_wk_cr': 8.0,
     'L0_attn_wq_d': 8.0,
     'L0_attn_wk_d': 8.0,
     'L1_ffn_Wq': 8.0,
     'L1_ffn_Wk': 8.0,
     'L1_ffn_Wv': 6.145,
     'L1_ffn_Wo': 6.582,
     'L1_ffn_W1': 4.03,
     'L1_ffn_W2': 3.664}
    for name, (base, spread) in spreads.items():
        noise = np.random.default_rng([zlib.crc32(name.encode()), seed]).standard_normal(out[name].shape)
        drawn = base * np.exp(spread * noise) if base else spread * noise
        out[name] = jnp.asarray(drawn.astype(out[name].dtype))
    for name, factor in factors.items():
        out[name] = (out[name] * factor).astype(out[name].dtype)
    return out
```

```python
from contextlib import ExitStack

import concourse.bass as bass
from concourse import mybir

F32 = mybir.dt.float32
BF16 = mybir.dt.bfloat16
U32 = mybir.dt.uint32
ALU = mybir.AluOpType
ACT = mybir.ActivationFunctionType
AX = mybir.AxisListType

P = 128
B, T_IN, D_IN = 32, 125, 23
CONTEXT = 5
T = T_IN - CONTEXT + 1
GB = 4
G = B // GB
N = GB * T
BANK = 512
TD = (T + 2 - 3) // 2 + 1
FK = CONTEXT * D_IN
EPS = 1e-5
LAYERS = 5
STATES = 16
RANK = 8
HEADS, DH = 8, 16
EXPERTS, HID = 8, 512
FP8_MAX = 448.0

COLS = ["tok_b", "tok_gamma", "tok_beta", "db", "bq_cr", "bk_cr", "bq_d", "bk_d", "bq_c", "bk_c",
        "bq", "bk", "bv", "bo", "g1", "beta1", "g2", "beta2"]
COL = {n: i for i, n in enumerate(COLS)}
MATS = ["dw0", "dw1", "dw2", "wq_cr", "wk_cr", "wv_cr", "wq_d", "wk_d", "wq_c", "wk_c", "wv_d", "wv_c", "ffn",
        "Wq", "Wk", "Wv", "Wo"]
MAT = {n: i for i, n in enumerate(MATS)}
ROWS = [("bv", 384), ("ln_g", 384), ("ln_b", 384), ("gw", 1152), ("gb", 3), ("temp", 1), ("bg", EXPERTS),
        ("places", EXPERTS), ("scales", 3)]
ROW = {}
for _n, _k in ROWS:
    ROW[_n] = (sum(v[1] - v[0] for v in ROW.values()), sum(v[1] - v[0] for v in ROW.values()) + _k)
ROW_ALL = sum(k for _, k in ROWS)
LW = {}
for _n, _k in [("ln1_g", 1), ("ln1_b", 1), ("in_w", 512), ("conv_w", 8), ("conv_b", 2), ("xproj", 256),
               ("dtproj", 256), ("A_log", 32), ("D_skip", 2), ("out_w", 256), ("ln2_g", 1), ("ln2_b", 1),
               ("w1", 256), ("b1", 2), ("w2", 256), ("b2", 1)]:
    LW[_n] = (sum(v[1] - v[0] for v in LW.values()), sum(v[1] - v[0] for v in LW.values()) + _k)
LW_ALL = max(v[1] for v in LW.values())


ARENA = 31500


class Count:

    def __init__(self, sem, per=1, credit=0):
        self.sem, self.per, self.credit = sem, per, credit

    def at(self, r, k=None):
        return self.credit + self.per * r + (self.per if k is None else k)


def audio_tower(nc, x_t, tok_w, cols_d, mats_d, rows_d, layers_d, w1_d, w2_d, moe_rows_d, wg_d, ident_d, selcol_d, out):
    with ExitStack() as ctx:
        def sb(name, shape, dt=F32):
            return ctx.enter_context(nc.sbuf_tensor(name, shape, dt))

        def count(name, per=1, credit=0):
            c = Count(ctx.enter_context(nc.semaphore(name)), per, credit)
            if credit:
                credits.append(c)
            return c

        arena = sb("arena", [P, ARENA])

        def stage():
            used = [0]

            def place(_, shape, dtype=F32):
                n = 1
                for k in shape[1:]:
                    n *= k
                words = n if dtype == F32 else (n + 1) // 2
                flat = arena[0:shape[0], used[0]:used[0] + words]
                used[0] += words
                assert used[0] <= ARENA
                if dtype != F32:
                    flat = flat.bitcast(dtype)
                if len(shape) == 2:
                    return flat
                names = "abcd"[:len(shape) - 1]
                return flat.rearrange("p (%s) -> p %s" % (" ".join(names), " ".join(names)),
                                      **dict(zip(names[1:], shape[2:])))
            return place

        credits = []
        ps = ctx.enter_context(nc.psum_tensor("ps", [P, 8, BANK], F32))

        def bank(k):
            return ps[:, k, 0:N]

        def bank4(k):
            return ps[:, k, 0:N].rearrange("p (b t) -> p b t", b=GB)

        cols = sb("cols", [P, len(COLS)])
        mats = sb("mats", [P, len(MATS), P])
        rows = sb("rows", [P, ROW_ALL])
        ident = sb("ident", [P, P])
        mean_w = sb("mean_w", [P, P])
        ones_w = sb("ones_w", [P, P])
        eps_c = sb("eps_c", [P, 1])

        def col(name):
            return cols[:, COL[name]:COL[name] + 1]

        def mat(name, k=1):
            return mats[:, MAT[name]:MAT[name] + k, :].rearrange("p a b -> p (a b)")

        def row(name, n=P):
            return rows[0:n, ROW[name][0]:ROW[name][1]]

        h = sb("h", [P, G, N])
        xs = sb("xs", [P, G, N])

        param = count("param")
        consts = count("consts")

        ln_mean = count("ln_mean")
        ln_cent = count("ln_cent")
        ln_square = count("ln_square")
        ln_var = count("ln_var")
        ln_log = count("ln_log", credit=1)
        ln_rstd = count("ln_rstd")
        cent = sb("cent", [P, N])
        rstd = sb("rstd", [P, N])
        LNB = 0

        def ln_pe(pe, u, src):
            pe.wait_ge(ln_log.sem, ln_log.at(u - 1))
            nc.tensor.matmul(bank(LNB), mean_w[:], src, start=True, stop=True).then_inc(ln_mean.sem, 1)
            pe.wait_ge(ln_square.sem, ln_square.at(u))
            nc.tensor.matmul(bank(LNB), mean_w[:], rstd[:], start=True, stop=True).then_inc(ln_var.sem, 1)

        def ln_act(act, u):
            act.wait_ge(ln_cent.sem, ln_cent.at(u))
            nc.scalar.activation(rstd[:], cent[:], ACT.Square).then_inc(ln_square.sem, 1)
            act.wait_ge(ln_var.sem, ln_var.at(u))
            nc.scalar.activation(rstd[:], bank(LNB), ACT.Ln, bias=eps_c[:]).then_inc(ln_log.sem, 1)
            act.wait_ge(ln_log.sem, ln_log.at(u))
            nc.scalar.activation(rstd[:], rstd[:], ACT.Exp, scale=-0.5).then_inc(ln_rstd.sem, 1)

        def ln_dve(dve, u, src):
            dve.wait_ge(ln_mean.sem, ln_mean.at(u))
            nc.vector.tensor_tensor(cent[:], src, bank(LNB), ALU.subtract).then_inc(ln_cent.sem, 1)
            dve.wait_ge(ln_rstd.sem, ln_rstd.at(u))

        tok_ws = sb("tok_ws", [FK, P])
        tok_mm = count("tok_mm")
        tok_y = count("tok_y")
        tok_stats = count("tok_stats", G)
        tok_norm = count("tok_norm")
        bn = sb("bn", [P, G, 6])
        bn_mv = sb("bn_mv", [P, 2])
        bn_sc = sb("bn_sc", [P, 4])
        bn_step = count("bn_step")
        frames_in = count("frames_in")
        h_tok = count("h_tok")

        att = stage()
        xp = att("xp", [P, GB, T + 2])
        xd = att("xd", [P, GB, TD])
        q_cr, q_d, q_c, k_d, k_c = (att(n, [P, GB, T]) for n in ("q_cr", "q_d", "q_c", "k_d", "k_c"))
        k_cr = att("k_cr", [P, GB, TD])
        v_dc = att("v_dc", [T, GB, 2 * P])
        v_cr = att("v_cr", [TD, GB, P])
        nq = att("nq", [P, 2, N])
        SC = TD + 2 * T
        prob = att("prob", [T, GB, SC])
        probT = att("probT", [T, GB, 3 * T])
        nmax = att("nmax", [T, GB, 3])
        nbias = att("nbias", [T, GB, 3])
        rsum = att("rsum", [T, GB, 3])
        rinv = att("rinv", [T, GB, 3])
        ao = att("ao", [T, GB, 3, P])
        ast = att("ast", [T, GB, 3, 6])
        amv = att("amv", [T, GB * 3, 2])
        ad = att("ad", [T, GB * 3])
        ars = att("ars", [T, GB * 3])
        junk = att("junk", [T, 3 * P])
        glog = att("glog", [T, GB, 3])
        gmx = att("gmx", [T, GB])
        z = att("z", [T, GB, P])
        rtemp = sb("rtemp", [P, 1])
        BR = [(0, TD), (TD, TD + T), (TD + T, SC)]
        KEYS = [TD, T, T]

        xn_ready = count("xn_ready")
        at_conv = count("at_conv")
        at_xd = count("at_xd")
        at_proj = count("at_proj", 5)
        at_kcr = count("at_kcr")
        at_q_act = count("at_q_act", 4)
        at_qc = count("at_qc")
        at_kcr_out = count("at_kcr_out")
        at_v = count("at_v", 3)
        at_v_out = count("at_v_out", 3)
        at_sq = count("at_sq", 2)
        at_ss = count("at_ss", 2)
        at_nrm = count("at_nrm", 2)
        at_nstep = count("at_nstep", 2)
        at_qkn = count("at_qkn", 2)
        at_score = count("at_score", GB)
        at_max = count("at_max", 2)
        at_bias = count("at_bias")
        at_exp = count("at_exp", GB)
        at_rinv = count("at_rinv")
        at_pt = count("at_pt", GB)
        at_pt_out = count("at_pt_out", GB)
        at_o = count("at_o", GB)
        at_on = count("at_on")
        at_st = count("at_st", 4)
        at_log = count("at_log")
        at_rstd = count("at_rstd")
        at_aff = count("at_aff", 3)
        at_logit = count("at_logit", 3 * GB)
        at_gate = count("at_gate", 3)
        at_gexp = count("at_gexp")
        at_gn = count("at_gn", 3)
        at_z = count("at_z", 3)
        at_zt = count("at_zt")
        h_attn = count("h_attn", credit=1)

        fx = count("fx", credit=0)
        f_max = count("f_max")
        f_gmax = count("f_gmax")
        f_step = count("f_step")
        f_q = count("f_q", 6)
        f_wq = count("f_wq")
        f_mm = count("f_mm")
        h_ffn = count("h_ffn")
        ffn = stage()
        famax = ffn("famax", [P, G + 1])
        f_wstep = count("f_wstep", 6)
        fpair = ffn("fpair", [P, 2])
        fall = ffn("fall", [P, 2])
        fsc = ffn("fsc", [P, 4])
        wq8 = ffn("wq8", [P, P], BF16)
        wtmp = ffn("wtmp", [P, 3, P])
        ftmp = ffn("ftmp", [P, 2, N])
        xq8 = ffn("xq8", [P, N], BF16)
        C2 = 2 * N
        PRE = ["ln1_g", "ln1_b", "in_w", "conv_w", "conv_b", "xproj", "dtproj"]
        POST = ["D_skip", "out_w", "ln2_g", "ln2_b", "w1", "b1", "w2", "b2"]
        PRE_N = LW["dtproj"][1]
        POST_0 = LW["D_skip"][0]
        wp = sb("wp", [P, PRE_N])
        wo = sb("wo", [P, LW_ALL - POST_0])

        def pw(name, lo=0, n=None):
            a, b = LW[name]
            return wp[:, a + lo:(b if n is None else a + lo + n)]

        def ow(name, lo=0, n=None):
            a, b = LW[name]
            return wo[:, a + lo - POST_0:(b if n is None else a + lo + n) - POST_0]

        nega = sb("nega", [P, LAYERS, 2 * STATES])
        selcol = sb("selcol", [P, 2 * STATES + HEADS + EXPERTS + 1])
        sel = sb("sel", [P, 2 * STATES, P], BF16)
        ssm = stage()
        LAG = 3
        DB = 4
        dt = ssm("dt", [P, 2, 2, N])
        u = ssm("u", [P, 2, 2, N])
        xc = ssm("xc", [P, 2, 2, N])
        sz = ssm("sz", [P, 2, 2, N])
        bc = ssm("bc", [P, 2, N], BF16)
        dA = ssm("dA", [P, DB, 2, N])
        db = ssm("db", [P, 2, 2, N])
        hs = ssm("hs", [P, DB, 2, N])
        cb = ssm("cb", [P, DB, N])
        gq = ssm("gq", [P, DB, 2, N])
        xn = ssm("xn", [P, N])
        sig_x = ssm("sig_x", [P, 2, N])
        sig_z = ssm("sig_z", [P, 2, N])
        spx = ssm("spx", [P, 2, N])
        drow = ssm("drow", [P, N])
        resid = ssm("resid", [P, N])
        yv = ssm("yv", [P, 2, N])
        xn2 = ssm("xn2", [P, N])
        gl = ssm("gl", [P, 2, N])
        LP, Y, BB, CC, L0 = LNB, 1, 3, 5, 6

        wp_in, wo_in = count("wp_in", 16), count("wo_in", 16)
        a_in = count("a_in", 16)
        sel_in = count("sel_in", 16)
        sel_made = count("sel_made")
        a_neg = count("a_neg", 2)
        x_in = count("x_in")
        p_xn = count("p_xn", 2)
        p_xin = count("p_xin")
        p_conv = count("p_conv", 5)
        p_sx = count("p_sx", 3)
        p_xc = count("p_xc")
        p_z = count("p_z")
        p_zc = count("p_zc")
        p_sz = count("p_sz", 3)
        p_silz = count("p_silz")
        p_xp = count("p_xp")
        p_bc = count("p_bc", 3)
        p_drow = count("p_drow")
        p_dtm = count("p_dtm")
        p_clip = count("p_clip", 2)
        p_sp = count("p_sp", 2)
        p_dt = count("p_dt")
        p_u = count("p_u")
        s_b = count("s_b", STATES)
        s_c = count("s_c", STATES)
        s_da = count("s_da", STATES)
        s_cb = count("s_cb", STATES, credit=2)
        s_db = count("s_db", STATES, credit=2)
        s_h = count("s_h", STATES, credit=DB)
        s_gq = count("s_gq", STATES, credit=DB)
        s_sum = count("s_sum", STATES, credit=DB)
        o_y = count("o_y", 1, credit=1)
        o_yg = count("o_yg")
        o_out = count("o_out")
        o_x = count("o_x")
        o_xn = count("o_xn", 2)
        o_m1 = count("o_m1")
        o_gl = count("o_gl")
        o_m2 = count("o_m2")
        o_x2 = count("o_x2", 1, credit=1)
        h_mamba = count("h_mamba")
        ROUNDS = LAYERS * G
        LN0 = 3 * G

        SLOT = dict(pre_mean=0, pre_cent=0, pre_square=1, pre_var=1, pre_rstd=2, pre_xn=2, in_x=2, conv=(3, 3, 4, 4),
                    floor=5, sig_x=(6, 6, 7), in_z=5, xc=7, zclip=7, xproj=7, drow=8, sig_z=(14, 14, 14), split=9,
                    dtproj=9, clip=10, softplus=(11, 11), silz=15, dt=12, u=13,
                    y=3, out=4, x=4, post_mean=5, post_cent=5, post_square=6, post_var=6, post_rstd=7, post_xn=8,
                    mlp1=11, gelu=12, mlp2=12, x2=13)

        def mamba_rounds(eng, body, post):
            body(0, 0, LN0 + 1, None)
            with eng.Fori(0, (ROUNDS - 2) // 2) as q:
                j = q * 2 + 1
                body(j, 1, j * 2 + LN0, j * 2 + (LN0 + 1))
                body(j + 1, 0, j * 2 + (LN0 + 2), j * 2 + (LN0 + 3))
            last = ROUNDS - 1
            body(last, last % 2, None, LN0 + 2 * last)
            post(last, last % 2, LN0 + 2 * last + 1)

        wg = sb("wg", [P, EXPERTS])
        moe_b = sb("moe_b", [EXPERTS, HID + P])
        last = stage()
        w1 = last("w1", [P, EXPERTS, HID])
        w2 = last("w2", [P, EXPERTS, HID // P, P])
        esel = last("esel", [P, EXPERTS, P], BF16)
        xe = last("xe", [P, N])
        qh = last("qh", [P, N])
        qm = last("qm", [P, HEADS, N])
        kh = last("kh", [P, N])
        vh = last("vh", [T, GB, P])
        mp_ = last("mp_", [T, 2, HEADS, T])
        mpT = last("mpT", [T, 2, HEADS, T])
        mmax = last("mmax", [T, 2, HEADS])
        msum = last("msum", [T, 2, HEADS])
        mctx = last("mctx", [T, GB, P])
        ctxT = last("ctxT", [P, N])
        r1 = last("r1", [P, N])
        x1 = last("x1", [P, N])
        lg = last("lg", [T, GB, EXPERTS])
        eq = last("eq", [T, GB, EXPERTS])
        lmx = last("lmx", [T, GB])
        ohT = last("ohT", [EXPERTS, N])
        ohb = last("ohb", [P, N], BF16)
        mask = last("mask", [P, EXPERTS, N])
        xm = last("xm", [P, 2, N])
        gh = last("gh", [P, HID // P, N])
        yt = last("yt", [P, 2, N])
        acc = last("acc", [P, N])
        moe_in = count("moe_in", 16)
        m_const = count("m_const")
        m_xe = count("m_xe")
        m_qk = count("m_qk", 3)
        m_qk_out = count("m_qk_out", 3)
        m_qm = count("m_qm")
        m_sc = count("m_sc", GB)
        m_mx = count("m_mx", 2 * GB)
        m_exp = count("m_exp", GB)
        m_ri = count("m_ri", GB)
        m_pt = count("m_pt", GB)
        m_pt_out = count("m_pt_out", GB, credit=2)
        m_ctx = count("m_ctx", GB)
        m_ctx_n = count("m_ctx_n", GB)
        m_ct = count("m_ct")
        m_ct_out = count("m_ct_out")
        m_sa = count("m_sa")
        m_r1 = count("m_r1")
        m_x1 = count("m_x1", 2)
        m_lg = count("m_lg")
        m_top = count("m_top", 6)
        m_oh = count("m_oh")
        m_oh_out = count("m_oh_out", 2)
        m_mask = count("m_mask", EXPERTS)
        m_mask_out = count("m_mask_out", EXPERTS, credit=2)
        m_xm = count("m_xm", EXPERTS, credit=2)
        m_hid_e = count("m_hid_e", EXPERTS, credit=2)
        m_hid = count("m_hid")
        m_gelu = count("m_gelu")
        m_b2 = count("m_b2")
        m_y = count("m_y", EXPERTS)
        m_yt = count("m_yt", EXPERTS, credit=2)
        m_acc = count("m_acc", EXPERTS + 1, credit=2)
        m_g2 = count("m_g2")
        h_out = count("h_out", 1, credit=1)
        LE = LN0 + 2 * ROUNDS

        out_done = count("out_done")

        block = ctx.enter_context(nc.Block())

        @block.sync
        def _(sp):
            for c in credits:
                sp.sem_inc(c.sem, c.credit)
            frames = xs[0:FK, :, :].rearrange("p g (b t) -> p (g b) t", b=GB)
            for k in range(CONTEXT):
                sp.dma_start(frames[k * D_IN:(k + 1) * D_IN, :, :], x_t[:, :, k:k + T]).then_inc(frames_in.sem, 16)
            sp.dma_start(tok_ws[:], tok_w).then_inc(frames_in.sem, 16)
            sp.dma_start(cols[:], cols_d).then_inc(frames_in.sem, 16)
            sp.dma_start(mats[:], mats_d).then_inc(param.sem, 16)
            sp.dma_start(ident[:], ident_d).then_inc(param.sem, 16)
            sp.dma_start(rows[:], rows_d.partition_broadcast(P)).then_inc(param.sem, 16)
            sp.dma_start(nega[:], layers_d[:, :, LW["A_log"][0]:LW["A_log"][1]].rearrange("l p c -> p l c"))\
                .then_inc(a_in.sem, 16)
            sp.dma_start(selcol[:], selcol_d).then_inc(sel_in.sem, 16)
            sp.dma_start(wp[:], layers_d[0, :, 0:PRE_N]).then_inc(wp_in.sem, 16)
            sp.dma_start(wo[:], layers_d[0, :, POST_0:LW_ALL]).then_inc(wo_in.sem, 16)
            with sp.Fori(1, LAYERS) as l:
                sp.wait_ge(p_dtm.sem, p_dtm.at(l * G - 1))
                sp.dma_start(wp[:], layers_d[bass.ds(l, 1), :, 0:PRE_N].squeeze(0)).then_inc(wp_in.sem, 16)
                sp.wait_ge(o_x2.sem, o_x2.at(l * G - 1))
                sp.dma_start(wo[:], layers_d[bass.ds(l, 1), :, POST_0:LW_ALL].squeeze(0)).then_inc(wo_in.sem, 16)
            sp.wait_ge(h_mamba.sem, h_mamba.at(G - 1))
            sp.dma_start(w1[:], w1_d).then_inc(moe_in.sem, 16)
            sp.dma_start(w2[:], w2_d).then_inc(moe_in.sem, 16)
            sp.dma_start(wg[:], wg_d).then_inc(moe_in.sem, 16)
            sp.dma_start(moe_b[:], moe_rows_d).then_inc(moe_in.sem, 16)
            with sp.Fori(0, G) as g:
                sp.wait_ge(h_out.sem, h_out.at(g))
                sp.dma_start(out[:, bass.ds(g, 1), :], h[:, bass.ds(g, 1), :]).then_inc(out_done.sem, 16)
            sp.wait_ge(out_done.sem, 16 * G)

        PARAM_ALL = 16 * 3
        FRAMES_ALL = 16 * (CONTEXT + 2)

        @block.tensor
        def _(pe):
            pe.wait_ge(frames_in.sem, FRAMES_ALL)
            with pe.Fori(0, G) as g:
                nc.tensor.matmul(ps[:, g, 0:N], tok_ws[:], xs[0:FK, g, :], start=True, stop=True)\
                    .then_inc(tok_mm.sem, 1)
            pe.wait_ge(consts.sem, 1)
            pe.wait_ge(param.sem, PARAM_ALL)
            pe.wait_ge(tok_y.sem, tok_y.at(G - 1))

            with pe.Fori(0, G) as g:
                pe.wait_ge(h_tok.sem, h_tok.at(g))
                pe.wait_ge(h_attn.sem, h_attn.at(g - 1))
                ln_pe(pe, g, h[:, g, :])
                pe.wait_ge(xn_ready.sem, xn_ready.at(g))
                for k in range(3):
                    mm = nc.tensor.matmul(ps[:, 1, 0:GB * TD], mat(f"dw{k}"), xp[:, :, k:k + 2 * TD - 1:2],
                                          start=(k == 0), stop=(k == 2))
                mm.then_inc(at_conv.sem, 1)
                for i, w in enumerate(("wq_cr", "wq_d", "wq_c", "wk_d", "wk_c")):
                    nc.tensor.matmul(bank(2 + i), mat(w), xp[:, :, 1:T + 1], start=True, stop=True)\
                        .then_inc(at_proj.sem, 1)
                for b in range(GB):
                    mm = nc.tensor.matmul(ps[0:T, (7, 0)[b // 2], 256 * (b % 2):256 * (b % 2) + 256],
                                          xp[:, b, 1:T + 1], mat("wv_d", 2), start=True, stop=True)
                    if b % 2:
                        mm.then_inc(at_v.sem, 1)
                pe.wait_ge(at_xd.sem, at_xd.at(g))
                nc.tensor.matmul(ps[:, 1, 0:GB * TD], mat("wk_cr"), xd[:], start=True, stop=True)\
                    .then_inc(at_kcr.sem, 1)
                pe.wait_ge(at_q_act.sem, at_q_act.at(g, 3))
                for b in range(GB):
                    mm = nc.tensor.matmul(ps[0:TD, 5, P * b:P * b + P], xd[:, b, :], mat("wv_cr"),
                                          start=True, stop=True)
                mm.then_inc(at_v.sem, 1)
                pe.wait_ge(at_qc.sem, at_qc.at(g))
                for k, i in enumerate((1, 0)):
                    pe.wait_ge(at_sq.sem, at_sq.at(g, k + 1))
                    nc.tensor.matmul(bank((4, 6)[i]), ones_w[:], nq[:, i, :], start=True, stop=True)\
                        .then_inc(at_ss.sem, 1)
                pe.wait_ge(at_kcr_out.sem, at_kcr_out.at(g))
                pe.wait_ge(at_qkn.sem, at_qkn.at(g))
                pe.wait_ge(at_v_out.sem, at_v_out.at(g))
                for b in range(GB):
                    for (lo, hi), q, k in zip(BR, (q_cr, q_d, q_c), (k_cr, k_d, k_c)):
                        mm = nc.tensor.matmul(ps[0:T, b, lo:hi], q[:, b, :], k[:, b, :], start=True, stop=True)
                    mm.then_inc(at_score.sem, 1)
                for b in range(GB):
                    pe.wait_ge(at_exp.sem, at_exp.at(g, b + 1))
                    for i in (1, 2, 0):
                        lo, hi = BR[i]
                        mm = nc.tensor.transpose(ps[0:KEYS[i], 4 + b, T * i:T * i + T], prob[:, b, lo:hi],
                                                 ident[0:T, 0:T])
                    mm.then_inc(at_pt.sem, 1)
                for b in range(GB):
                    pe.wait_ge(at_pt_out.sem, at_pt_out.at(g, b + 1))
                    for i in range(3):
                        v = v_cr[:, b, :] if i == 0 else v_dc[:, b, P * (i - 1):P * i]
                        mm = nc.tensor.matmul(ps[0:T, b, P * i:P * i + P], probT[0:KEYS[i], b, T * i:T * i + T], v,
                                              start=True, stop=True)
                    mm.then_inc(at_o.sem, 1)
                pe.wait_ge(at_z.sem, at_z.at(g))
                for b in range(GB):
                    mm = nc.tensor.transpose(ps[:, 4, T * b:T * b + T], z[:, b, :], ident[0:T, 0:T])
                mm.then_inc(at_zt.sem, 1)

            with pe.Fori(0, G) as g:
                ln_pe(pe, g + G, h[:, g, :])
            pe.wait_ge(f_wq.sem, 1)
            with pe.Fori(0, G) as g:
                pe.wait_ge(f_q.sem, f_q.at(g))
                nc.tensor.matmul(ps[:, g, 0:N], wq8[:], xq8[:], start=True, stop=True).then_inc(f_mm.sem, 1)
            with pe.Fori(0, G) as g:
                ln_pe(pe, g + 2 * G, h[:, g, :])

            def pe_norm_mean(uu, src):
                pe.wait_ge(ln_log.sem, ln_log.at(uu - 1))
                nc.tensor.matmul(bank(LNB), mean_w[:], src, start=True, stop=True).then_inc(ln_mean.sem, 1)

            def pe_norm_var(uu):
                pe.wait_ge(ln_square.sem, ln_square.at(uu))
                nc.tensor.matmul(bank(LNB), mean_w[:], rstd[:], start=True, stop=True).then_inc(ln_var.sem, 1)

            def pre_in_x(j, par):
                pe.wait_ge(p_xn.sem, p_xn.at(j))
                pe.wait_ge(wp_in.sem, wp_in.at(j // G))
                for i in range(2):
                    mm = nc.tensor.matmul(bank(L0 + i), pw("in_w", P * i, P), xn[:], start=True, stop=True)
                mm.then_inc(p_xin.sem, 1)

            def pre_in_z(j, par):
                pe.wait_ge(p_conv.sem, p_conv.at(j, 4))
                for i in range(2):
                    mm = nc.tensor.matmul(bank(L0 + i), pw("in_w", P * (2 + i), P), xn[:], start=True, stop=True)
                mm.then_inc(p_z.sem, 1)

            def pre_xproj(j, par):
                pe.wait_ge(p_xc.sem, p_xc.at(j))
                pe.wait_ge(p_zc.sem, p_zc.at(j))
                for i in range(2):
                    mm = nc.tensor.matmul(bank(L0), pw("xproj", P * i, P), xc[:, par, i, :],
                                          start=(i == 0), stop=(i == 1))
                mm.then_inc(p_xp.sem, 1)

            def pre_dtproj(j, par):
                pe.wait_ge(p_drow.sem, p_drow.at(j))
                pe.wait_ge(p_bc.sem, p_bc.at(j))
                for i in range(2):
                    mm = nc.tensor.matmul(bank(L0 + i), pw("dtproj", P * i, P), drow[:], start=True, stop=True)
                mm.then_inc(p_dtm.sem, 1)

            def scan_c(j, par, n):
                par, row = (par, n) if n < STATES else (1 - par, n - STATES)
                pe.wait_ge(s_cb.sem, s_cb.at(j, n))
                nc.tensor.matmul(bank(CC), sel[:, STATES + row, :], bc[:, par, :], start=True, stop=True)\
                    .then_inc(s_c.sem, 1)

            def scan_b(j, par, n):
                if n % STATES == 0:
                    pe.wait_ge(p_bc.sem, p_bc.at(j + n // STATES))
                par, row = (par, n) if n < STATES else (1 - par, n - STATES)
                pe.wait_ge(s_db.sem, s_db.at(j, n - 1))
                nc.tensor.matmul(bank(BB + n % 2), sel[:, row, :], bc[:, par, :], start=True, stop=True)\
                    .then_inc(s_b.sem, 1)

            def scan_sum(j, n):
                pe.wait_ge(s_gq.sem, s_gq.at(j, n + 1))
                if n == 0:
                    pe.wait_ge(o_y.sem, o_y.at(j - 1))
                for i in range(2):
                    mm = nc.tensor.matmul(bank(Y + i), ident[:], gq[:, n % DB, i, :],
                                          start=(n == 0), stop=(n % STATES == STATES - 1))
                mm.then_inc(s_sum.sem, 1)

            def post_out(j, uu):
                pe.wait_ge(ln_log.sem, ln_log.at(uu - 1))
                pe.wait_ge(o_yg.sem, o_yg.at(j))
                pe.wait_ge(wo_in.sem, wo_in.at(j // G))
                for i in range(2):
                    mm = nc.tensor.matmul(bank(LP), ow("out_w", P * i, P), yv[:, i, :], start=(i == 0), stop=(i == 1))
                mm.then_inc(o_out.sem, 1)

            def post_mlp1(j):
                pe.wait_ge(o_xn.sem, o_xn.at(j))
                for i in range(2):
                    mm = nc.tensor.matmul(bank(L0 + i), ow("w1", P * i, P), xn2[:], start=True, stop=True)
                mm.then_inc(o_m1.sem, 1)

            def post_mlp2(j):
                pe.wait_ge(o_gl.sem, o_gl.at(j))
                for i in range(2):
                    mm = nc.tensor.matmul(bank(LP), ow("w2", P * i, P), gl[:, i, :], start=(i == 0), stop=(i == 1))
                mm.then_inc(o_m2.sem, 1)

            def xgroup(j):
                return xs[:, j % G, :] if isinstance(j, int) else xs[:, bass.ds(j % G, 1), :].squeeze(1)

            def pe_round(j, par, u_pre, u_post):
                for n in range(STATES):
                    if n + 1 < STATES or u_pre is not None:
                        scan_c(j, par, n + 1)
                    if n + 2 < STATES or u_pre is not None:
                        scan_b(j, par, n + 2)
                    if n >= LAG or u_post is not None:
                        scan_sum(j, n - LAG)
                    if u_pre is not None:
                        if n == SLOT["pre_mean"]:
                            if u_post is not None:
                                pe.wait_ge(o_x2.sem, o_x2.at(j - 2))
                            pe_norm_mean(u_pre, xgroup(j + 1))
                        if n == SLOT["pre_var"]:
                            pe_norm_var(u_pre)
                        if n == SLOT["in_x"]:
                            pre_in_x(j + 1, 1 - par)
                        if n == SLOT["in_z"]:
                            pre_in_z(j + 1, 1 - par)
                        if n == SLOT["xproj"]:
                            pre_xproj(j + 1, 1 - par)
                        if n == SLOT["dtproj"]:
                            pre_dtproj(j + 1, 1 - par)
                    if u_post is not None:
                        if n == SLOT["out"]:
                            post_out(j - 1, u_post)
                        if n == SLOT["post_mean"]:
                            pe.wait_ge(o_x.sem, o_x.at(j - 1))
                            pe_norm_mean(u_post, resid[:])
                        if n == SLOT["post_var"]:
                            pe_norm_var(u_post)
                        if n == SLOT["mlp1"]:
                            if u_pre is not None:
                                pe.wait_ge(p_clip.sem, p_clip.at(j + 1))
                            post_mlp1(j - 1)
                        if n == SLOT["mlp2"]:
                            post_mlp2(j - 1)
                if u_pre is None:
                    for n in range(STATES - LAG, STATES):
                        scan_sum(j, n)

            def pe_post(j, par, uu):
                post_out(j, uu)
                pe.wait_ge(o_x.sem, o_x.at(j))
                pe_norm_mean(uu, resid[:])
                pe_norm_var(uu)
                post_mlp1(j)
                post_mlp2(j)

            pe.wait_ge(sel_made.sem, 1)
            pe.wait_ge(x_in.sem, x_in.at(G - 1))
            pe_norm_mean(LN0, xgroup(0))
            pe_norm_var(LN0)
            pre_in_x(0, 0)
            pre_in_z(0, 0)
            pre_xproj(0, 0)
            pre_dtproj(0, 0)
            scan_b(0, 0, 0)
            scan_c(0, 0, 0)
            scan_b(0, 0, 1)
            mamba_rounds(pe, pe_round, pe_post)
            pe.wait_ge(moe_in.sem, 64)
            pe.wait_ge(m_const.sem, 1)
            pe.wait_ge(h_mamba.sem, h_mamba.at(G - 1))
            with pe.Fori(0, G) as g:
                u0 = g * 3 + LE
                pe.wait_ge(h_out.sem, h_out.at(g - 1))
                pe_norm_mean(u0, h[:, g, :])
                pe_norm_var(u0)
                pe.wait_ge(m_xe.sem, m_xe.at(g))
                nc.tensor.matmul(bank(1), mat("Wq"), xe[:], start=True, stop=True).then_inc(m_qk.sem, 1)
                nc.tensor.matmul(bank(2), mat("Wk"), xe[:], start=True, stop=True).then_inc(m_qk.sem, 1)
                for b in range(GB):
                    mm = nc.tensor.matmul(ps[0:T, 3, P * b:P * b + P], xe[:, T * b:T * b + T], mat("Wv"),
                                          start=True, stop=True)
                mm.then_inc(m_qk.sem, 1)

                def scores(b):
                    pe.wait_ge(m_pt_out.sem, m_pt_out.at(g, b - 1))
                    for hd in range(HEADS):
                        bk = 4 + 2 * (b % 2) + hd // 4
                        mm = nc.tensor.matmul(ps[0:T, bk, T * (hd % 4):T * (hd % 4) + T], qm[:, hd, T * b:T * b + T],
                                              kh[:, T * b:T * b + T], start=True, stop=True)
                    mm.then_inc(m_sc.sem, 1)

                def transposes(b):
                    pe.wait_ge(m_exp.sem, m_exp.at(g, b + 1))
                    for hd in range(HEADS):
                        bk = 4 + 2 * (b % 2) + hd // 4
                        mm = nc.tensor.transpose(ps[0:T, bk, T * (hd % 4):T * (hd % 4) + T], mp_[:, b % 2, hd, :],
                                                 ident[0:T, 0:T])
                    mm.then_inc(m_pt.sem, 1)

                def context(b):
                    pe.wait_ge(m_pt_out.sem, m_pt_out.at(g, b + 1))
                    for hd in range(HEADS):
                        mm = nc.tensor.matmul(ps[0:T, 1, P * b + DH * hd:P * b + DH * hd + DH], mpT[:, b % 2, hd, :],
                                              vh[:, b, DH * hd:DH * hd + DH], start=True, stop=True)
                    mm.then_inc(m_ctx.sem, 1)

                pe.wait_ge(m_qk_out.sem, m_qk_out.at(g))
                pe.wait_ge(m_qm.sem, m_qm.at(g))
                scores(0)
                scores(1)
                for b in range(GB):
                    transposes(b)
                    if b:
                        context(b - 1)
                        if b + 1 < GB:
                            scores(b + 1)
                context(GB - 1)
                pe.wait_ge(m_ctx_n.sem, m_ctx_n.at(g))
                for b in range(GB):
                    mm = nc.tensor.transpose(ps[:, 2, T * b:T * b + T], mctx[:, b, :], ident[0:T, 0:T])
                mm.then_inc(m_ct.sem, 1)
                pe.wait_ge(m_ct_out.sem, m_ct_out.at(g))
                nc.tensor.matmul(bank(1), mat("Wo"), ctxT[:], start=True, stop=True).then_inc(m_sa.sem, 1)
                pe.wait_ge(m_r1.sem, m_r1.at(g))
                pe_norm_mean(u0 + 1, r1[:])
                pe_norm_var(u0 + 1)
                pe.wait_ge(m_x1.sem, m_x1.at(g))
                for b in range(GB):
                    mm = nc.tensor.matmul(ps[0:T, 3, EXPERTS * b:EXPERTS * b + EXPERTS], x1[:, T * b:T * b + T], wg[:],
                                          start=True, stop=True)
                mm.then_inc(m_lg.sem, 1)
                pe.wait_ge(m_top.sem, m_top.at(g))
                for b in range(GB):
                    mm = nc.tensor.matmul(ps[0:EXPERTS, 4, T * b:T * b + T], eq[:, b, :], ident[0:T, 0:T],
                                          start=True, stop=True)
                mm.then_inc(m_oh.sem, 1)
                pe.wait_ge(m_oh_out.sem, m_oh_out.at(g))

                def expert_mask(e):
                    pe.wait_ge(m_mask_out.sem, m_mask_out.at(g, e - 1))
                    nc.tensor.matmul(bank(5 + e % 2), esel[:, e, :], ohb[:], start=True, stop=True)\
                        .then_inc(m_mask.sem, 1)

                expert_mask(0)
                expert_mask(1)
                for c in range(HID // P):
                    nc.tensor.matmul(bank(c), moe_b[:, P * c:P * c + P], ohT[:], start=True, stop=False)
                nc.tensor.matmul(bank(7), moe_b[:, HID:HID + P], ohT[:], start=True, stop=True).then_inc(m_b2.sem, 1)
                for e in range(EXPERTS):
                    pe.wait_ge(m_xm.sem, m_xm.at(g, e + 1))
                    for c in range(HID // P):
                        mm = nc.tensor.matmul(bank(c), w1[:, e, P * c:P * c + P], xm[:, e % 2, :], start=False,
                                              stop=(e == EXPERTS - 1))
                    mm.then_inc(m_hid_e.sem, 1)
                    if e + 2 < EXPERTS:
                        expert_mask(e + 2)
                for e in range(EXPERTS):
                    if e == 0:
                        pe.wait_ge(m_gelu.sem, m_gelu.at(g))
                    pe.wait_ge(m_yt.sem, m_yt.at(g, e - 1))
                    for c in range(HID // P):
                        mm = nc.tensor.matmul(bank(4 + e % 2), w2[:, e, c, :], gh[:, c, :],
                                              start=(c == 0), stop=(c == HID // P - 1))
                    mm.then_inc(m_y.sem, 1)
                pe.wait_ge(m_acc.sem, m_acc.at(g))
                pe_norm_mean(u0 + 2, acc[:])
                pe_norm_var(u0 + 2)

        @block.scalar
        def _(act):
            act.wait_ge(consts.sem, 1)
            nc.scalar.preload_act_table_set("natural_log_exp_and_others")
            act.wait_ge(bn_step.sem, 1)
            nc.scalar.activation(bn_sc[:, 0:1], bn_mv[:, 1:2], ACT.Ln, bias=eps_c[:]).then_inc(bn_step.sem, 1)
            act.wait_ge(bn_step.sem, 2)
            nc.scalar.activation(bn_sc[:, 1:2], bn_sc[:, 0:1], ACT.Exp, scale=-0.5).then_inc(bn_step.sem, 1)

            act.wait_ge(param.sem, PARAM_ALL)
            with act.Fori(0, G) as g:
                ln_act(act, g)
                for i, (dst, b, k) in enumerate(((q_cr, "bq_cr", 1), (q_d, "bq_d", 2), (k_d, "bk_d", 4),
                                                 (k_c, "bk_c", 5))):
                    act.wait_ge(at_proj.sem, at_proj.at(g, k))
                    nc.scalar.activation(dst[:], bank4(k + 1), ACT.Identity, bias=col(b)).then_inc(at_q_act.sem, 1)
                act.wait_ge(at_q_act.sem, at_q_act.at(g))
                nc.scalar.activation(nq[:, 1, :], k_c[:].rearrange("p b t -> p (b t)"), ACT.Square)\
                    .then_inc(at_sq.sem, 1)
                act.wait_ge(at_qc.sem, at_qc.at(g))
                nc.scalar.activation(nq[:, 0, :], q_c[:].rearrange("p b t -> p (b t)"), ACT.Square)\
                    .then_inc(at_sq.sem, 1)
                for i in range(2):
                    act.wait_ge(at_v.sem, at_v.at(g, i + 1))
                    nc.scalar.copy(v_dc[:, 2 * i:2 * i + 2, :].rearrange("p b c -> p (b c)"), ps[0:T, (7, 0)[i], :])\
                        .then_inc(at_v_out.sem, 1)
                act.wait_ge(at_v.sem, at_v.at(g, 3))
                nc.scalar.copy(v_cr[:].rearrange("p b c -> p (b c)"), ps[0:TD, 5, :]).then_inc(at_v_out.sem, 1)
                for k, i in enumerate((1, 0)):
                    act.wait_ge(at_ss.sem, at_ss.at(g, k + 1))
                    nc.scalar.activation(nq[:, i, :], bank((4, 6)[i]), ACT.Sqrt).then_inc(at_nrm.sem, 1)
                nc.scalar.preload_act_table_set("natural_log_exp_and_others")
                act.wait_ge(at_bias.sem, at_bias.at(g))
                for b in range(GB):
                    for i, (lo, hi) in enumerate(BR):
                        a = nc.scalar.activation(prob[:, b, lo:hi], ps[0:T, b, lo:hi], ACT.Exp,
                                                 bias=nbias[:, b, i:i + 1], scale=(P ** -0.5, P ** -0.5, 1.0)[i],
                                                 accum_out=rsum[:, b, i:i + 1])
                    a.then_inc(at_exp.sem, 1)
                for b in range(GB):
                    act.wait_ge(at_pt.sem, at_pt.at(g, b + 1))
                    nc.scalar.copy(probT[0:TD, b, 0:T], ps[0:TD, 4 + b, 0:T])
                    nc.scalar.copy(probT[:, b, T:3 * T], ps[0:T, 4 + b, T:3 * T]).then_inc(at_pt_out.sem, 1)
                act.wait_ge(at_st.sem, at_st.at(g))
                nc.scalar.activation(ars[:], amv[:, :, 1], ACT.Ln, bias=eps_c[0:T, :]).then_inc(at_log.sem, 1)
                act.wait_ge(at_log.sem, at_log.at(g))
                nc.scalar.activation(ars[:], ars[:], ACT.Exp, scale=-0.5).then_inc(at_rstd.sem, 1)
                act.wait_ge(at_gate.sem, at_gate.at(g))
                nc.scalar.activation(glog[:], glog[:], ACT.Exp).then_inc(at_gexp.sem, 1)

            with act.Fori(0, G) as g:
                ln_act(act, g + G)
            act.wait_ge(a_in.sem, 16)
            nc.scalar.activation(nega[:], nega[:], ACT.Exp).then_inc(a_neg.sem, 1)
            with act.Fori(0, G) as g:
                ln_act(act, g + 2 * G)

            def act_norm_square(uu):
                act.wait_ge(ln_cent.sem, ln_cent.at(uu))
                nc.scalar.activation(rstd[:], cent[:], ACT.Square).then_inc(ln_square.sem, 1)

            def act_norm_rstd(uu):
                act.wait_ge(ln_var.sem, ln_var.at(uu))
                nc.scalar.activation(rstd[:], bank(LNB), ACT.Ln, bias=eps_c[:]).then_inc(ln_log.sem, 1)
                act.wait_ge(ln_log.sem, ln_log.at(uu))
                nc.scalar.activation(rstd[:], rstd[:], ACT.Exp, scale=-0.5).then_inc(ln_rstd.sem, 1)

            def sigmoid(k, src, dst, ready, sig, j):
                if k == 0:
                    act.wait_ge(ready.sem, ready.at(j))
                    nc.scalar.activation(dst, src, ACT.Exp, scale=-1.0).then_inc(sig.sem, 1)
                elif k == 1:
                    act.wait_ge(sig.sem, sig.at(j, 1))
                    nc.scalar.activation(dst, dst, ACT.Ln, bias=1.0).then_inc(sig.sem, 1)
                else:
                    act.wait_ge(sig.sem, sig.at(j, 2))
                    nc.scalar.activation(dst, dst, ACT.Exp, scale=-1.0).then_inc(sig.sem, 1)

            def pre_drow(j, par):
                act.wait_ge(p_xp.sem, p_xp.at(j))
                for lo, hi in ((32, 64), (64, P)):
                    nc.scalar.copy(bc[lo:hi, par, :], ps[lo:hi, L0, 0:N])
                nc.scalar.activation(drow[0:32, :], ps[0:32, L0, 0:N], ACT.Identity,
                                     bias=selcol[0:32, -1:]).then_inc(p_drow.sem, 1)

            def pre_softplus(j, k):
                if k == 0:
                    act.wait_ge(p_clip.sem, p_clip.at(j, 1))
                    nc.scalar.activation(spx[:], spx[:], ACT.Exp).then_inc(p_sp.sem, 1)
                else:
                    act.wait_ge(p_sp.sem, p_sp.at(j, 1))
                    nc.scalar.activation(spx[:], spx[:], ACT.Ln, bias=1.0).then_inc(p_sp.sem, 1)

            def scan_cb(j, n):
                act.wait_ge(s_c.sem, s_c.at(j, n + 1))
                act.wait_ge(s_gq.sem, s_gq.at(j, n + 1 - DB))
                nc.scalar.copy(cb[:, n % DB, :], bank(CC)).then_inc(s_cb.sem, 1)

            def scan_da(j, par, n):
                if n == 0:
                    act.wait_ge(p_dt.sem, p_dt.at(j))
                act.wait_ge(s_h.sem, s_h.at(j, n + 1 - DB))
                for i in range(2):
                    at = (j // G) * (2 * STATES) + (STATES * i + n)
                    scale = nega[:].rearrange("p l s -> p (l s)")[:, bass.ds(at, 1)]
                    a = nc.scalar.activation(
                        dA[:, n % DB, i, :].rearrange("p (b t) -> p b t", b=GB)[:, :, 1:T],
                        dt[:, par, i, :].rearrange("p (b t) -> p b t", b=GB)[:, :, 1:T], ACT.Exp, scale=scale)
                a.then_inc(s_da.sem, 1)

            def post_gelu(j):
                act.wait_ge(o_m1.sem, o_m1.at(j))
                for i in range(2):
                    a = nc.scalar.activation(gl[:, i, :], bank(L0 + i), ACT.Gelu, bias=ow("b1", i, 1))
                a.then_inc(o_gl.sem, 1)
                nc.scalar.preload_act_table_set("natural_log_exp_and_others")

            def act_round(j, par, u_pre, u_post):
                for n in range(STATES):
                    scan_da(j, par, n)
                    scan_cb(j, n)
                    if u_pre is not None:
                        if n == SLOT["pre_square"]:
                            act_norm_square(u_pre)
                        if n == SLOT["pre_rstd"]:
                            act_norm_rstd(u_pre)
                        for k in range(3):
                            if n == SLOT["sig_x"][k]:
                                sigmoid(k, xc[:, 1 - par, :, :], sig_x[:], p_conv, p_sx, j + 1)
                            if n == SLOT["sig_z"][k]:
                                sigmoid(k, sz[:, 1 - par, :, :], sig_z[:], p_zc, p_sz, j + 1)
                        if n == SLOT["drow"]:
                            pre_drow(j + 1, 1 - par)
                        for k in range(2):
                            if n == SLOT["softplus"][k]:
                                pre_softplus(j + 1, k)
                    if u_post is not None:
                        if n == SLOT["post_square"]:
                            act_norm_square(u_post)
                        if n == SLOT["post_rstd"]:
                            act_norm_rstd(u_post)
                        if n == SLOT["gelu"]:
                            post_gelu(j - 1)

            def act_post(j, par, uu):
                act_norm_square(uu)
                act_norm_rstd(uu)
                post_gelu(j)

            act.wait_ge(a_neg.sem, 2)
            act.wait_ge(sel_in.sem, 16)
            act_norm_square(LN0)
            act_norm_rstd(LN0)
            for k in range(3):
                sigmoid(k, xc[:, 0, :, :], sig_x[:], p_conv, p_sx, 0)
            for k in range(3):
                sigmoid(k, sz[:, 0, :, :], sig_z[:], p_zc, p_sz, 0)
            pre_drow(0, 0)
            pre_softplus(0, 0)
            pre_softplus(0, 1)
            mamba_rounds(act, act_round, act_post)
            act.wait_ge(h_mamba.sem, h_mamba.at(G - 1))
            with act.Fori(0, G) as g:
                u0 = g * 3 + LE
                act_norm_square(u0)
                act_norm_rstd(u0)
                for i, (dst, bias) in enumerate(((qh, "bq"), (kh, "bk"))):
                    act.wait_ge(m_qk.sem, m_qk.at(g, i + 1))
                    nc.scalar.activation(dst[:], bank(1 + i), ACT.Identity, bias=col(bias)).then_inc(m_qk_out.sem, 1)
                act.wait_ge(m_qk.sem, m_qk.at(g))
                nc.scalar.copy(vh[:].rearrange("p b c -> p (b c)"), ps[0:T, 3, :]).then_inc(m_qk_out.sem, 1)
                for b in range(GB):
                    act.wait_ge(m_mx.sem, m_mx.at(g, 2 * b + 2))
                    for hd in range(HEADS):
                        bk = 4 + 2 * (b % 2) + hd // 4
                        a = nc.scalar.activation(mp_[:, b % 2, hd, :], ps[0:T, bk, T * (hd % 4):T * (hd % 4) + T],
                                                 ACT.Exp, bias=mmax[:, b % 2, hd:hd + 1], scale=DH ** -0.5,
                                                 accum_out=msum[:, b % 2, hd:hd + 1])
                    a.then_inc(m_exp.sem, 1)
                act.wait_ge(m_ct.sem, m_ct.at(g))
                nc.scalar.activation(ctxT[:], bank(2), ACT.Identity, bias=col("bv")).then_inc(m_ct_out.sem, 1)
                act_norm_square(u0 + 1)
                act_norm_rstd(u0 + 1)
                act.wait_ge(m_oh.sem, m_oh.at(g))
                nc.scalar.copy(ohT[:], ps[0:EXPERTS, 4, 0:N]).then_inc(m_oh_out.sem, 1)
                for e in range(EXPERTS):
                    act.wait_ge(m_mask.sem, m_mask.at(g, e + 1))
                    nc.scalar.copy(mask[:, e, :], bank(5 + e % 2)).then_inc(m_mask_out.sem, 1)
                act.wait_ge(m_hid_e.sem, m_hid_e.at(g))
                for c in range(HID // P):
                    a = nc.scalar.activation(gh[:, c, :], bank(c), ACT.Gelu)
                a.then_inc(m_gelu.sem, 1)
                nc.scalar.preload_act_table_set("natural_log_exp_and_others")
                act_norm_square(u0 + 2)
                act_norm_rstd(u0 + 2)

        @block.gpsimd
        def _(pool):
            pool.wait_ge(f_max.sem, G + 2)
            nc.gpsimd.partition_all_reduce(fall[:], fpair[:], P, bass.bass_isa.ReduceOp.max)\
                .then_inc(f_gmax.sem, 1)
            def pre_silz(j, par):
                pool.wait_ge(p_sz.sem, p_sz.at(j))
                nc.gpsimd.tensor_tensor(sz[:, par, :, :], sz[:, par, :, :], sig_z[:], ALU.mult).then_inc(p_silz.sem, 1)

            pre_silz(0, 0)

            def pool_round(j, par, u_pre, u_post):
                for n in range(STATES):
                    pool.wait_ge(s_h.sem, s_h.at(j, n + 1))
                    pool.wait_ge(s_cb.sem, s_cb.at(j, n + 1))
                    pool.wait_ge(s_sum.sem, s_sum.at(j, n + 1 - DB))
                    nc.gpsimd.tensor_tensor(gq[:, n % DB, :, :], hs[:, n % DB, :, :],
                                            cb[:, n % DB:n % DB + 1, :].to_broadcast([P, 2, N]), ALU.mult)\
                        .then_inc(s_gq.sem, 1)
                    if u_pre is not None and n == SLOT["silz"]:
                        pre_silz(j + 1, 1 - par)

            mamba_rounds(pool, pool_round, lambda j, par, uu: None)

        @block.vector
        def _(dve):
            nc.vector.memset(mean_w[:], 1.0 / P)
            nc.vector.memset(ones_w[:], 1.0)
            nc.vector.memset(xp[:], 0.0)
            nc.vector.memset(eps_c[:], EPS).then_inc(consts.sem, 1)
            dve.wait_ge(frames_in.sem, FRAMES_ALL)
            with dve.Fori(0, G) as g:
                dve.wait_ge(tok_mm.sem, tok_mm.at(g))
                nc.vector.tensor_scalar(h[:, g, :], ps[:, g, 0:N], col("tok_b"), 0.0, ALU.add, ALU.max)\
                    .then_inc(tok_y.sem, 1)
                dve.wait_ge(tok_y.sem, tok_y.at(g))
                nc.vector.bn_stats(bn[:, g, :], h[:, g, :]).then_inc(tok_stats.sem, 1)
            dve.wait_ge(tok_stats.sem, G)
            nc.vector.bn_aggr(bn_mv[:], bn[:].rearrange("p g s -> p (g s)")).then_inc(bn_step.sem, 1)
            dve.wait_ge(bn_step.sem, 3)
            nc.vector.tensor_tensor(bn_sc[:, 2:3], bn_sc[:, 1:2], col("tok_gamma"), ALU.mult).then_inc(bn_step.sem, 1)
            dve.wait_ge(bn_step.sem, 4)
            nc.vector.tensor_scalar(bn_sc[:, 3:4], bn_mv[:, 0:1], bn_sc[:, 2:3], None, ALU.mult)\
                .then_inc(bn_step.sem, 1)
            dve.wait_ge(bn_step.sem, 5)
            nc.vector.tensor_tensor(bn_sc[:, 0:1], col("tok_beta"), bn_sc[:, 3:4], ALU.subtract)\
                .then_inc(bn_step.sem, 1)
            dve.wait_ge(bn_step.sem, 6)
            with dve.Fori(0, G) as g:
                nc.vector.tensor_scalar(h[:, g, :], h[:, g, :], bn_sc[:, 2:3], bn_sc[:, 0:1], ALU.mult, ALU.add)\
                    .then_inc(h_tok.sem, 1)

            dve.wait_ge(param.sem, PARAM_ALL)
            nc.vector.tensor_scalar(rtemp[:], row("temp"), 0.01, None, ALU.max).then_inc(bn_step.sem, 1)
            dve.wait_ge(bn_step.sem, 7)
            nc.vector.reciprocal(rtemp[:], rtemp[:]).then_inc(bn_step.sem, 1)
            dve.wait_ge(bn_step.sem, 8)
            with dve.Fori(0, G) as g:
                dve.wait_ge(h_tok.sem, h_tok.at(g))
                ln_dve(dve, g, h[:, g, :])
                nc.vector.tensor_tensor(xp[:, :, 1:T + 1], cent[:].rearrange("p (b t) -> p b t", b=GB),
                                        rstd[:].rearrange("p (b t) -> p b t", b=GB), ALU.mult)\
                    .then_inc(xn_ready.sem, 1)
                dve.wait_ge(at_conv.sem, at_conv.at(g))
                nc.vector.tensor_scalar(xd[:], ps[:, 1, 0:GB * TD].rearrange("p (b t) -> p b t", b=GB), col("db"),
                                        None, ALU.add).then_inc(at_xd.sem, 1)
                dve.wait_ge(at_proj.sem, at_proj.at(g, 3))
                nc.vector.tensor_scalar(q_c[:], bank4(4), col("bq_c"), None, ALU.add).then_inc(at_qc.sem, 1)
                dve.wait_ge(at_kcr.sem, at_kcr.at(g))
                nc.vector.tensor_scalar(k_cr[:], ps[:, 1, 0:GB * TD].rearrange("p (b t) -> p b t", b=GB),
                                        col("bk_cr"), None, ALU.add).then_inc(at_kcr_out.sem, 1)
                dve.wait_ge(at_nrm.sem, at_nrm.at(g))
                nc.vector.tensor_scalar(nq[:], nq[:], 1e-8, None, ALU.add).then_inc(at_nstep.sem, 1)
                dve.wait_ge(at_nstep.sem, at_nstep.at(g, 1))
                nc.vector.reciprocal(nq[:], nq[:]).then_inc(at_nstep.sem, 1)
                dve.wait_ge(at_nstep.sem, at_nstep.at(g, 2))
                dve.wait_ge(at_q_act.sem, at_q_act.at(g))
                nc.vector.scalar_tensor_tensor(q_c[:].rearrange("p b t -> p (b t)"),
                                               q_c[:].rearrange("p b t -> p (b t)"), rtemp[:], nq[:, 0, :],
                                               ALU.mult, ALU.mult).then_inc(at_qkn.sem, 1)
                nc.vector.tensor_tensor(k_c[:].rearrange("p b t -> p (b t)"), k_c[:].rearrange("p b t -> p (b t)"),
                                        nq[:, 1, :], ALU.mult).then_inc(at_qkn.sem, 1)
                dve.wait_ge(at_score.sem, at_score.at(g))
                nc.vector.tensor_reduce(nmax[:, :, 0:1].squeeze(2), ps[0:T, 0:GB, 0:TD], AX.X, ALU.max, negate=True)\
                    .then_inc(at_max.sem, 1)
                nc.vector.tensor_reduce(nmax[:, :, 1:3], ps[0:T, 0:GB, TD:SC].rearrange("p b (i s) -> p b i s", i=2),
                                        AX.X, ALU.max, negate=True).then_inc(at_max.sem, 1)
                dve.wait_ge(at_max.sem, at_max.at(g))
                nc.vector.tensor_tensor(nbias[:], nmax[:], row("scales", T).unsqueeze(1).to_broadcast([T, GB, 3]),
                                        ALU.mult).then_inc(at_bias.sem, 1)
                dve.wait_ge(at_exp.sem, at_exp.at(g))
                nc.vector.reciprocal(rinv[:], rsum[:]).then_inc(at_rinv.sem, 1)
                dve.wait_ge(at_rinv.sem, at_rinv.at(g))
                for b in range(GB):
                    dve.wait_ge(at_o.sem, at_o.at(g, b + 1))
                    for i in range(3):
                        a = nc.vector.scalar_tensor_tensor(ao[:, b, i, :], ps[0:T, b, P * i:P * i + P],
                                                           rinv[:, b, i:i + 1], row("bv", T)[:, P * i:P * i + P],
                                                           ALU.mult, ALU.add)
                a.then_inc(at_on.sem, 1)
                dve.wait_ge(at_on.sem, at_on.at(g))
                for b in range(GB):
                    for i in range(3):
                        a = nc.vector.bn_stats(ast[:, b, i, :], ao[:, b, i, :])
                a.then_inc(at_st.sem, 1)
                dve.wait_ge(at_st.sem, at_st.at(g, 1))
                st = ast[:].rearrange("p b i s -> p (b i) s")
                nc.vector.tensor_tensor(amv[:, :, 0], st[:, :, 1], st[:, :, 4], ALU.add)
                nc.vector.tensor_tensor(amv[:, :, 1], st[:, :, 2], st[:, :, 5], ALU.add)
                nc.vector.tensor_tensor(ad[:], st[:, :, 1], st[:, :, 4], ALU.subtract).then_inc(at_st.sem, 1)
                dve.wait_ge(at_st.sem, at_st.at(g, 2))
                nc.vector.tensor_scalar(amv[:, :, 0], amv[:, :, 0], 0.5, None, ALU.mult)
                nc.vector.scalar_tensor_tensor(ad[:], ad[:], 0.25, ad[:], ALU.mult, ALU.mult).then_inc(at_st.sem, 1)
                dve.wait_ge(at_st.sem, at_st.at(g, 3))
                nc.vector.scalar_tensor_tensor(amv[:, :, 1], amv[:, :, 1], 1.0 / P, ad[:], ALU.mult, ALU.add)\
                    .then_inc(at_st.sem, 1)
                dve.wait_ge(at_rstd.sem, at_rstd.at(g))
                for b in range(GB):
                    for i in range(3):
                        k = 3 * b + i
                        a = nc.vector.tensor_scalar(ao[:, b, i, :], ao[:, b, i, :], amv[:, k, 0:1], ars[:, k:k + 1],
                                                    ALU.subtract, ALU.mult)
                a.then_inc(at_aff.sem, 1)
                ao3 = ao[:].rearrange("p b i c -> p b (i c)")
                dve.wait_ge(at_aff.sem, at_aff.at(g, 1))
                nc.vector.tensor_tensor(ao3, ao3, row("ln_g", T).unsqueeze(1).to_broadcast([T, GB, 3 * P]), ALU.mult)\
                    .then_inc(at_aff.sem, 1)
                dve.wait_ge(at_aff.sem, at_aff.at(g, 2))
                nc.vector.tensor_tensor(ao3, ao3, row("ln_b", T).unsqueeze(1).to_broadcast([T, GB, 3 * P]), ALU.add)\
                    .then_inc(at_aff.sem, 1)
                dve.wait_ge(at_aff.sem, at_aff.at(g, 3))
                for b in range(GB):
                    for i in range(3):
                        if b or i:
                            dve.wait_ge(at_logit.sem, at_logit.at(g, 3 * b + i))
                        nc.vector.tensor_tensor_reduce(junk[:], ao3[:, b, :],
                                                       row("gw", T)[:, 3 * P * i:3 * P * (i + 1)], 1.0, 0.0,
                                                       ALU.mult, ALU.add, glog[:, b, i:i + 1])\
                            .then_inc(at_logit.sem, 1)
                dve.wait_ge(at_logit.sem, at_logit.at(g))
                nc.vector.tensor_tensor(glog[:], glog[:], row("gb", T).unsqueeze(1).to_broadcast([T, GB, 3]), ALU.add)\
                    .then_inc(at_gate.sem, 1)
                dve.wait_ge(at_gate.sem, at_gate.at(g, 1))
                nc.vector.tensor_reduce(gmx[:], glog[:], AX.X, ALU.max).then_inc(at_gate.sem, 1)
                dve.wait_ge(at_gate.sem, at_gate.at(g, 2))
                nc.vector.tensor_tensor(glog[:], glog[:], gmx[:].unsqueeze(2).to_broadcast([T, GB, 3]), ALU.subtract)\
                    .then_inc(at_gate.sem, 1)
                dve.wait_ge(at_gexp.sem, at_gexp.at(g))
                nc.vector.tensor_reduce(gmx[:], glog[:], AX.X, ALU.add).then_inc(at_gn.sem, 1)
                dve.wait_ge(at_gn.sem, at_gn.at(g, 1))
                nc.vector.reciprocal(gmx[:], gmx[:]).then_inc(at_gn.sem, 1)
                dve.wait_ge(at_gn.sem, at_gn.at(g, 2))
                nc.vector.tensor_tensor(glog[:], glog[:], gmx[:].unsqueeze(2).to_broadcast([T, GB, 3]), ALU.mult)\
                    .then_inc(at_gn.sem, 1)
                dve.wait_ge(at_gn.sem, at_gn.at(g))
                for b in range(GB):
                    a = nc.vector.tensor_scalar(z[:, b, :], ao[:, b, 0, :], glog[:, b, 0:1], None, ALU.mult)
                a.then_inc(at_z.sem, 1)
                for i in range(1, 3):
                    dve.wait_ge(at_z.sem, at_z.at(g, i))
                    for b in range(GB):
                        a = nc.vector.scalar_tensor_tensor(z[:, b, :], ao[:, b, i, :], glog[:, b, i:i + 1], z[:, b, :],
                                                           ALU.mult, ALU.add)
                    a.then_inc(at_z.sem, 1)
                dve.wait_ge(at_zt.sem, at_zt.at(g))
                nc.vector.tensor_tensor(h[:, g, :], h[:, g, :], bank(4), ALU.add).then_inc(h_attn.sem, 1)

            dve.wait_ge(h_attn.sem, h_attn.at(G - 1))
            with dve.Fori(0, G) as g:
                ln_dve(dve, g + G, h[:, g, :])
                nc.vector.tensor_tensor(xs[:, g, :], cent[:], rstd[:], ALU.mult).then_inc(fx.sem, 1)
                dve.wait_ge(fx.sem, fx.at(g))
                nc.vector.tensor_reduce(famax[:, bass.ds(g, 1)], xs[:, g, :], AX.X, ALU.max, apply_absolute_value=True)\
                    .then_inc(f_max.sem, 1)
            dve.wait_ge(f_max.sem, G)
            nc.vector.tensor_reduce(fpair[:, 0:1], famax[:, 0:G], AX.X, ALU.max).then_inc(f_max.sem, 1)
            nc.vector.tensor_reduce(fpair[:, 1:2], mat("ffn"), AX.X, ALU.max, apply_absolute_value=True)\
                .then_inc(f_max.sem, 1)
            dve.wait_ge(f_gmax.sem, 1)
            nc.vector.tensor_scalar(fall[:], fall[:], 1e-12, None, ALU.max).then_inc(f_step.sem, 1)
            dve.wait_ge(f_step.sem, 1)
            nc.vector.reciprocal(fpair[:], fall[:]).then_inc(f_step.sem, 1)
            dve.wait_ge(f_step.sem, 2)
            nc.vector.tensor_scalar(fsc[:, 0:2], fpair[:], FP8_MAX, None, ALU.mult).then_inc(f_step.sem, 1)
            dve.wait_ge(f_step.sem, 3)
            nc.vector.reciprocal(fpair[:], fsc[:, 0:2]).then_inc(f_step.sem, 1)
            dve.wait_ge(f_step.sem, 4)
            nc.vector.tensor_tensor(fsc[:, 2:3], fpair[:, 0:1], fpair[:, 1:2], ALU.mult).then_inc(f_step.sem, 1)
            dve.wait_ge(f_step.sem, 5)

            def quantise(dst, src, scale, a, m, sig, r):
                nc.vector.tensor_scalar(a, src, scale, FP8_MAX, ALU.mult, ALU.min).then_inc(sig.sem, 1)
                dve.wait_ge(sig.sem, sig.at(r, 1))
                nc.vector.tensor_scalar(a, a, -FP8_MAX, None, ALU.max).then_inc(sig.sem, 1)
                dve.wait_ge(sig.sem, sig.at(r, 2))
                nc.vector.tensor_scalar(m.bitcast(U32), a.bitcast(U32), 0x7F800000, None, ALU.bitwise_and)\
                    .then_inc(sig.sem, 1)
                dve.wait_ge(sig.sem, sig.at(r, 3))
                nc.vector.tensor_scalar(m, m, 2.0 ** -6, 1.5 * 2.0 ** 20, ALU.max, ALU.mult).then_inc(sig.sem, 1)
                dve.wait_ge(sig.sem, sig.at(r, 4))
                nc.vector.tensor_tensor(a, a, m, ALU.add).then_inc(sig.sem, 1)
                dve.wait_ge(sig.sem, sig.at(r, 5))
                nc.vector.tensor_tensor(dst, a, m, ALU.subtract).then_inc(sig.sem, 1)

            quantise(wq8[:], mat("ffn"), fsc[:, 1:2], wtmp[:, 0, :], wtmp[:, 1, :], f_wstep, 0)
            dve.wait_ge(f_wstep.sem, f_wstep.at(0))
            nc.vector.memset(wtmp[:, 2, :], 0.0).then_inc(f_wq.sem, 1)

            def dequantise(g):
                dve.wait_ge(f_mm.sem, f_mm.at(g))
                nc.vector.scalar_tensor_tensor(h[:, g, :], ps[:, g, 0:N], fsc[:, 2:3], h[:, g, :],
                                               ALU.mult, ALU.add).then_inc(h_ffn.sem, 1)

            with dve.Fori(0, G) as g:
                quantise(xq8[:], xs[:, g, :], fsc[:, 0:1], ftmp[:, 0, :], ftmp[:, 1, :], f_q, g)
                dequantise(g)
            dve.wait_ge(sel_in.sem, 16)
            nc.vector.memset(dA[:], 0.0)
            nc.vector.memset(drow[:], 0.0)
            nc.vector.memset(bc[:], 0.0)
            nc.vector.tensor_copy(sel[:], selcol[:, 0:2 * STATES].unsqueeze(2).to_broadcast([P, 2 * STATES, P]))\
                .then_inc(sel_made.sem, 1)
            dve.wait_ge(a_neg.sem, 1)
            nc.vector.tensor_scalar(nega[:], nega[:], -1.0, None, ALU.mult).then_inc(a_neg.sem, 1)
            with dve.Fori(0, G) as g:
                ln_dve(dve, g + 2 * G, h[:, g, :])
                nc.vector.tensor_tensor(xs[:, g, :], cent[:], rstd[:], ALU.mult).then_inc(x_in.sem, 1)
                dve.wait_ge(x_in.sem, x_in.at(g))

            def xgroup(j):
                return xs[:, j % G, :] if isinstance(j, int) else xs[:, bass.ds(j % G, 1), :].squeeze(1)

            def dve_norm_center(uu, src):
                dve.wait_ge(ln_mean.sem, ln_mean.at(uu))
                nc.vector.tensor_tensor(cent[:], src, bank(LNB), ALU.subtract).then_inc(ln_cent.sem, 1)

            def dve_norm_out(uu, dst, gamma, beta, sig, j, w_in):
                dve.wait_ge(w_in.sem, w_in.at(j // G))
                dve.wait_ge(ln_rstd.sem, ln_rstd.at(uu))
                nc.vector.scalar_tensor_tensor(cent[:], cent[:], gamma, rstd[:], ALU.mult, ALU.mult)\
                    .then_inc(sig.sem, 1)
                dve.wait_ge(sig.sem, sig.at(j, 1))
                nc.vector.tensor_scalar(dst, cent[:], beta, None, ALU.add).then_inc(sig.sem, 1)
                dve.wait_ge(sig.sem, sig.at(j))

            def pre_conv(j, par, s):
                if s == 0:
                    dve.wait_ge(p_xin.sem, p_xin.at(j))
                    for i in range(2):
                        a = nc.vector.tensor_scalar(xc[:, par, i, :], bank(L0 + i), pw("conv_w", 4 * i + 3, 1),
                                                    pw("conv_b", i, 1), ALU.mult, ALU.add)
                else:
                    dve.wait_ge(p_conv.sem, p_conv.at(j, s))
                    for i in range(2):
                        dst = xc[:, par, i, :].rearrange("p (b t) -> p b t", b=GB)[:, :, s:T]
                        a = nc.vector.scalar_tensor_tensor(dst, bank4(L0 + i)[:, :, 0:T - s],
                                                           pw("conv_w", 4 * i + 3 - s, 1), dst, ALU.mult, ALU.add)
                a.then_inc(p_conv.sem, 1)

            def pre_floor(j, par):
                dve.wait_ge(p_conv.sem, p_conv.at(j, 4))
                nc.vector.tensor_scalar(xc[:, par, :, :], xc[:, par, :, :], -40.0, None, ALU.max)\
                    .then_inc(p_conv.sem, 1)

            def pre_xc(j, par):
                dve.wait_ge(p_sx.sem, p_sx.at(j))
                nc.vector.tensor_tensor(xc[:, par, :, :], xc[:, par, :, :], sig_x[:], ALU.mult).then_inc(p_xc.sem, 1)

            def pre_zclip(j, par):
                dve.wait_ge(p_z.sem, p_z.at(j))
                nc.vector.tensor_scalar(sz[:, par, :, :], ps[:, L0:L0 + 2, 0:N], -40.0, None, ALU.max)\
                    .then_inc(p_zc.sem, 1)

            def pre_split(j, par):
                dve.wait_ge(p_drow.sem, p_drow.at(j))
                nc.vector.tensor_tensor(spx[64:P, 0, :], ps[64:P, L0, 0:N], bc[64:P, par, :], ALU.subtract)\
                    .then_inc(p_bc.sem, 1)
                dve.wait_ge(p_bc.sem, p_bc.at(j, 1))
                nc.vector.tensor_copy(bc[64:P, par, :], spx[64:P, 0, :]).then_inc(p_bc.sem, 1)
                dve.wait_ge(p_bc.sem, p_bc.at(j, 2))
                nc.vector.tensor_tensor(bc[96:P, par, :], spx[96:P, 0, :], bc[96:P, par, :], ALU.subtract)\
                    .then_inc(p_bc.sem, 1)

            def pre_clip(j, par):
                dve.wait_ge(p_dtm.sem, p_dtm.at(j))
                nc.vector.tensor_scalar(spx[:], ps[:, L0:L0 + 2, 0:N], 20.0, None, ALU.min).then_inc(p_clip.sem, 1)
                nc.vector.tensor_scalar(dt[:, par, :, :], ps[:, L0:L0 + 2, 0:N], -20.0, 0.0, ALU.add, ALU.max)\
                    .then_inc(p_clip.sem, 1)

            def pre_dt(j, par):
                dve.wait_ge(p_clip.sem, p_clip.at(j))
                dve.wait_ge(p_sp.sem, p_sp.at(j))
                nc.vector.tensor_tensor(dt[:, par, :, :], dt[:, par, :, :], spx[:], ALU.add).then_inc(p_dt.sem, 1)

            def pre_u(j, par):
                dve.wait_ge(p_dt.sem, p_dt.at(j))
                nc.vector.tensor_tensor(u[:, par, :, :], dt[:, par, :, :], xc[:, par, :, :], ALU.mult)\
                    .then_inc(p_u.sem, 1)

            def scan_db(j, par, n):
                if n == 0:
                    dve.wait_ge(p_u.sem, p_u.at(j))
                dve.wait_ge(s_h.sem, s_h.at(j, n - 1))
                dve.wait_ge(s_b.sem, s_b.at(j, n + 1))
                nc.vector.tensor_tensor(db[:, n % 2, :, :], u[:, par, :, :],
                                        ps[:, BB + n % 2:BB + n % 2 + 1, 0:N].to_broadcast([P, 2, N]), ALU.mult)\
                    .then_inc(s_db.sem, 1)

            def scan_h(j, n):
                dve.wait_ge(s_db.sem, s_db.at(j, n + 1))
                dve.wait_ge(s_da.sem, s_da.at(j, n + 1))
                dve.wait_ge(s_gq.sem, s_gq.at(j, n + 1 - DB))
                nc.vector.tensor_tensor_scan(hs[:, n % DB, :, :].rearrange("p i t -> p (i t)"),
                                             dA[:, n % DB, :, :].rearrange("p i t -> p (i t)"),
                                             db[:, n % 2, :, :].rearrange("p i t -> p (i t)"),
                                             0.0, ALU.mult, ALU.add).then_inc(s_h.sem, 1)

            def post_y(j, par):
                dve.wait_ge(wo_in.sem, wo_in.at(j // G))
                dve.wait_ge(s_sum.sem, s_sum.at(j))
                for i in range(2):
                    a = nc.vector.scalar_tensor_tensor(yv[:, i, :], xc[:, par, i, :], ow("D_skip", i, 1),
                                                       bank(Y + i), ALU.mult, ALU.add)
                a.then_inc(o_y.sem, 1)
                dve.wait_ge(o_y.sem, o_y.at(j))
                dve.wait_ge(p_silz.sem, p_silz.at(j))
                nc.vector.tensor_tensor(yv[:], yv[:], sz[:, par, :, :], ALU.mult).then_inc(o_yg.sem, 1)

            def post_x(j):
                dve.wait_ge(o_out.sem, o_out.at(j))
                nc.vector.tensor_tensor(resid[:], xgroup(j), bank(LP), ALU.add).then_inc(o_x.sem, 1)

            def post_x2(j):
                dve.wait_ge(o_m2.sem, o_m2.at(j))
                nc.vector.scalar_tensor_tensor(xgroup(j), bank(LP), ow("b2"), resid[:], ALU.add, ALU.add)\
                    .then_inc(o_x2.sem, 1)

            def dve_round(j, par, u_pre, u_post):
                for n in range(STATES):
                    if n == 0:
                        scan_db(j, par, 0)
                    if n + 1 < STATES:
                        scan_db(j, par, n + 1)
                    scan_h(j, n)
                    if u_post is not None and n == SLOT["y"]:
                        post_y(j - 1, 1 - par)
                    if u_pre is not None:
                        if n == SLOT["pre_cent"]:
                            dve_norm_center(u_pre, xgroup(j + 1))
                        if n == SLOT["pre_xn"]:
                            dve_norm_out(u_pre, xn[:], pw("ln1_g"), pw("ln1_b"), p_xn, j + 1, wp_in)
                        for s in range(4):
                            if n == SLOT["conv"][s]:
                                pre_conv(j + 1, 1 - par, s)
                        if n == SLOT["floor"]:
                            pre_floor(j + 1, 1 - par)
                        if n == SLOT["zclip"]:
                            pre_zclip(j + 1, 1 - par)
                        if n == SLOT["xc"]:
                            pre_xc(j + 1, 1 - par)
                        if n == SLOT["split"]:
                            pre_split(j + 1, 1 - par)
                        if n == SLOT["clip"]:
                            pre_clip(j + 1, 1 - par)
                        if n == SLOT["dt"]:
                            pre_dt(j + 1, 1 - par)
                        if n == SLOT["u"]:
                            pre_u(j + 1, 1 - par)
                    if u_post is not None:
                        if n == SLOT["x"]:
                            post_x(j - 1)
                        if n == SLOT["post_cent"]:
                            dve_norm_center(u_post, resid[:])
                        if n == SLOT["post_xn"]:
                            dve_norm_out(u_post, xn2[:], ow("ln2_g"), ow("ln2_b"), o_xn, j - 1, wo_in)
                        if n == SLOT["x2"]:
                            post_x2(j - 1)

            def dve_post(j, par, uu):
                post_y(j, par)
                post_x(j)
                dve_norm_center(uu, resid[:])
                dve_norm_out(uu, xn2[:], ow("ln2_g"), ow("ln2_b"), o_xn, j, wo_in)
                post_x2(j)

            dve_norm_center(LN0, xgroup(0))
            dve_norm_out(LN0, xn[:], pw("ln1_g"), pw("ln1_b"), p_xn, 0, wp_in)
            for s in range(4):
                pre_conv(0, 0, s)
            pre_floor(0, 0)
            pre_zclip(0, 0)
            pre_xc(0, 0)
            pre_split(0, 0)
            pre_clip(0, 0)
            pre_dt(0, 0)
            pre_u(0, 0)
            mamba_rounds(dve, dve_round, dve_post)
            dve.wait_ge(o_x2.sem, o_x2.at(ROUNDS - 1))
            with dve.Fori(0, G) as g:
                nc.vector.tensor_tensor(h[:, g, :], h[:, g, :], xs[:, g, :], ALU.add).then_inc(h_mamba.sem, 1)
            dve.wait_ge(h_mamba.sem, h_mamba.at(G - 1))
            nc.vector.memset(ohb[:], 0.0)
            nc.vector.tensor_copy(esel[:], selcol[:, 2 * STATES + HEADS:2 * STATES + HEADS + EXPERTS].unsqueeze(2)
                                  .to_broadcast([P, EXPERTS, P])).then_inc(m_const.sem, 1)
            dve.wait_ge(m_const.sem, 1)
            with dve.Fori(0, G) as g:
                u0 = g * 3 + LE
                dve_norm_center(u0, h[:, g, :])
                dve.wait_ge(ln_rstd.sem, ln_rstd.at(u0))
                nc.vector.tensor_tensor(xe[:], cent[:], rstd[:], ALU.mult).then_inc(m_xe.sem, 1)
                dve.wait_ge(m_qk_out.sem, m_qk_out.at(g, 1))
                for hd in range(HEADS):
                    a = nc.vector.tensor_scalar(qm[:, hd, :], qh[:], selcol[:, 2 * STATES + hd:2 * STATES + hd + 1],
                                                None, ALU.mult)
                a.then_inc(m_qm.sem, 1)

                def maxima(b):
                    dve.wait_ge(m_sc.sem, m_sc.at(g, b + 1))
                    k = 4 + 2 * (b % 2)
                    nc.vector.tensor_reduce(mmax[:, b % 2, :].rearrange("p (k i) -> p k i", k=2),
                                            ps[0:T, k:k + 2, 0:N].rearrange("p k (i s) -> p k i s", i=4),
                                            AX.X, ALU.max, negate=True).then_inc(m_mx.sem, 1)
                    dve.wait_ge(m_mx.sem, m_mx.at(g, 2 * b + 1))
                    nc.vector.tensor_scalar(mmax[:, b % 2, :], mmax[:, b % 2, :], DH ** -0.5, None, ALU.mult)\
                        .then_inc(m_mx.sem, 1)

                def probs_out(b):
                    dve.wait_ge(m_pt.sem, m_pt.at(g, b + 1))
                    k = 4 + 2 * (b % 2)
                    nc.vector.tensor_copy(mpT[:, b % 2, :, :].rearrange("p (k i) t -> p k (i t)", k=2),
                                          ps[0:T, k:k + 2, 0:N]).then_inc(m_pt_out.sem, 1)
                    nc.vector.reciprocal(msum[:, b % 2, :], msum[:, b % 2, :]).then_inc(m_ri.sem, 1)

                def normalise(b):
                    dve.wait_ge(m_ctx.sem, m_ctx.at(g, b + 1))
                    dve.wait_ge(m_ri.sem, m_ri.at(g, b + 1))
                    nc.vector.tensor_tensor(mctx[:, b, :].rearrange("p (h d) -> p h d", h=HEADS),
                                            ps[0:T, 1, P * b:P * b + P].rearrange("p (h d) -> p h d", h=HEADS),
                                            msum[:, b % 2, :].unsqueeze(2).to_broadcast([T, HEADS, DH]), ALU.mult)\
                        .then_inc(m_ctx_n.sem, 1)

                maxima(0)
                maxima(1)
                for b in range(GB):
                    probs_out(b)
                    normalise(b)
                    if b + 2 < GB:
                        dve.wait_ge(m_ctx_n.sem, m_ctx_n.at(g, b + 1))
                        maxima(b + 2)
                dve.wait_ge(m_sa.sem, m_sa.at(g))
                nc.vector.scalar_tensor_tensor(r1[:], bank(1), col("bo"), xe[:], ALU.add, ALU.add)\
                    .then_inc(m_r1.sem, 1)
                dve_norm_center(u0 + 1, r1[:])
                dve.wait_ge(ln_rstd.sem, ln_rstd.at(u0 + 1))
                nc.vector.scalar_tensor_tensor(cent[:], cent[:], col("g1"), rstd[:], ALU.mult, ALU.mult)\
                    .then_inc(m_x1.sem, 1)
                dve.wait_ge(m_x1.sem, m_x1.at(g, 1))
                nc.vector.tensor_scalar(x1[:], cent[:], col("beta1"), None, ALU.add).then_inc(m_x1.sem, 1)
                dve.wait_ge(m_lg.sem, m_lg.at(g))
                nc.vector.tensor_tensor(lg[:], ps[0:T, 3, 0:GB * EXPERTS].rearrange("p (b e) -> p b e", b=GB),
                                        row("bg", T).unsqueeze(1).to_broadcast([T, GB, EXPERTS]), ALU.add)\
                    .then_inc(m_top.sem, 1)
                dve.wait_ge(m_top.sem, m_top.at(g, 1))
                nc.vector.tensor_reduce(lmx[:], lg[:], AX.X, ALU.max).then_inc(m_top.sem, 1)
                dve.wait_ge(m_top.sem, m_top.at(g, 2))
                nc.vector.tensor_tensor(eq[:], lg[:], lmx[:].unsqueeze(2).to_broadcast([T, GB, EXPERTS]), ALU.is_equal)\
                    .then_inc(m_top.sem, 1)
                dve.wait_ge(m_top.sem, m_top.at(g, 3))
                nc.vector.tensor_tensor(lg[:], eq[:], row("places", T).unsqueeze(1).to_broadcast([T, GB, EXPERTS]),
                                        ALU.mult).then_inc(m_top.sem, 1)
                dve.wait_ge(m_top.sem, m_top.at(g, 4))
                nc.vector.tensor_reduce(lmx[:], lg[:], AX.X, ALU.max).then_inc(m_top.sem, 1)
                dve.wait_ge(m_top.sem, m_top.at(g, 5))
                nc.vector.tensor_tensor(eq[:], lg[:], lmx[:].unsqueeze(2).to_broadcast([T, GB, EXPERTS]), ALU.is_equal)\
                    .then_inc(m_top.sem, 1)
                dve.wait_ge(m_oh_out.sem, m_oh_out.at(g, 1))
                nc.vector.tensor_copy(ohb[0:EXPERTS, :], ohT[:]).then_inc(m_oh_out.sem, 1)
                for e in range(EXPERTS):
                    dve.wait_ge(m_mask_out.sem, m_mask_out.at(g, e + 1))
                    dve.wait_ge(m_hid_e.sem, m_hid_e.at(g, e - 1))
                    nc.vector.tensor_tensor(xm[:, e % 2, :], x1[:], mask[:, e, :], ALU.mult).then_inc(m_xm.sem, 1)
                dve.wait_ge(m_b2.sem, m_b2.at(g))
                nc.vector.tensor_tensor(acc[:], x1[:], bank(7), ALU.add).then_inc(m_acc.sem, 1)
                for e in range(EXPERTS):
                    dve.wait_ge(m_y.sem, m_y.at(g, e + 1))
                    nc.vector.tensor_tensor(yt[:, e % 2, :], mask[:, e, :], bank(4 + e % 2), ALU.mult)\
                        .then_inc(m_yt.sem, 1)
                    dve.wait_ge(m_yt.sem, m_yt.at(g, e + 1))
                    dve.wait_ge(m_acc.sem, m_acc.at(g, e + 1))
                    nc.vector.tensor_tensor(acc[:], acc[:], yt[:, e % 2, :], ALU.add).then_inc(m_acc.sem, 1)
                dve_norm_center(u0 + 2, acc[:])
                dve.wait_ge(ln_rstd.sem, ln_rstd.at(u0 + 2))
                nc.vector.scalar_tensor_tensor(cent[:], cent[:], col("g2"), rstd[:], ALU.mult, ALU.mult)\
                    .then_inc(m_g2.sem, 1)
                dve.wait_ge(m_g2.sem, m_g2.at(g, 1))
                nc.vector.scalar_tensor_tensor(h[:, g, :], cent[:], col("beta2"), h[:, g, :], ALU.add, ALU.add)\
                    .then_inc(h_out.sem, 1)
                dve.wait_ge(h_out.sem, h_out.at(g))


ORDER = ["x_t", "tok_w", "cols", "mats", "rows", "layers", "w1", "w2", "moe_rows", "wg", "ident", "selcol"]


def kernel(**inputs):
    import numpy as np
    import concourse.bacc as bacc
    from concourse.bass_utils import run_bass_kernel_spmd

    i = {k: np.asarray(v) for k, v in inputs.items()}
    a0, l1, f1 = (lambda n: i["L0_attn_" + n]), (lambda n: i["L1_attn_" + n]), (lambda n: i["L1_ffn_" + n])

    cols = {"tok_b": i["L0_tok_b"], "tok_gamma": i["L0_tok_gamma"], "tok_beta": i["L0_tok_beta"]}
    for n in ("db", "bq_cr", "bk_cr", "bq_d", "bk_d", "bq_c", "bk_c"):
        cols[n] = a0(n)
    for n in ("bq", "bk", "bv", "bo", "g1", "beta1", "g2", "beta2"):
        cols[n] = f1(n)
    mats = {f"dw{k}": a0("dw")[:, :, k].T for k in range(3)}
    for n in ("wq_cr", "wk_cr", "wv_cr", "wq_d", "wk_d", "wv_d", "wq_c", "wk_c", "wv_c"):
        mats[n] = a0(n).T
    mats["ffn"] = i["L0_ffn_weight"]
    for n in ("Wq", "Wk", "Wv", "Wo"):
        mats[n] = f1(n)
    f32 = np.float32
    rows = {"bv": np.concatenate([a0("bv_" + n) for n in ("cr", "d", "c")]),
            "ln_g": np.concatenate([a0(f"ln_{n}_g") for n in ("cr", "d", "c")]),
            "ln_b": np.concatenate([a0(f"ln_{n}_b") for n in ("cr", "d", "c")]),
            "gw": a0("gw").reshape(-1), "gb": a0("gb"), "temp": a0("temp").reshape(1), "bg": f1("bg"),
            "places": np.arange(EXPERTS, 0, -1).astype(f32),
            "scales": np.array([P ** -0.5, P ** -0.5, 1.0], f32)}
    xw = l1("xproj_w").transpose(0, 2, 1).reshape(LAYERS, 2, P, RANK + 2 * STATES)
    xproj = np.zeros((LAYERS, 2, P, P), f32)
    xproj[..., 0:RANK] = xw[..., 0:RANK]
    for q in range(1, 4):
        xproj[..., 32 * q:32 * q + 32] = xw[..., RANK:]
    dtproj = np.zeros((LAYERS, P, 2 * P), f32)
    dtproj[:, 0:RANK] = l1("dtproj_w").transpose(0, 2, 1)
    dtproj[:, RANK] = l1("dtproj_b")

    def halves(w):
        return w.reshape(LAYERS, 2, P, -1).transpose(0, 2, 1, 3).reshape(LAYERS, P, -1)

    lw = {"ln1_g": l1("ln1_g")[:, :, None], "ln1_b": l1("ln1_b")[:, :, None], "in_w": l1("in_w").transpose(0, 2, 1),
          "conv_w": halves(l1("conv_w")), "conv_b": halves(l1("conv_b")), "xproj": halves(xproj.reshape(LAYERS, 2 * P, P)),
          "dtproj": dtproj, "A_log": halves(l1("A_log")), "D_skip": halves(l1("D_skip")),
          "out_w": halves(l1("out_w").transpose(0, 2, 1)), "ln2_g": l1("ln2_g")[:, :, None],
          "ln2_b": l1("ln2_b")[:, :, None], "w1": l1("mlp_w1").transpose(0, 2, 1), "b1": halves(l1("mlp_b1")),
          "w2": halves(l1("mlp_w2").transpose(0, 2, 1)), "b2": l1("mlp_b2")[:, :, None]}
    layers = np.concatenate([lw[n] for n in LW], axis=2)
    selcol = np.zeros((P, 2 * STATES + HEADS + EXPERTS + 1), f32)
    for n in range(2 * STATES):
        selcol[[32 + n, 64 + n, 96 + n], n] = 1.0
    for n in range(HEADS):
        selcol[DH * n:DH * n + DH, 2 * STATES + n] = 1.0
    for n in range(EXPERTS):
        selcol[n, 2 * STATES + HEADS + n] = 1.0
    selcol[RANK, -1] = 1.0
    arrays = {
        "x_t": i["x"].transpose(2, 0, 1), "tok_w": i["L0_tok_W"].T,
        "cols": np.stack([cols[n] for n in COLS], axis=1), "mats": np.stack([mats[n] for n in MATS], axis=1),
        "rows": np.concatenate([rows[n] for n, _ in ROWS]), "layers": layers,
        "w1": f1("W1").transpose(1, 0, 2), "w2": f1("W2").reshape(EXPERTS, HID // P, P, P).transpose(2, 0, 1, 3),
        "moe_rows": np.concatenate([f1("b1"), f1("b2")], axis=1), "wg": f1("Wg"),
        "ident": np.eye(P, dtype=f32), "selcol": selcol,
    }
    arrays = {k + "_dram": np.ascontiguousarray(v) for k, v in arrays.items()}
    nc = bacc.Bacc("TRN2", target_bir_lowering=False, num_devices=1)
    aps = {k[:-5]: nc.dram_tensor(k, v.shape, mybir.dt.float32, kind="ExternalInput").ap() for k, v in arrays.items()}
    out = nc.dram_tensor("out_dram", (P, G, N), mybir.dt.float32, kind="ExternalOutput").ap()
    audio_tower(nc, *[aps[n] for n in ORDER], out)
    r = run_bass_kernel_spmd(nc, [arrays], core_ids=[0])
    return np.ascontiguousarray(r.results[0]["out_dram"].reshape(P, B, T).transpose(1, 2, 0))
```

```python
from contextlib import ExitStack

import concourse.bass as bass
from concourse import mybir

F32 = mybir.dt.float32
BF16 = mybir.dt.bfloat16
U32 = mybir.dt.uint32
ALU = mybir.AluOpType
ACT = mybir.ActivationFunctionType
AX = mybir.AxisListType

P = 128
B, T_IN, D_IN = 32, 125, 23
CONTEXT = 5
T = T_IN - CONTEXT + 1
GB = 4
G = B // GB
N = GB * T
BANK = 512
TD = (T + 2 - 3) // 2 + 1
FK = CONTEXT * D_IN
EPS = 1e-5
LAYERS = 5
STATES = 16
RANK = 8
HEADS, DH = 8, 16
EXPERTS, HID = 8, 512
FP8_MAX = 448.0

COLS = ["tok_b", "tok_gamma", "tok_beta", "db", "bq_cr", "bk_cr", "bq_d", "bk_d", "bq_c", "bk_c",
        "bq", "bk", "bv", "bo", "g1", "beta1", "g2", "beta2"] + [f"gw{k}" for k in range(9)]
COL = {n: i for i, n in enumerate(COLS)}
MATS = ["dw0", "dw1", "dw2", "wq_cr", "wk_cr", "wv_cr", "wq_d", "wk_d", "wq_c", "wk_c", "wv_d", "wv_c", "ffn",
        "Wq", "Wk", "Wv", "Wo"]
MAT = {n: i for i, n in enumerate(MATS)}
ROWS = [("bv", 384), ("ln_g", 384), ("ln_b", 384), ("gb", 3), ("temp", 1), ("bg", EXPERTS),
        ("places", EXPERTS), ("scales", 3)]
ROW = {}
for _n, _k in ROWS:
    ROW[_n] = (sum(v[1] - v[0] for v in ROW.values()), sum(v[1] - v[0] for v in ROW.values()) + _k)
ROW_ALL = sum(k for _, k in ROWS)
LW = {}
for _n, _k in [("ln1_g", 1), ("ln1_b", 1), ("in_w", 512), ("conv_w", 8), ("conv_b", 2), ("xproj", 256),
               ("dtproj", 256), ("A_log", 32), ("D_skip", 2), ("out_w", 256), ("ln2_g", 1), ("ln2_b", 1),
               ("w1", 256), ("b1", 2), ("w2", 256), ("b2", 1)]:
    LW[_n] = (sum(v[1] - v[0] for v in LW.values()), sum(v[1] - v[0] for v in LW.values()) + _k)
LW_ALL = max(v[1] for v in LW.values())


ARENA = 31500


class Count:

    def __init__(self, sem, per=1, credit=0):
        self.sem, self.per, self.credit = sem, per, credit

    def at(self, r, k=None):
        return self.credit + self.per * r + (self.per if k is None else k)


def audio_tower(nc, x_t, tok_w, cols_d, mats_d, rows_d, layers_d, w1_d, w2_d, moe_rows_d, wg_d, ident_d, selcol_d, out):
    with ExitStack() as ctx:
        def sb(name, shape, dt=F32):
            return ctx.enter_context(nc.sbuf_tensor(name, shape, dt))

        def count(name, per=1, credit=0):
            c = Count(ctx.enter_context(nc.semaphore(name)), per, credit)
            if credit:
                credits.append(c)
            return c

        arena = sb("arena", [P, ARENA])

        def stage():
            used = [0]

            def place(_, shape, dtype=F32):
                n = 1
                for k in shape[1:]:
                    n *= k
                words = n if dtype == F32 else (n + 1) // 2
                flat = arena[0:shape[0], used[0]:used[0] + words]
                used[0] += words
                assert used[0] <= ARENA
                if dtype != F32:
                    flat = flat.bitcast(dtype)
                if len(shape) == 2:
                    return flat
                names = "abcd"[:len(shape) - 1]
                return flat.rearrange("p (%s) -> p %s" % (" ".join(names), " ".join(names)),
                                      **dict(zip(names[1:], shape[2:])))
            return place

        credits = []
        ps = ctx.enter_context(nc.psum_tensor("ps", [P, 8, BANK], F32))

        def bank(k):
            return ps[:, k, 0:N]

        def bank4(k):
            return ps[:, k, 0:N].rearrange("p (b t) -> p b t", b=GB)

        cols = sb("cols", [P, len(COLS)])
        mats = sb("mats", [P, len(MATS), P])
        rows = sb("rows", [P, ROW_ALL])
        ident = sb("ident", [P, P])
        mean_w = sb("mean_w", [P, P])
        ones_w = sb("ones_w", [P, P])
        eps_c = sb("eps_c", [P, 1])

        def col(name):
            return cols[:, COL[name]:COL[name] + 1]

        def mat(name, k=1):
            return mats[:, MAT[name]:MAT[name] + k, :].rearrange("p a b -> p (a b)")

        def row(name, n=P):
            return rows[0:n, ROW[name][0]:ROW[name][1]]

        h = sb("h", [P, G, N])
        xs = sb("xs", [P, G, N])

        param = count("param")
        consts = count("consts")

        ln_mean = count("ln_mean")
        ln_cent = count("ln_cent")
        ln_square = count("ln_square")
        ln_var = count("ln_var")
        ln_log = count("ln_log", credit=1)
        ln_rstd = count("ln_rstd")
        cent = sb("cent", [P, N])
        rstd = sb("rstd", [P, N])
        LNB = 0

        def ln_pe(pe, u, src):
            pe.wait_ge(ln_log.sem, ln_log.at(u - 1))
            nc.tensor.matmul(bank(LNB), mean_w[:], src, start=True, stop=True).then_inc(ln_mean.sem, 1)
            pe.wait_ge(ln_square.sem, ln_square.at(u))
            nc.tensor.matmul(bank(LNB), mean_w[:], rstd[:], start=True, stop=True).then_inc(ln_var.sem, 1)

        def ln_act(act, u):
            act.wait_ge(ln_cent.sem, ln_cent.at(u))
            nc.scalar.activation(rstd[:], cent[:], ACT.Square).then_inc(ln_square.sem, 1)
            act.wait_ge(ln_var.sem, ln_var.at(u))
            nc.scalar.activation(rstd[:], bank(LNB), ACT.Ln, bias=eps_c[:]).then_inc(ln_log.sem, 1)
            act.wait_ge(ln_log.sem, ln_log.at(u))
            nc.scalar.activation(rstd[:], rstd[:], ACT.Exp, scale=-0.5).then_inc(ln_rstd.sem, 1)

        def ln_dve(dve, u, src):
            dve.wait_ge(ln_mean.sem, ln_mean.at(u))
            nc.vector.tensor_tensor(cent[:], src, bank(LNB), ALU.subtract).then_inc(ln_cent.sem, 1)
            dve.wait_ge(ln_rstd.sem, ln_rstd.at(u))

        tok_ws = sb("tok_ws", [FK, P])
        tok_mm = count("tok_mm")
        tok_y = count("tok_y")
        tok_stats = count("tok_stats", G)
        tok_norm = count("tok_norm")
        bn = sb("bn", [P, G, 6])
        bn_mv = sb("bn_mv", [P, 2])
        bn_sc = sb("bn_sc", [P, 4])
        bn_step = count("bn_step")
        frames_in = count("frames_in")
        h_tok = count("h_tok")

        att = stage()
        xp = att("xp", [P, GB, T + 2])
        xd = att("xd", [P, GB, TD])
        q_cr, q_d, q_c, k_d, k_c = (att(n, [P, GB, T]) for n in ("q_cr", "q_d", "q_c", "k_d", "k_c"))
        k_cr = att("k_cr", [P, GB, TD])
        v_dc = att("v_dc", [T, GB, 2 * P])
        v_cr = att("v_cr", [TD, GB, P])
        nq = att("nq", [P, 2, N])
        SC = TD + 2 * T
        prob = att("prob", [T, GB, SC])
        probT = att("probT", [T, GB, 3 * T])
        nmax = att("nmax", [T, GB, 3])
        nbias = att("nbias", [T, GB, 3])
        rsum = att("rsum", [T, GB, 3])
        rinv = att("rinv", [T, GB, 3])
        ao = att("ao", [T, GB, 3, P])
        ast = att("ast", [T, GB, 3, 6])
        amv = att("amv", [T, GB * 3, 2])
        ad = att("ad", [T, GB * 3])
        ars = att("ars", [T, GB * 3])
        aoT = att("aoT", [P, 2, 3, T])
        glog = att("glog", [T, GB, 3])
        gmx = att("gmx", [T, GB])
        z = att("z", [T, GB, P])
        rtemp = sb("rtemp", [P, 1])
        BR = [(0, TD), (TD, TD + T), (TD + T, SC)]
        KEYS = [TD, T, T]

        xn_ready = count("xn_ready")
        at_conv = count("at_conv")
        at_xd = count("at_xd")
        at_proj = count("at_proj", 5)
        at_kcr = count("at_kcr")
        at_q_act = count("at_q_act", 4)
        at_qc = count("at_qc")
        at_kcr_out = count("at_kcr_out")
        at_v = count("at_v", 3)
        at_v_out = count("at_v_out", 3)
        at_sq = count("at_sq", 2)
        at_ss = count("at_ss", 2)
        at_nrm = count("at_nrm", 8)
        at_qkn = count("at_qkn", 2)
        at_score = count("at_score", GB)
        at_max = count("at_max", 4)
        at_bias = count("at_bias", 2)
        at_exp = count("at_exp", GB)
        at_rinv = count("at_rinv")
        at_pt = count("at_pt", GB)
        at_pt_out = count("at_pt_out", GB)
        at_o = count("at_o", GB)
        at_on = count("at_on")
        at_st = count("at_st", 4)
        at_log = count("at_log")
        at_rstd = count("at_rstd")
        at_aff = count("at_aff", 3)
        at_aot = count("at_aot", GB)
        at_aot_out = count("at_aot_out", GB)
        at_logit = count("at_logit", GB)
        at_gate = count("at_gate", 3)
        at_gexp = count("at_gexp")
        at_gn = count("at_gn", 3)
        at_z = count("at_z", 3)
        at_zt = count("at_zt")
        h_attn = count("h_attn", credit=1)
        norm_c = sb("norm_c", [P, 2])
        GATE_B = 6

        def attention_groups(eng, body):
            body(0, None)
            with eng.Fori(1, G) as g:
                body(g, g - 1)
            body(None, G - 1)

        def hgroup(g):
            return h[:, g, :] if isinstance(g, int) else h[:, bass.ds(g, 1), :].squeeze(1)

        fx = count("fx", credit=0)
        f_max = count("f_max")
        f_gmax = count("f_gmax")
        f_step = count("f_step")
        f_q = count("f_q", 6)
        f_wq = count("f_wq")
        f_mm = count("f_mm")
        h_ffn = count("h_ffn")
        ffn = stage()
        famax = ffn("famax", [P, G + 1])
        f_wstep = count("f_wstep", 6)
        fpair = ffn("fpair", [P, 2])
        fall = ffn("fall", [P, 2])
        fsc = ffn("fsc", [P, 4])
        wq8 = ffn("wq8", [P, P], BF16)
        wtmp = ffn("wtmp", [P, 3, P])
        ftmp = ffn("ftmp", [P, 2, N])
        xq8 = ffn("xq8", [P, N], BF16)
        C2 = 2 * N
        PRE = ["ln1_g", "ln1_b", "in_w", "conv_w", "conv_b", "xproj", "dtproj"]
        POST = ["D_skip", "out_w", "ln2_g", "ln2_b", "w1", "b1", "w2", "b2"]
        PRE_N = LW["dtproj"][1]
        POST_0 = LW["D_skip"][0]
        wp = sb("wp", [P, PRE_N])
        wo = sb("wo", [P, LW_ALL - POST_0])

        def pw(name, lo=0, n=None):
            a, b = LW[name]
            return wp[:, a + lo:(b if n is None else a + lo + n)]

        def ow(name, lo=0, n=None):
            a, b = LW[name]
            return wo[:, a + lo - POST_0:(b if n is None else a + lo + n) - POST_0]

        nega = sb("nega", [P, LAYERS, 2 * STATES])
        selcol = sb("selcol", [P, 2 * STATES + HEADS + EXPERTS + 1])
        sel = sb("sel", [P, 2 * STATES, P], BF16)
        ssm = stage()
        LAG = 3
        DB = 4
        dt = ssm("dt", [P, 2, 2, N])
        u = ssm("u", [P, 2, 2, N])
        xc = ssm("xc", [P, 2, 2, N])
        sz = ssm("sz", [P, 2, 2, N])
        bc = ssm("bc", [P, 2, N], BF16)
        dA = ssm("dA", [P, DB, 2, N])
        db = ssm("db", [P, 2, 2, N])
        hs = ssm("hs", [P, DB, 2, N])
        cb = ssm("cb", [P, DB, N])
        gq = ssm("gq", [P, DB, 2, N])
        xn = ssm("xn", [P, N])
        sig_x = ssm("sig_x", [P, 2, N])
        sig_z = ssm("sig_z", [P, 2, N])
        spx = ssm("spx", [P, 2, N])
        drow = ssm("drow", [P, N])
        resid = ssm("resid", [P, N])
        yv = ssm("yv", [P, 2, N])
        xn2 = ssm("xn2", [P, N])
        gl = ssm("gl", [P, 2, N])
        LP, Y, BB, CC, L0 = LNB, 1, 3, 5, 6

        wp_in, wo_in = count("wp_in", 16), count("wo_in", 16)
        a_in = count("a_in", 16)
        sel_in = count("sel_in", 16)
        sel_made = count("sel_made")
        a_neg = count("a_neg", 2)
        x_in = count("x_in")
        p_xn = count("p_xn", 2)
        p_xin = count("p_xin")
        p_conv = count("p_conv", 5)
        p_sx = count("p_sx", 3)
        p_xc = count("p_xc")
        p_z = count("p_z")
        p_zc = count("p_zc")
        p_sz = count("p_sz", 3)
        p_silz = count("p_silz")
        p_xp = count("p_xp")
        p_bc = count("p_bc", 3)
        p_drow = count("p_drow")
        p_dtm = count("p_dtm")
        p_clip = count("p_clip", 2)
        p_sp = count("p_sp", 2)
        p_dt = count("p_dt")
        p_u = count("p_u")
        s_b = count("s_b", STATES)
        s_c = count("s_c", STATES)
        s_da = count("s_da", STATES)
        s_cb = count("s_cb", STATES, credit=2)
        s_db = count("s_db", STATES, credit=2)
        s_h = count("s_h", STATES, credit=DB)
        s_gq = count("s_gq", STATES, credit=DB)
        s_sum = count("s_sum", STATES, credit=DB)
        o_y = count("o_y", 1, credit=1)
        o_yg = count("o_yg")
        o_out = count("o_out")
        o_x = count("o_x")
        o_xn = count("o_xn", 2)
        o_m1 = count("o_m1")
        o_gl = count("o_gl")
        o_m2 = count("o_m2")
        o_x2 = count("o_x2", 1, credit=1)
        h_mamba = count("h_mamba")
        ROUNDS = LAYERS * G
        LN0 = 3 * G

        SLOT = dict(pre_mean=0, pre_cent=0, pre_square=1, pre_var=1, pre_rstd=2, pre_xn=2, in_x=2, conv=(3, 3, 4, 4),
                    floor=5, sig_x=(6, 6, 7), in_z=5, xc=7, zclip=7, xproj=7, drow=8, sig_z=(14, 14, 14), split=9,
                    dtproj=9, clip=10, softplus=(11, 11), silz=15, dt=12, u=13,
                    y=3, out=4, x=4, post_mean=5, post_cent=5, post_square=6, post_var=6, post_rstd=7, post_xn=8,
                    mlp1=11, gelu=12, mlp2=12, x2=13)

        def mamba_rounds(eng, body, post):
            body(0, 0, LN0 + 1, None)
            with eng.Fori(0, (ROUNDS - 2) // 2) as q:
                j = q * 2 + 1
                body(j, 1, j * 2 + LN0, j * 2 + (LN0 + 1))
                body(j + 1, 0, j * 2 + (LN0 + 2), j * 2 + (LN0 + 3))
            last = ROUNDS - 1
            body(last, last % 2, None, LN0 + 2 * last)
            post(last, last % 2, LN0 + 2 * last + 1)

        wg = sb("wg", [P, EXPERTS])
        moe_b = sb("moe_b", [EXPERTS, HID + P])
        UH = HEADS // 2
        UNITS = 2 * GB
        last = stage()
        w1 = last("w1", [P, EXPERTS, HID])
        w2 = last("w2", [P, EXPERTS, HID // P, P])
        esel = last("esel", [P, EXPERTS, P], BF16)
        xe = last("xe", [P, N])
        qh = last("qh", [P, N])
        qm = last("qm", [P, HEADS, N])
        kh = last("kh", [P, N])
        vh = last("vh", [T, GB, P])
        mp_ = last("mp_", [T, 2, UH, T])
        mpT = last("mpT", [T, 2, UH, T])
        mmax = last("mmax", [T, 2, UH])
        msum = last("msum", [T, GB, HEADS])
        mctx = last("mctx", [T, GB, P])
        ctxT = last("ctxT", [P, N])
        r1 = last("r1", [P, N])
        x1 = last("x1", [P, N])
        lg = last("lg", [T, GB, EXPERTS])
        eq = last("eq", [T, GB, EXPERTS])
        lmx = last("lmx", [T, GB])
        ohT = last("ohT", [EXPERTS, N])
        ohb = last("ohb", [P, N], BF16)
        mask = last("mask", [P, EXPERTS, N])
        xm = last("xm", [P, 2, N])
        gh = last("gh", [P, HID // P, N])
        yt = last("yt", [P, 2, N])
        acc = last("acc", [P, N])
        moe_in = count("moe_in", 16)
        m_const = count("m_const")
        m_xe = count("m_xe")
        m_qk = count("m_qk", 3)
        m_qk_out = count("m_qk_out", 3)
        m_qm = count("m_qm")
        m_sc = count("m_sc", UNITS)
        m_mx = count("m_mx", 2 * UNITS)
        m_exp = count("m_exp", UNITS)
        m_ri = count("m_ri")
        m_pt = count("m_pt", UNITS)
        m_pt_out = count("m_pt_out", UNITS)
        m_ctx = count("m_ctx", UNITS)
        m_ctx_n = count("m_ctx_n")
        m_ct = count("m_ct")
        m_ct_out = count("m_ct_out")
        m_sa = count("m_sa")
        m_r1 = count("m_r1")
        m_x1 = count("m_x1", 2)
        m_lg = count("m_lg")
        m_top = count("m_top", 6)
        m_oh = count("m_oh")
        m_oh_out = count("m_oh_out", 2)
        m_mask = count("m_mask", EXPERTS)
        m_mask_out = count("m_mask_out", EXPERTS)
        m_xm = count("m_xm", EXPERTS)
        m_hid_e = count("m_hid_e", EXPERTS - 1)
        m_hid = count("m_hid", HID // P)
        m_gelu = count("m_gelu", HID // P)
        m_b2 = count("m_b2")
        m_y = count("m_y", EXPERTS)
        m_yt = count("m_yt", EXPERTS)
        m_acc = count("m_acc", EXPERTS + 1)
        m_g2 = count("m_g2")
        h_out = count("h_out")
        LE = LN0 + 2 * ROUNDS
        HALF = 2 * EXPERTS
        SLOTS = 2 * HALF
        CTX, HB, MK, QB = LNB, 1, 5, 6
        AT = dict(mean=0, var=1, qkv=3, scores=5, probs=7, context=9, ctx_t=25, sa=26, post_mean=27, post_var=28,
                  logits=29, onehot=31)

        def unit_at(s, what):
            k, rest = divmod(s - AT[what], 2)
            return k if rest == 0 and 0 <= k < UNITS else None

        def tower_end(eng, body):
            body(None, 0, LE)
            with eng.Fori(0, G - 1) as g:
                body(g, g + 1, g * 3 + (LE + 2))
            body(G - 1, None, LE + 3 * G - 1)

        out_done = count("out_done")

        block = ctx.enter_context(nc.Block())

        @block.sync
        def _(sp):
            for c in credits:
                sp.sem_inc(c.sem, c.credit)
            frames = xs[0:FK, :, :].rearrange("p g (b t) -> p (g b) t", b=GB)
            for k in range(CONTEXT):
                sp.dma_start(frames[k * D_IN:(k + 1) * D_IN, :, :], x_t[:, :, k:k + T]).then_inc(frames_in.sem, 16)
            sp.dma_start(tok_ws[:], tok_w).then_inc(frames_in.sem, 16)
            sp.dma_start(cols[:], cols_d).then_inc(frames_in.sem, 16)
            sp.dma_start(mats[:], mats_d).then_inc(param.sem, 16)
            sp.dma_start(ident[:], ident_d).then_inc(param.sem, 16)
            sp.dma_start(rows[:], rows_d.partition_broadcast(P)).then_inc(param.sem, 16)
            sp.dma_start(nega[:], layers_d[:, :, LW["A_log"][0]:LW["A_log"][1]].rearrange("l p c -> p l c"))\
                .then_inc(a_in.sem, 16)
            sp.dma_start(selcol[:], selcol_d).then_inc(sel_in.sem, 16)
            sp.dma_start(wp[:], layers_d[0, :, 0:PRE_N]).then_inc(wp_in.sem, 16)
            sp.dma_start(wo[:], layers_d[0, :, POST_0:LW_ALL]).then_inc(wo_in.sem, 16)
            with sp.Fori(1, LAYERS) as l:
                sp.wait_ge(p_dtm.sem, p_dtm.at(l * G - 1))
                sp.dma_start(wp[:], layers_d[bass.ds(l, 1), :, 0:PRE_N].squeeze(0)).then_inc(wp_in.sem, 16)
                sp.wait_ge(o_x2.sem, o_x2.at(l * G - 1))
                sp.dma_start(wo[:], layers_d[bass.ds(l, 1), :, POST_0:LW_ALL].squeeze(0)).then_inc(wo_in.sem, 16)
            sp.wait_ge(h_mamba.sem, h_mamba.at(G - 1))
            sp.dma_start(w1[:], w1_d).then_inc(moe_in.sem, 16)
            sp.dma_start(w2[:], w2_d).then_inc(moe_in.sem, 16)
            sp.dma_start(wg[:], wg_d).then_inc(moe_in.sem, 16)
            sp.dma_start(moe_b[:], moe_rows_d).then_inc(moe_in.sem, 16)
            with sp.Fori(0, G) as g:
                sp.wait_ge(h_out.sem, h_out.at(g))
                sp.dma_start(out[:, bass.ds(g, 1), :], h[:, bass.ds(g, 1), :]).then_inc(out_done.sem, 16)
            sp.wait_ge(out_done.sem, 16 * G)

        PARAM_ALL = 16 * 3
        FRAMES_ALL = 16 * (CONTEXT + 2)

        @block.tensor
        def _(pe):
            pe.wait_ge(frames_in.sem, FRAMES_ALL)
            with pe.Fori(0, G) as g:
                nc.tensor.matmul(ps[:, g, 0:N], tok_ws[:], xs[0:FK, g, :], start=True, stop=True)\
                    .then_inc(tok_mm.sem, 1)
            pe.wait_ge(consts.sem, 1)
            pe.wait_ge(param.sem, PARAM_ALL)
            pe.wait_ge(tok_y.sem, tok_y.at(G - 1))

            def pe_project(g):
                pe.wait_ge(h_tok.sem, h_tok.at(g))
                ln_pe(pe, g, hgroup(g))
                pe.wait_ge(xn_ready.sem, xn_ready.at(g))
                for k in range(3):
                    mm = nc.tensor.matmul(ps[:, 1, 0:GB * TD], mat(f"dw{k}"), xp[:, :, k:k + 2 * TD - 1:2],
                                          start=(k == 0), stop=(k == 2))
                mm.then_inc(at_conv.sem, 1)
                for i, w in enumerate(("wq_cr", "wq_d", "wq_c", "wk_d", "wk_c")):
                    nc.tensor.matmul(bank(2 + i), mat(w), xp[:, :, 1:T + 1], start=True, stop=True)\
                        .then_inc(at_proj.sem, 1)
                for b in range(GB):
                    mm = nc.tensor.matmul(ps[0:T, (7, 0)[b // 2], 256 * (b % 2):256 * (b % 2) + 256],
                                          xp[:, b, 1:T + 1], mat("wv_d", 2), start=True, stop=True)
                    if b % 2:
                        mm.then_inc(at_v.sem, 1)
                pe.wait_ge(at_xd.sem, at_xd.at(g))
                nc.tensor.matmul(ps[:, 1, 0:GB * TD], mat("wk_cr"), xd[:], start=True, stop=True)\
                    .then_inc(at_kcr.sem, 1)
                pe.wait_ge(at_q_act.sem, at_q_act.at(g, 3))
                for b in range(GB):
                    mm = nc.tensor.matmul(ps[0:TD, 5, P * b:P * b + P], xd[:, b, :], mat("wv_cr"),
                                          start=True, stop=True)
                mm.then_inc(at_v.sem, 1)

            def pe_square_sums(g):
                pe.wait_ge(at_qc.sem, at_qc.at(g))
                for k, i in enumerate((1, 0)):
                    pe.wait_ge(at_sq.sem, at_sq.at(g, k + 1))
                    nc.tensor.matmul(bank((4, 3)[i]), ones_w[:], nq[:, i, :], start=True, stop=True)\
                        .then_inc(at_ss.sem, 1)

            def pe_gate_transposed(g, b):
                if b >= 2:
                    pe.wait_ge(at_aot_out.sem, at_aot_out.at(g, b - 1))
                for i in range(3):
                    mm = nc.tensor.transpose(ps[:, (5, 7)[b % 2], T * i:T * i + T], ao[:, b, i, :],
                                             ident[0:T, 0:T])
                mm.then_inc(at_aot.sem, 1)

            def pe_gate_logits(g, b):
                pe.wait_ge(at_aot_out.sem, at_aot_out.at(g, b + 1))
                for i in range(3):
                    gw = cols[:, COL["gw0"] + 3 * i:COL["gw0"] + 3 * i + 3]
                    mm = nc.tensor.matmul(ps[0:T, GATE_B, 3 * b:3 * b + 3], aoT[:, b % 2, i, :], gw,
                                          start=(i == 0), stop=(i == 2))
                mm.then_inc(at_logit.sem, 1)

            def pe_scores(g):
                pe.wait_ge(at_kcr_out.sem, at_kcr_out.at(g))
                pe.wait_ge(at_qkn.sem, at_qkn.at(g))
                pe.wait_ge(at_v_out.sem, at_v_out.at(g))
                for b in range(GB):
                    for (lo, hi), q, k in zip(BR, (q_cr, q_d, q_c), (k_cr, k_d, k_c)):
                        mm = nc.tensor.matmul(ps[0:T, b, lo:hi], q[:, b, :], k[:, b, :], start=True, stop=True)
                    mm.then_inc(at_score.sem, 1)

            def pe_outputs(g):
                def outputs(b):
                    pe.wait_ge(at_pt_out.sem, at_pt_out.at(g, b + 1))
                    for i in range(3):
                        v = v_cr[:, b, :] if i == 0 else v_dc[:, b, P * (i - 1):P * i]
                        mm = nc.tensor.matmul(ps[0:T, b, P * i:P * i + P], probT[0:KEYS[i], b, T * i:T * i + T], v,
                                              start=True, stop=True)
                    mm.then_inc(at_o.sem, 1)

                for b in range(GB):
                    pe.wait_ge(at_exp.sem, at_exp.at(g, b + 1))
                    for i in (1, 2, 0):
                        lo, hi = BR[i]
                        mm = nc.tensor.transpose(ps[0:KEYS[i], b, T * i:T * i + T], prob[:, b, lo:hi],
                                                 ident[0:T, 0:T])
                    mm.then_inc(at_pt.sem, 1)
                    if b:
                        outputs(b - 1)
                outputs(GB - 1)

            def pe_mix(g):
                pe.wait_ge(at_z.sem, at_z.at(g))
                for b in range(GB):
                    mm = nc.tensor.transpose(ps[:, GATE_B, T * b:T * b + T], z[:, b, :], ident[0:T, 0:T])
                mm.then_inc(at_zt.sem, 1)

            def pe_attention_groups(ga, gb):
                if ga is not None:
                    if gb is not None:
                        pe.wait_ge(at_on.sem, at_on.at(gb))
                        pe.wait_ge(h_attn.sem, h_attn.at(gb - 1))
                    pe_project(ga)
                if gb is not None:
                    if ga is not None:
                        pe.wait_ge(at_v_out.sem, at_v_out.at(ga))
                        pe.wait_ge(at_q_act.sem, at_q_act.at(ga))
                    pe.wait_ge(at_aff.sem, at_aff.at(gb))
                    pe_gate_transposed(gb, 0)
                    pe_gate_transposed(gb, 1)
                if ga is not None:
                    pe_square_sums(ga)
                if gb is not None:
                    for b in range(GB):
                        pe_gate_logits(gb, b)
                        if b + 2 < GB:
                            pe_gate_transposed(gb, b + 2)
                if ga is not None:
                    pe_scores(ga)
                    pe_outputs(ga)
                if gb is not None:
                    pe_mix(gb)

            attention_groups(pe, pe_attention_groups)

            with pe.Fori(0, G) as g:
                ln_pe(pe, g + G, h[:, g, :])
            pe.wait_ge(f_wq.sem, 1)
            with pe.Fori(0, G) as g:
                pe.wait_ge(f_q.sem, f_q.at(g))
                nc.tensor.matmul(ps[:, g, 0:N], wq8[:], xq8[:], start=True, stop=True).then_inc(f_mm.sem, 1)
            with pe.Fori(0, G) as g:
                ln_pe(pe, g + 2 * G, h[:, g, :])

            def pe_norm_mean(uu, src):
                pe.wait_ge(ln_log.sem, ln_log.at(uu - 1))
                nc.tensor.matmul(bank(LNB), mean_w[:], src, start=True, stop=True).then_inc(ln_mean.sem, 1)

            def pe_norm_var(uu):
                pe.wait_ge(ln_square.sem, ln_square.at(uu))
                nc.tensor.matmul(bank(LNB), mean_w[:], rstd[:], start=True, stop=True).then_inc(ln_var.sem, 1)

            def pre_in_x(j, par):
                pe.wait_ge(p_xn.sem, p_xn.at(j))
                pe.wait_ge(wp_in.sem, wp_in.at(j // G))
                for i in range(2):
                    mm = nc.tensor.matmul(bank(L0 + i), pw("in_w", P * i, P), xn[:], start=True, stop=True)
                mm.then_inc(p_xin.sem, 1)

            def pre_in_z(j, par):
                pe.wait_ge(p_conv.sem, p_conv.at(j, 4))
                for i in range(2):
                    mm = nc.tensor.matmul(bank(L0 + i), pw("in_w", P * (2 + i), P), xn[:], start=True, stop=True)
                mm.then_inc(p_z.sem, 1)

            def pre_xproj(j, par):
                pe.wait_ge(p_xc.sem, p_xc.at(j))
                pe.wait_ge(p_zc.sem, p_zc.at(j))
                for i in range(2):
                    mm = nc.tensor.matmul(bank(L0), pw("xproj", P * i, P), xc[:, par, i, :],
                                          start=(i == 0), stop=(i == 1))
                mm.then_inc(p_xp.sem, 1)

            def pre_dtproj(j, par):
                pe.wait_ge(p_drow.sem, p_drow.at(j))
                pe.wait_ge(p_bc.sem, p_bc.at(j))
                for i in range(2):
                    mm = nc.tensor.matmul(bank(L0 + i), pw("dtproj", P * i, P), drow[:], start=True, stop=True)
                mm.then_inc(p_dtm.sem, 1)

            def scan_c(j, par, n):
                par, row = (par, n) if n < STATES else (1 - par, n - STATES)
                pe.wait_ge(s_cb.sem, s_cb.at(j, n))
                nc.tensor.matmul(bank(CC), sel[:, STATES + row, :], bc[:, par, :], start=True, stop=True)\
                    .then_inc(s_c.sem, 1)

            def scan_b(j, par, n):
                if n % STATES == 0:
                    pe.wait_ge(p_bc.sem, p_bc.at(j + n // STATES))
                par, row = (par, n) if n < STATES else (1 - par, n - STATES)
                pe.wait_ge(s_db.sem, s_db.at(j, n - 1))
                nc.tensor.matmul(bank(BB + n % 2), sel[:, row, :], bc[:, par, :], start=True, stop=True)\
                    .then_inc(s_b.sem, 1)

            def scan_sum(j, n):
                pe.wait_ge(s_gq.sem, s_gq.at(j, n + 1))
                if n == 0:
                    pe.wait_ge(o_y.sem, o_y.at(j - 1))
                for i in range(2):
                    mm = nc.tensor.matmul(bank(Y + i), ident[:], gq[:, n % DB, i, :],
                                          start=(n == 0), stop=(n % STATES == STATES - 1))
                mm.then_inc(s_sum.sem, 1)

            def post_out(j, uu):
                pe.wait_ge(ln_log.sem, ln_log.at(uu - 1))
                pe.wait_ge(o_yg.sem, o_yg.at(j))
                pe.wait_ge(wo_in.sem, wo_in.at(j // G))
                for i in range(2):
                    mm = nc.tensor.matmul(bank(LP), ow("out_w", P * i, P), yv[:, i, :], start=(i == 0), stop=(i == 1))
                mm.then_inc(o_out.sem, 1)

            def post_mlp1(j):
                pe.wait_ge(o_xn.sem, o_xn.at(j))
                for i in range(2):
                    mm = nc.tensor.matmul(bank(L0 + i), ow("w1", P * i, P), xn2[:], start=True, stop=True)
                mm.then_inc(o_m1.sem, 1)

            def post_mlp2(j):
                pe.wait_ge(o_gl.sem, o_gl.at(j))
                for i in range(2):
                    mm = nc.tensor.matmul(bank(LP), ow("w2", P * i, P), gl[:, i, :], start=(i == 0), stop=(i == 1))
                mm.then_inc(o_m2.sem, 1)

            def xgroup(j):
                return xs[:, j % G, :] if isinstance(j, int) else xs[:, bass.ds(j % G, 1), :].squeeze(1)

            def pe_round(j, par, u_pre, u_post):
                for n in range(STATES):
                    if n + 1 < STATES or u_pre is not None:
                        scan_c(j, par, n + 1)
                    if n + 2 < STATES or u_pre is not None:
                        scan_b(j, par, n + 2)
                    if n >= LAG or u_post is not None:
                        scan_sum(j, n - LAG)
                    if u_pre is not None:
                        if n == SLOT["pre_mean"]:
                            if u_post is not None:
                                pe.wait_ge(o_x2.sem, o_x2.at(j - 2))
                            pe_norm_mean(u_pre, xgroup(j + 1))
                        if n == SLOT["pre_var"]:
                            pe_norm_var(u_pre)
                        if n == SLOT["in_x"]:
                            pre_in_x(j + 1, 1 - par)
                        if n == SLOT["in_z"]:
                            pre_in_z(j + 1, 1 - par)
                        if n == SLOT["xproj"]:
                            pre_xproj(j + 1, 1 - par)
                        if n == SLOT["dtproj"]:
                            pre_dtproj(j + 1, 1 - par)
                    if u_post is not None:
                        if n == SLOT["out"]:
                            post_out(j - 1, u_post)
                        if n == SLOT["post_mean"]:
                            pe.wait_ge(o_x.sem, o_x.at(j - 1))
                            pe_norm_mean(u_post, resid[:])
                        if n == SLOT["post_var"]:
                            pe_norm_var(u_post)
                        if n == SLOT["mlp1"]:
                            if u_pre is not None:
                                pe.wait_ge(p_clip.sem, p_clip.at(j + 1))
                            post_mlp1(j - 1)
                        if n == SLOT["mlp2"]:
                            post_mlp2(j - 1)
                if u_pre is None:
                    for n in range(STATES - LAG, STATES):
                        scan_sum(j, n)

            def pe_post(j, par, uu):
                post_out(j, uu)
                pe.wait_ge(o_x.sem, o_x.at(j))
                pe_norm_mean(uu, resid[:])
                pe_norm_var(uu)
                post_mlp1(j)
                post_mlp2(j)

            pe.wait_ge(sel_made.sem, 1)
            pe.wait_ge(x_in.sem, x_in.at(G - 1))
            pe_norm_mean(LN0, xgroup(0))
            pe_norm_var(LN0)
            pre_in_x(0, 0)
            pre_in_z(0, 0)
            pre_xproj(0, 0)
            pre_dtproj(0, 0)
            scan_b(0, 0, 0)
            scan_c(0, 0, 0)
            scan_b(0, 0, 1)
            mamba_rounds(pe, pe_round, pe_post)
            pe.wait_ge(moe_in.sem, 64)
            pe.wait_ge(m_const.sem, 1)
            pe.wait_ge(h_mamba.sem, h_mamba.at(G - 1))

            def group_of(g):
                return h[:, g, :] if isinstance(g, int) else h[:, bass.ds(g, 1), :].squeeze(1)

            def pe_attention(g, s, u):
                if s == AT["mean"]:
                    pe_norm_mean(u, group_of(g))
                if s == AT["var"]:
                    pe_norm_var(u)
                if s == AT["qkv"]:
                    pe.wait_ge(m_xe.sem, m_xe.at(g))
                    nc.tensor.matmul(bank(QB), mat("Wq"), xe[:], start=True, stop=True).then_inc(m_qk.sem, 1)
                    nc.tensor.matmul(bank(QB + 1), mat("Wk"), xe[:], start=True, stop=True).then_inc(m_qk.sem, 1)
                    for b in range(GB):
                        mm = nc.tensor.matmul(ps[0:T, CTX, P * b:P * b + P], xe[:, T * b:T * b + T], mat("Wv"),
                                              start=True, stop=True)
                    mm.then_inc(m_qk.sem, 1)
                k = unit_at(s, "context")
                if k is not None:
                    b = k // 2
                    pe.wait_ge(m_pt_out.sem, m_pt_out.at(g, k + 1))
                    for i in range(UH):
                        lo = DH * (UH * (k % 2) + i)
                        mm = nc.tensor.matmul(ps[0:T, CTX, P * b + lo:P * b + lo + DH], mpT[:, k % 2, i, :],
                                              vh[:, b, lo:lo + DH], start=True, stop=True)
                    mm.then_inc(m_ctx.sem, 1)
                k = unit_at(s, "scores")
                if k is not None:
                    b = k // 2
                    if k == 0:
                        pe.wait_ge(m_qk_out.sem, m_qk_out.at(g))
                        pe.wait_ge(m_qm.sem, m_qm.at(g))
                    if k >= 2:
                        pe.wait_ge(m_pt_out.sem, m_pt_out.at(g, k - 1))
                    for i in range(UH):
                        mm = nc.tensor.matmul(ps[0:T, QB + k % 2, T * i:T * i + T],
                                              qm[:, UH * (k % 2) + i, T * b:T * b + T], kh[:, T * b:T * b + T],
                                              start=True, stop=True)
                    mm.then_inc(m_sc.sem, 1)
                k = unit_at(s, "probs")
                if k is not None:
                    pe.wait_ge(m_exp.sem, m_exp.at(g, k + 1))
                    for i in range(UH):
                        mm = nc.tensor.transpose(ps[0:T, QB + k % 2, T * i:T * i + T], mp_[:, k % 2, i, :],
                                                 ident[0:T, 0:T])
                    mm.then_inc(m_pt.sem, 1)
                if s == AT["ctx_t"]:
                    pe.wait_ge(m_ctx_n.sem, m_ctx_n.at(g))
                    for b in range(GB):
                        mm = nc.tensor.transpose(ps[:, QB, T * b:T * b + T], mctx[:, b, :], ident[0:T, 0:T])
                    mm.then_inc(m_ct.sem, 1)
                if s == AT["sa"]:
                    pe.wait_ge(m_ct_out.sem, m_ct_out.at(g))
                    nc.tensor.matmul(bank(QB + 1), mat("Wo"), ctxT[:], start=True, stop=True).then_inc(m_sa.sem, 1)
                if s == AT["post_mean"]:
                    pe.wait_ge(m_r1.sem, m_r1.at(g))
                    pe_norm_mean(u + 1, r1[:])
                if s == AT["post_var"]:
                    pe_norm_var(u + 1)
                if s == AT["logits"]:
                    pe.wait_ge(m_x1.sem, m_x1.at(g))
                    for b in range(GB):
                        mm = nc.tensor.matmul(ps[0:T, QB, EXPERTS * b:EXPERTS * b + EXPERTS], x1[:, T * b:T * b + T],
                                              wg[:], start=True, stop=True)
                    mm.then_inc(m_lg.sem, 1)
                if s == AT["onehot"]:
                    pe.wait_ge(m_top.sem, m_top.at(g))
                    for b in range(GB):
                        mm = nc.tensor.matmul(ps[0:EXPERTS, QB + 1, T * b:T * b + T], eq[:, b, :], ident[0:T, 0:T],
                                              start=True, stop=True)
                    mm.then_inc(m_oh.sem, 1)

            def expert_mask(g, e):
                if e == 0:
                    pe.wait_ge(m_oh_out.sem, m_oh_out.at(g))
                else:
                    pe.wait_ge(m_mask_out.sem, m_mask_out.at(g, e))
                nc.tensor.matmul(bank(MK), esel[:, e, :], ohb[:], start=True, stop=True).then_inc(m_mask.sem, 1)

            def pe_experts(g, s):
                e, half = (s % HALF) // 2, s % 2
                cs = range(half * HID // P // 2, (half + 1) * HID // P // 2)
                if s < HALF:
                    if half == 0:
                        pe.wait_ge(m_xm.sem, m_xm.at(g, e + 1))
                    for c in cs:
                        mm = nc.tensor.matmul(bank(HB + c), w1[:, e, P * c:P * c + P], xm[:, e % 2, :], start=False,
                                              stop=(e == EXPERTS - 1))
                        if e == EXPERTS - 1:
                            mm.then_inc(m_hid.sem, 1)
                    if half == 1 and e < EXPERTS - 1:
                        mm.then_inc(m_hid_e.sem, 1)
                        if e + 2 < EXPERTS:
                            expert_mask(g, e + 2)
                    if s == HALF - 1:
                        pe.wait_ge(m_mask_out.sem, m_mask_out.at(g))
                        nc.tensor.matmul(bank(MK), moe_b[:, HID:HID + P], ohT[:], start=True, stop=True)\
                            .then_inc(m_b2.sem, 1)
                else:
                    if half == 0 and e >= 2:
                        pe.wait_ge(m_yt.sem, m_yt.at(g, e - 1))
                    for c in cs:
                        if e == 0:
                            pe.wait_ge(m_gelu.sem, m_gelu.at(g, c + 1))
                        mm = nc.tensor.matmul(bank(HB + e % 2), w2[:, e, c, :], gh[:, c, :],
                                              start=(c == 0), stop=(c == HID // P - 1))
                    if half == 1:
                        mm.then_inc(m_y.sem, 1)

            def pe_end(ge, ga, u):
                for s in range(SLOTS):
                    if ge is not None:
                        pe_experts(ge, s)
                    if ga is not None:
                        pe_attention(ga, s, u)
                uf = u if ga is None else u + 2
                if ga is not None:
                    expert_mask(ga, 0)
                if ge is not None:
                    pe.wait_ge(m_acc.sem, m_acc.at(ge))
                    pe_norm_mean(uf, acc[:])
                if ga is not None:
                    for c in range(HID // P):
                        nc.tensor.matmul(bank(HB + c), moe_b[:, P * c:P * c + P], ohT[:], start=True, stop=False)
                    expert_mask(ga, 1)
                if ge is not None:
                    pe_norm_var(uf)

            tower_end(pe, pe_end)

        @block.scalar
        def _(act):
            act.wait_ge(consts.sem, 1)
            nc.scalar.preload_act_table_set("natural_log_exp_and_others")
            act.wait_ge(bn_step.sem, 1)
            nc.scalar.activation(bn_sc[:, 0:1], bn_mv[:, 1:2], ACT.Ln, bias=eps_c[:]).then_inc(bn_step.sem, 1)
            act.wait_ge(bn_step.sem, 2)
            nc.scalar.activation(bn_sc[:, 1:2], bn_sc[:, 0:1], ACT.Exp, scale=-0.5).then_inc(bn_step.sem, 1)

            act.wait_ge(param.sem, PARAM_ALL)
            def act_project(g):
                for i, (dst, b, k) in enumerate(((q_cr, "bq_cr", 1), (q_d, "bq_d", 2), (k_d, "bk_d", 4),
                                                 (k_c, "bk_c", 5))):
                    act.wait_ge(at_proj.sem, at_proj.at(g, k))
                    nc.scalar.activation(dst[:], bank4(k + 1), ACT.Identity, bias=col(b)).then_inc(at_q_act.sem, 1)
                act.wait_ge(at_q_act.sem, at_q_act.at(g))
                nc.scalar.activation(nq[:, 1, :], k_c[:].rearrange("p b t -> p (b t)"), ACT.Square)\
                    .then_inc(at_sq.sem, 1)
                act.wait_ge(at_qc.sem, at_qc.at(g))
                nc.scalar.activation(nq[:, 0, :], q_c[:].rearrange("p b t -> p (b t)"), ACT.Square)\
                    .then_inc(at_sq.sem, 1)
                for i in range(2):
                    act.wait_ge(at_v.sem, at_v.at(g, i + 1))
                    nc.scalar.copy(v_dc[:, 2 * i:2 * i + 2, :].rearrange("p b c -> p (b c)"), ps[0:T, (7, 0)[i], :])\
                        .then_inc(at_v_out.sem, 1)
                act.wait_ge(at_v.sem, at_v.at(g, 3))
                nc.scalar.copy(v_cr[:].rearrange("p b c -> p (b c)"), ps[0:TD, 5, :]).then_inc(at_v_out.sem, 1)

            def act_norms(g, steps):
                for step in steps:
                    for k, i in enumerate((1, 0)):
                        if step == 0:
                            act.wait_ge(at_ss.sem, at_ss.at(g, k + 1))
                        else:
                            act.wait_ge(at_nrm.sem, at_nrm.at(g, 2 * step - 1 + k))
                        src = bank((4, 3)[i]) if step == 0 else nq[:, i, :]
                        if step % 2 == 0:
                            a = nc.scalar.activation(nq[:, i, :], src, ACT.Ln, bias=norm_c[:, step // 2:step // 2 + 1])
                        else:
                            a = nc.scalar.activation(nq[:, i, :], src, ACT.Exp, scale=(0.5, -1.0)[step // 2])
                        a.then_inc(at_nrm.sem, 1)

            def act_exponents(g):
                for b in range(GB):
                    act.wait_ge(at_bias.sem, at_bias.at(g, b // 2 + 1))
                    for i, (lo, hi) in enumerate(BR):
                        a = nc.scalar.activation(prob[:, b, lo:hi], ps[0:T, b, lo:hi], ACT.Exp,
                                                 bias=nbias[:, b, i:i + 1], scale=(P ** -0.5, P ** -0.5, 1.0)[i],
                                                 accum_out=rsum[:, b, i:i + 1])
                    a.then_inc(at_exp.sem, 1)
                for b in range(GB):
                    act.wait_ge(at_pt.sem, at_pt.at(g, b + 1))
                    nc.scalar.copy(probT[0:TD, b, 0:T], ps[0:TD, b, 0:T])
                    nc.scalar.copy(probT[:, b, T:3 * T], ps[0:T, b, T:3 * T]).then_inc(at_pt_out.sem, 1)

            def act_branch_rstd(g):
                act.wait_ge(at_st.sem, at_st.at(g))
                nc.scalar.activation(ars[:], amv[:, :, 1], ACT.Ln, bias=eps_c[0:T, :]).then_inc(at_log.sem, 1)
                act.wait_ge(at_log.sem, at_log.at(g))
                nc.scalar.activation(ars[:], ars[:], ACT.Exp, scale=-0.5).then_inc(at_rstd.sem, 1)

            def act_gate_inputs(g, bs):
                for b in bs:
                    act.wait_ge(at_aot.sem, at_aot.at(g, b + 1))
                    if b >= 2:
                        act.wait_ge(at_logit.sem, at_logit.at(g, b - 1))
                    nc.scalar.copy(aoT[:, b % 2, :, :].rearrange("p i t -> p (i t)"), ps[:, (5, 7)[b % 2], 0:3 * T])\
                        .then_inc(at_aot_out.sem, 1)

            def act_gates(g):
                act.wait_ge(at_gate.sem, at_gate.at(g))
                nc.scalar.activation(glog[:], glog[:], ACT.Exp).then_inc(at_gexp.sem, 1)

            def act_attention_groups(ga, gb):
                if ga is not None:
                    ln_act(act, ga)
                if gb is not None:
                    act_branch_rstd(gb)
                if ga is not None:
                    act_project(ga)
                if gb is not None:
                    act_gate_inputs(gb, (0, 1))
                if ga is not None:
                    act_norms(ga, (0, 1))
                if gb is not None:
                    act_gate_inputs(gb, (2, 3))
                if ga is not None:
                    act_norms(ga, (2, 3))
                if gb is not None:
                    act_gates(gb)
                if ga is not None:
                    act_exponents(ga)

            attention_groups(act, act_attention_groups)

            with act.Fori(0, G) as g:
                ln_act(act, g + G)
            act.wait_ge(a_in.sem, 16)
            nc.scalar.activation(nega[:], nega[:], ACT.Exp).then_inc(a_neg.sem, 1)
            with act.Fori(0, G) as g:
                ln_act(act, g + 2 * G)

            def act_norm_square(uu):
                act.wait_ge(ln_cent.sem, ln_cent.at(uu))
                nc.scalar.activation(rstd[:], cent[:], ACT.Square).then_inc(ln_square.sem, 1)

            def act_norm_rstd(uu):
                act.wait_ge(ln_var.sem, ln_var.at(uu))
                nc.scalar.activation(rstd[:], bank(LNB), ACT.Ln, bias=eps_c[:]).then_inc(ln_log.sem, 1)
                act.wait_ge(ln_log.sem, ln_log.at(uu))
                nc.scalar.activation(rstd[:], rstd[:], ACT.Exp, scale=-0.5).then_inc(ln_rstd.sem, 1)

            def sigmoid(k, src, dst, ready, sig, j):
                if k == 0:
                    act.wait_ge(ready.sem, ready.at(j))
                    nc.scalar.activation(dst, src, ACT.Exp, scale=-1.0).then_inc(sig.sem, 1)
                elif k == 1:
                    act.wait_ge(sig.sem, sig.at(j, 1))
                    nc.scalar.activation(dst, dst, ACT.Ln, bias=1.0).then_inc(sig.sem, 1)
                else:
                    act.wait_ge(sig.sem, sig.at(j, 2))
                    nc.scalar.activation(dst, dst, ACT.Exp, scale=-1.0).then_inc(sig.sem, 1)

            def pre_drow(j, par):
                act.wait_ge(p_xp.sem, p_xp.at(j))
                for lo, hi in ((32, 64), (64, P)):
                    nc.scalar.copy(bc[lo:hi, par, :], ps[lo:hi, L0, 0:N])
                nc.scalar.activation(drow[0:32, :], ps[0:32, L0, 0:N], ACT.Identity,
                                     bias=selcol[0:32, -1:]).then_inc(p_drow.sem, 1)

            def pre_softplus(j, k):
                if k == 0:
                    act.wait_ge(p_clip.sem, p_clip.at(j, 1))
                    nc.scalar.activation(spx[:], spx[:], ACT.Exp).then_inc(p_sp.sem, 1)
                else:
                    act.wait_ge(p_sp.sem, p_sp.at(j, 1))
                    nc.scalar.activation(spx[:], spx[:], ACT.Ln, bias=1.0).then_inc(p_sp.sem, 1)

            def scan_cb(j, n):
                act.wait_ge(s_c.sem, s_c.at(j, n + 1))
                act.wait_ge(s_gq.sem, s_gq.at(j, n + 1 - DB))
                nc.scalar.copy(cb[:, n % DB, :], bank(CC)).then_inc(s_cb.sem, 1)

            def scan_da(j, par, n):
                if n == 0:
                    act.wait_ge(p_dt.sem, p_dt.at(j))
                act.wait_ge(s_h.sem, s_h.at(j, n + 1 - DB))
                for i in range(2):
                    at = (j // G) * (2 * STATES) + (STATES * i + n)
                    scale = nega[:].rearrange("p l s -> p (l s)")[:, bass.ds(at, 1)]
                    a = nc.scalar.activation(
                        dA[:, n % DB, i, :].rearrange("p (b t) -> p b t", b=GB)[:, :, 1:T],
                        dt[:, par, i, :].rearrange("p (b t) -> p b t", b=GB)[:, :, 1:T], ACT.Exp, scale=scale)
                a.then_inc(s_da.sem, 1)

            def post_gelu(j):
                act.wait_ge(o_m1.sem, o_m1.at(j))
                for i in range(2):
                    a = nc.scalar.activation(gl[:, i, :], bank(L0 + i), ACT.Gelu, bias=ow("b1", i, 1))
                a.then_inc(o_gl.sem, 1)
                nc.scalar.preload_act_table_set("natural_log_exp_and_others")

            def act_round(j, par, u_pre, u_post):
                for n in range(STATES):
                    scan_da(j, par, n)
                    scan_cb(j, n)
                    if u_pre is not None:
                        if n == SLOT["pre_square"]:
                            act_norm_square(u_pre)
                        if n == SLOT["pre_rstd"]:
                            act_norm_rstd(u_pre)
                        for k in range(3):
                            if n == SLOT["sig_x"][k]:
                                sigmoid(k, xc[:, 1 - par, :, :], sig_x[:], p_conv, p_sx, j + 1)
                            if n == SLOT["sig_z"][k]:
                                sigmoid(k, sz[:, 1 - par, :, :], sig_z[:], p_zc, p_sz, j + 1)
                        if n == SLOT["drow"]:
                            pre_drow(j + 1, 1 - par)
                        for k in range(2):
                            if n == SLOT["softplus"][k]:
                                pre_softplus(j + 1, k)
                    if u_post is not None:
                        if n == SLOT["post_square"]:
                            act_norm_square(u_post)
                        if n == SLOT["post_rstd"]:
                            act_norm_rstd(u_post)
                        if n == SLOT["gelu"]:
                            post_gelu(j - 1)

            def act_post(j, par, uu):
                act_norm_square(uu)
                act_norm_rstd(uu)
                post_gelu(j)

            act.wait_ge(a_neg.sem, 2)
            act.wait_ge(sel_in.sem, 16)
            act_norm_square(LN0)
            act_norm_rstd(LN0)
            for k in range(3):
                sigmoid(k, xc[:, 0, :, :], sig_x[:], p_conv, p_sx, 0)
            for k in range(3):
                sigmoid(k, sz[:, 0, :, :], sig_z[:], p_zc, p_sz, 0)
            pre_drow(0, 0)
            pre_softplus(0, 0)
            pre_softplus(0, 1)
            mamba_rounds(act, act_round, act_post)
            act.wait_ge(h_mamba.sem, h_mamba.at(G - 1))

            def act_attention(g, s, u):
                if s == AT["mean"]:
                    act_norm_square(u)
                if s == AT["var"]:
                    act_norm_rstd(u)
                if s == AT["qkv"]:
                    for i, (dst, bias) in enumerate(((qh, "bq"), (kh, "bk"))):
                        act.wait_ge(m_qk.sem, m_qk.at(g, i + 1))
                        nc.scalar.activation(dst[:], bank(QB + i), ACT.Identity, bias=col(bias))\
                            .then_inc(m_qk_out.sem, 1)
                    act.wait_ge(m_qk.sem, m_qk.at(g))
                    nc.scalar.copy(vh[:].rearrange("p b c -> p (b c)"), ps[0:T, CTX, :]).then_inc(m_qk_out.sem, 1)
                k = unit_at(s, "scores")
                if k is not None:
                    act.wait_ge(m_mx.sem, m_mx.at(g, 2 * k + 2))
                    for i in range(UH):
                        hd = UH * (k % 2) + i
                        a = nc.scalar.activation(mp_[:, k % 2, i, :], ps[0:T, QB + k % 2, T * i:T * i + T],
                                                 ACT.Exp, bias=mmax[:, k % 2, i:i + 1], scale=DH ** -0.5,
                                                 accum_out=msum[:, k // 2, hd:hd + 1])
                    a.then_inc(m_exp.sem, 1)
                if s == AT["ctx_t"]:
                    act.wait_ge(m_ct.sem, m_ct.at(g))
                    nc.scalar.activation(ctxT[:], bank(QB), ACT.Identity, bias=col("bv")).then_inc(m_ct_out.sem, 1)
                if s == AT["post_mean"]:
                    act_norm_square(u + 1)
                if s == AT["post_var"]:
                    act_norm_rstd(u + 1)
                if s == AT["onehot"]:
                    act.wait_ge(m_oh.sem, m_oh.at(g))
                    nc.scalar.copy(ohT[:], ps[0:EXPERTS, QB + 1, 0:N]).then_inc(m_oh_out.sem, 1)

            def mask_copy(g, e):
                act.wait_ge(m_mask.sem, m_mask.at(g, e + 1))
                nc.scalar.copy(mask[:, e, :], bank(MK)).then_inc(m_mask_out.sem, 1)

            def act_experts(g, s):
                if s % 2 and s < HALF - 4:
                    mask_copy(g, s // 2 + 2)
                if s == HALF - 1:
                    for c in range(HID // P):
                        act.wait_ge(m_hid.sem, m_hid.at(g, c + 1))
                        nc.scalar.activation(gh[:, c, :], bank(HB + c), ACT.Gelu).then_inc(m_gelu.sem, 1)
                    nc.scalar.preload_act_table_set("natural_log_exp_and_others")

            def act_end(ge, ga, u):
                for s in range(SLOTS):
                    if ge is not None:
                        act_experts(ge, s)
                    if ga is not None:
                        act_attention(ga, s, u)
                uf = u if ga is None else u + 2
                if ga is not None:
                    mask_copy(ga, 0)
                if ge is not None:
                    act_norm_square(uf)
                if ga is not None:
                    mask_copy(ga, 1)
                if ge is not None:
                    act_norm_rstd(uf)

            tower_end(act, act_end)

        @block.gpsimd
        def _(pool):
            pool.wait_ge(f_max.sem, G + 2)
            nc.gpsimd.partition_all_reduce(fall[:], fpair[:], P, bass.bass_isa.ReduceOp.max)\
                .then_inc(f_gmax.sem, 1)
            def pre_silz(j, par):
                pool.wait_ge(p_sz.sem, p_sz.at(j))
                nc.gpsimd.tensor_tensor(sz[:, par, :, :], sz[:, par, :, :], sig_z[:], ALU.mult).then_inc(p_silz.sem, 1)

            pre_silz(0, 0)

            def pool_round(j, par, u_pre, u_post):
                for n in range(STATES):
                    pool.wait_ge(s_h.sem, s_h.at(j, n + 1))
                    pool.wait_ge(s_cb.sem, s_cb.at(j, n + 1))
                    pool.wait_ge(s_sum.sem, s_sum.at(j, n + 1 - DB))
                    nc.gpsimd.tensor_tensor(gq[:, n % DB, :, :], hs[:, n % DB, :, :],
                                            cb[:, n % DB:n % DB + 1, :].to_broadcast([P, 2, N]), ALU.mult)\
                        .then_inc(s_gq.sem, 1)
                    if u_pre is not None and n == SLOT["silz"]:
                        pre_silz(j + 1, 1 - par)

            mamba_rounds(pool, pool_round, lambda j, par, uu: None)

        @block.vector
        def _(dve):
            nc.vector.memset(mean_w[:], 1.0 / P)
            nc.vector.memset(ones_w[:], 1.0)
            nc.vector.memset(norm_c[:, 0:1], 1e-36)
            nc.vector.memset(norm_c[:, 1:2], 1e-8)
            nc.vector.memset(xp[:], 0.0)
            nc.vector.memset(eps_c[:], EPS).then_inc(consts.sem, 1)
            dve.wait_ge(frames_in.sem, FRAMES_ALL)
            with dve.Fori(0, G) as g:
                dve.wait_ge(tok_mm.sem, tok_mm.at(g))
                nc.vector.tensor_scalar(h[:, g, :], ps[:, g, 0:N], col("tok_b"), 0.0, ALU.add, ALU.max)\
                    .then_inc(tok_y.sem, 1)
                dve.wait_ge(tok_y.sem, tok_y.at(g))
                nc.vector.bn_stats(bn[:, g, :], h[:, g, :]).then_inc(tok_stats.sem, 1)
            dve.wait_ge(tok_stats.sem, G)
            nc.vector.bn_aggr(bn_mv[:], bn[:].rearrange("p g s -> p (g s)")).then_inc(bn_step.sem, 1)
            dve.wait_ge(bn_step.sem, 3)
            nc.vector.tensor_tensor(bn_sc[:, 2:3], bn_sc[:, 1:2], col("tok_gamma"), ALU.mult).then_inc(bn_step.sem, 1)
            dve.wait_ge(bn_step.sem, 4)
            nc.vector.tensor_scalar(bn_sc[:, 3:4], bn_mv[:, 0:1], bn_sc[:, 2:3], None, ALU.mult)\
                .then_inc(bn_step.sem, 1)
            dve.wait_ge(bn_step.sem, 5)
            nc.vector.tensor_tensor(bn_sc[:, 0:1], col("tok_beta"), bn_sc[:, 3:4], ALU.subtract)\
                .then_inc(bn_step.sem, 1)
            dve.wait_ge(bn_step.sem, 6)
            with dve.Fori(0, G) as g:
                nc.vector.tensor_scalar(h[:, g, :], h[:, g, :], bn_sc[:, 2:3], bn_sc[:, 0:1], ALU.mult, ALU.add)\
                    .then_inc(h_tok.sem, 1)

            dve.wait_ge(param.sem, PARAM_ALL)
            nc.vector.tensor_scalar(rtemp[:], row("temp"), 0.01, None, ALU.max).then_inc(bn_step.sem, 1)
            dve.wait_ge(bn_step.sem, 7)
            nc.vector.reciprocal(rtemp[:], rtemp[:]).then_inc(bn_step.sem, 1)
            dve.wait_ge(bn_step.sem, 8)
            def dve_project(g, gb):
                dve.wait_ge(h_tok.sem, h_tok.at(g))
                dve.wait_ge(ln_mean.sem, ln_mean.at(g))
                nc.vector.tensor_tensor(cent[:], hgroup(g), bank(LNB), ALU.subtract).then_inc(ln_cent.sem, 1)
                if gb is not None:
                    dve_branch_stats(gb)
                dve.wait_ge(ln_rstd.sem, ln_rstd.at(g))
                nc.vector.tensor_tensor(xp[:, :, 1:T + 1], cent[:].rearrange("p (b t) -> p b t", b=GB),
                                        rstd[:].rearrange("p (b t) -> p b t", b=GB), ALU.mult)\
                    .then_inc(xn_ready.sem, 1)

            def dve_branch_stats(g):
                for b in range(GB):
                    for i in range(3):
                        a = nc.vector.bn_stats(ast[:, b, i, :], ao[:, b, i, :])
                a.then_inc(at_st.sem, 1)
                dve.wait_ge(at_st.sem, at_st.at(g, 1))
                st = ast[:].rearrange("p b i s -> p (b i) s")
                nc.vector.tensor_tensor(amv[:, :, 0], st[:, :, 1], st[:, :, 4], ALU.add)
                nc.vector.tensor_tensor(amv[:, :, 1], st[:, :, 2], st[:, :, 5], ALU.add)
                nc.vector.tensor_tensor(ad[:], st[:, :, 1], st[:, :, 4], ALU.subtract).then_inc(at_st.sem, 1)
                dve.wait_ge(at_st.sem, at_st.at(g, 2))
                nc.vector.tensor_scalar(amv[:, :, 0], amv[:, :, 0], 0.5, None, ALU.mult)
                nc.vector.scalar_tensor_tensor(ad[:], ad[:], 0.25, ad[:], ALU.mult, ALU.mult).then_inc(at_st.sem, 1)
                dve.wait_ge(at_st.sem, at_st.at(g, 3))
                nc.vector.scalar_tensor_tensor(amv[:, :, 1], amv[:, :, 1], 1.0 / P, ad[:], ALU.mult, ALU.add)\
                    .then_inc(at_st.sem, 1)

            def dve_conv_out(g):
                dve.wait_ge(at_conv.sem, at_conv.at(g))
                nc.vector.tensor_scalar(xd[:], ps[:, 1, 0:GB * TD].rearrange("p (b t) -> p b t", b=GB), col("db"),
                                        None, ALU.add).then_inc(at_xd.sem, 1)

            def dve_project_out(g):
                dve.wait_ge(at_proj.sem, at_proj.at(g, 3))
                nc.vector.tensor_scalar(q_c[:], bank4(4), col("bq_c"), None, ALU.add).then_inc(at_qc.sem, 1)
                dve.wait_ge(at_kcr.sem, at_kcr.at(g))
                nc.vector.tensor_scalar(k_cr[:], ps[:, 1, 0:GB * TD].rearrange("p (b t) -> p b t", b=GB),
                                        col("bk_cr"), None, ALU.add).then_inc(at_kcr_out.sem, 1)

            def dve_branch_norm(g):
                dve.wait_ge(at_rstd.sem, at_rstd.at(g))
                for b in range(GB):
                    for i in range(3):
                        k = 3 * b + i
                        a = nc.vector.tensor_scalar(ao[:, b, i, :], ao[:, b, i, :], amv[:, k, 0:1], ars[:, k:k + 1],
                                                    ALU.subtract, ALU.mult)
                a.then_inc(at_aff.sem, 1)
                ao3 = ao[:].rearrange("p b i c -> p b (i c)")
                dve.wait_ge(at_aff.sem, at_aff.at(g, 1))
                nc.vector.tensor_tensor(ao3, ao3, row("ln_g", T).unsqueeze(1).to_broadcast([T, GB, 3 * P]), ALU.mult)\
                    .then_inc(at_aff.sem, 1)
                dve.wait_ge(at_aff.sem, at_aff.at(g, 2))
                nc.vector.tensor_tensor(ao3, ao3, row("ln_b", T).unsqueeze(1).to_broadcast([T, GB, 3 * P]), ALU.add)\
                    .then_inc(at_aff.sem, 1)

            def dve_normalise_qk(g):
                dve.wait_ge(at_nrm.sem, at_nrm.at(g))
                nc.vector.scalar_tensor_tensor(q_c[:].rearrange("p b t -> p (b t)"),
                                               q_c[:].rearrange("p b t -> p (b t)"), rtemp[:], nq[:, 0, :],
                                               ALU.mult, ALU.mult).then_inc(at_qkn.sem, 1)
                nc.vector.tensor_tensor(k_c[:].rearrange("p b t -> p (b t)"), k_c[:].rearrange("p b t -> p (b t)"),
                                        nq[:, 1, :], ALU.mult).then_inc(at_qkn.sem, 1)

            def dve_maxima(g):
                for p in range(2):
                    b0, b1 = 2 * p, 2 * p + 2
                    dve.wait_ge(at_score.sem, at_score.at(g, b1))
                    nc.vector.tensor_reduce(nmax[:, b0:b1, 0:1].squeeze(2), ps[0:T, b0:b1, 0:TD], AX.X, ALU.max,
                                            negate=True).then_inc(at_max.sem, 1)
                    nc.vector.tensor_reduce(nmax[:, b0:b1, 1:3],
                                            ps[0:T, b0:b1, TD:SC].rearrange("p b (i s) -> p b i s", i=2),
                                            AX.X, ALU.max, negate=True).then_inc(at_max.sem, 1)
                    dve.wait_ge(at_max.sem, at_max.at(g, b1))
                    nc.vector.tensor_tensor(nbias[:, b0:b1, :], nmax[:, b0:b1, :],
                                            row("scales", T).unsqueeze(1).to_broadcast([T, 2, 3]), ALU.mult)\
                        .then_inc(at_bias.sem, 1)

            def dve_gates(g):
                dve.wait_ge(at_logit.sem, at_logit.at(g))
                nc.vector.tensor_tensor(glog[:], ps[0:T, GATE_B, 0:3 * GB].rearrange("p (b i) -> p b i", b=GB),
                                        row("gb", T).unsqueeze(1).to_broadcast([T, GB, 3]), ALU.add)\
                    .then_inc(at_gate.sem, 1)
                dve.wait_ge(at_gate.sem, at_gate.at(g, 1))
                nc.vector.tensor_reduce(gmx[:], glog[:], AX.X, ALU.max).then_inc(at_gate.sem, 1)
                dve.wait_ge(at_gate.sem, at_gate.at(g, 2))
                nc.vector.tensor_tensor(glog[:], glog[:], gmx[:].unsqueeze(2).to_broadcast([T, GB, 3]), ALU.subtract)\
                    .then_inc(at_gate.sem, 1)

            def dve_mix(g):
                dve.wait_ge(at_gexp.sem, at_gexp.at(g))
                nc.vector.tensor_reduce(gmx[:], glog[:], AX.X, ALU.add).then_inc(at_gn.sem, 1)
                dve.wait_ge(at_gn.sem, at_gn.at(g, 1))
                nc.vector.reciprocal(gmx[:], gmx[:]).then_inc(at_gn.sem, 1)
                dve.wait_ge(at_gn.sem, at_gn.at(g, 2))
                nc.vector.tensor_tensor(glog[:], glog[:], gmx[:].unsqueeze(2).to_broadcast([T, GB, 3]), ALU.mult)\
                    .then_inc(at_gn.sem, 1)
                dve.wait_ge(at_gn.sem, at_gn.at(g))
                for b in range(GB):
                    a = nc.vector.tensor_scalar(z[:, b, :], ao[:, b, 0, :], glog[:, b, 0:1], None, ALU.mult)
                a.then_inc(at_z.sem, 1)
                for i in range(1, 3):
                    dve.wait_ge(at_z.sem, at_z.at(g, i))
                    for b in range(GB):
                        a = nc.vector.scalar_tensor_tensor(z[:, b, :], ao[:, b, i, :], glog[:, b, i:i + 1], z[:, b, :],
                                                           ALU.mult, ALU.add)
                    a.then_inc(at_z.sem, 1)

            def dve_outputs(g):
                dve.wait_ge(at_exp.sem, at_exp.at(g))
                nc.vector.reciprocal(rinv[:], rsum[:]).then_inc(at_rinv.sem, 1)
                dve.wait_ge(at_rinv.sem, at_rinv.at(g))
                for b in range(GB):
                    dve.wait_ge(at_o.sem, at_o.at(g, b + 1))
                    for i in range(3):
                        a = nc.vector.scalar_tensor_tensor(ao[:, b, i, :], ps[0:T, b, P * i:P * i + P],
                                                           rinv[:, b, i:i + 1], row("bv", T)[:, P * i:P * i + P],
                                                           ALU.mult, ALU.add)
                a.then_inc(at_on.sem, 1)
                dve.wait_ge(at_on.sem, at_on.at(g))

            def dve_add_mix(g):
                dve.wait_ge(at_zt.sem, at_zt.at(g))
                nc.vector.tensor_tensor(hgroup(g), hgroup(g), bank(GATE_B), ALU.add).then_inc(h_attn.sem, 1)

            def dve_attention_groups(ga, gb):
                if ga is not None:
                    dve_project(ga, gb)
                    dve_conv_out(ga)
                elif gb is not None:
                    dve_branch_stats(gb)
                if gb is not None:
                    dve_branch_norm(gb)
                if ga is not None:
                    dve_project_out(ga)
                    dve_normalise_qk(ga)
                if gb is not None:
                    dve_gates(gb)
                if ga is not None:
                    dve_maxima(ga)
                if gb is not None:
                    dve_mix(gb)
                    dve.wait_ge(at_z.sem, at_z.at(gb))
                if ga is not None:
                    dve_outputs(ga)
                if gb is not None:
                    dve_add_mix(gb)

            attention_groups(dve, dve_attention_groups)

            dve.wait_ge(h_attn.sem, h_attn.at(G - 1))
            with dve.Fori(0, G) as g:
                ln_dve(dve, g + G, h[:, g, :])
                nc.vector.tensor_tensor(xs[:, g, :], cent[:], rstd[:], ALU.mult).then_inc(fx.sem, 1)
                dve.wait_ge(fx.sem, fx.at(g))
                nc.vector.tensor_reduce(famax[:, bass.ds(g, 1)], xs[:, g, :], AX.X, ALU.max, apply_absolute_value=True)\
                    .then_inc(f_max.sem, 1)
            dve.wait_ge(f_max.sem, G)
            nc.vector.tensor_reduce(fpair[:, 0:1], famax[:, 0:G], AX.X, ALU.max).then_inc(f_max.sem, 1)
            nc.vector.tensor_reduce(fpair[:, 1:2], mat("ffn"), AX.X, ALU.max, apply_absolute_value=True)\
                .then_inc(f_max.sem, 1)
            dve.wait_ge(f_gmax.sem, 1)
            nc.vector.tensor_scalar(fall[:], fall[:], 1e-12, None, ALU.max).then_inc(f_step.sem, 1)
            dve.wait_ge(f_step.sem, 1)
            nc.vector.reciprocal(fpair[:], fall[:]).then_inc(f_step.sem, 1)
            dve.wait_ge(f_step.sem, 2)
            nc.vector.tensor_scalar(fsc[:, 0:2], fpair[:], FP8_MAX, None, ALU.mult).then_inc(f_step.sem, 1)
            dve.wait_ge(f_step.sem, 3)
            nc.vector.reciprocal(fpair[:], fsc[:, 0:2]).then_inc(f_step.sem, 1)
            dve.wait_ge(f_step.sem, 4)
            nc.vector.tensor_tensor(fsc[:, 2:3], fpair[:, 0:1], fpair[:, 1:2], ALU.mult).then_inc(f_step.sem, 1)
            dve.wait_ge(f_step.sem, 5)

            def quantise(dst, src, scale, a, m, sig, r):
                nc.vector.tensor_scalar(a, src, scale, FP8_MAX, ALU.mult, ALU.min).then_inc(sig.sem, 1)
                dve.wait_ge(sig.sem, sig.at(r, 1))
                nc.vector.tensor_scalar(a, a, -FP8_MAX, None, ALU.max).then_inc(sig.sem, 1)
                dve.wait_ge(sig.sem, sig.at(r, 2))
                nc.vector.tensor_scalar(m.bitcast(U32), a.bitcast(U32), 0x7F800000, None, ALU.bitwise_and)\
                    .then_inc(sig.sem, 1)
                dve.wait_ge(sig.sem, sig.at(r, 3))
                nc.vector.tensor_scalar(m, m, 2.0 ** -6, 1.5 * 2.0 ** 20, ALU.max, ALU.mult).then_inc(sig.sem, 1)
                dve.wait_ge(sig.sem, sig.at(r, 4))
                nc.vector.tensor_tensor(a, a, m, ALU.add).then_inc(sig.sem, 1)
                dve.wait_ge(sig.sem, sig.at(r, 5))
                nc.vector.tensor_tensor(dst, a, m, ALU.subtract).then_inc(sig.sem, 1)

            quantise(wq8[:], mat("ffn"), fsc[:, 1:2], wtmp[:, 0, :], wtmp[:, 1, :], f_wstep, 0)
            dve.wait_ge(f_wstep.sem, f_wstep.at(0))
            nc.vector.memset(wtmp[:, 2, :], 0.0).then_inc(f_wq.sem, 1)

            def dequantise(g):
                dve.wait_ge(f_mm.sem, f_mm.at(g))
                nc.vector.scalar_tensor_tensor(h[:, g, :], ps[:, g, 0:N], fsc[:, 2:3], h[:, g, :],
                                               ALU.mult, ALU.add).then_inc(h_ffn.sem, 1)

            with dve.Fori(0, G) as g:
                quantise(xq8[:], xs[:, g, :], fsc[:, 0:1], ftmp[:, 0, :], ftmp[:, 1, :], f_q, g)
                dequantise(g)
            dve.wait_ge(sel_in.sem, 16)
            nc.vector.memset(dA[:], 0.0)
            nc.vector.memset(drow[:], 0.0)
            nc.vector.memset(bc[:], 0.0)
            nc.vector.tensor_copy(sel[:], selcol[:, 0:2 * STATES].unsqueeze(2).to_broadcast([P, 2 * STATES, P]))\
                .then_inc(sel_made.sem, 1)
            dve.wait_ge(a_neg.sem, 1)
            nc.vector.tensor_scalar(nega[:], nega[:], -1.0, None, ALU.mult).then_inc(a_neg.sem, 1)
            with dve.Fori(0, G) as g:
                ln_dve(dve, g + 2 * G, h[:, g, :])
                nc.vector.tensor_tensor(xs[:, g, :], cent[:], rstd[:], ALU.mult).then_inc(x_in.sem, 1)
                dve.wait_ge(x_in.sem, x_in.at(g))

            def xgroup(j):
                return xs[:, j % G, :] if isinstance(j, int) else xs[:, bass.ds(j % G, 1), :].squeeze(1)

            def dve_norm_center(uu, src):
                dve.wait_ge(ln_mean.sem, ln_mean.at(uu))
                nc.vector.tensor_tensor(cent[:], src, bank(LNB), ALU.subtract).then_inc(ln_cent.sem, 1)

            def dve_norm_out(uu, dst, gamma, beta, sig, j, w_in):
                dve.wait_ge(w_in.sem, w_in.at(j // G))
                dve.wait_ge(ln_rstd.sem, ln_rstd.at(uu))
                nc.vector.scalar_tensor_tensor(cent[:], cent[:], gamma, rstd[:], ALU.mult, ALU.mult)\
                    .then_inc(sig.sem, 1)
                dve.wait_ge(sig.sem, sig.at(j, 1))
                nc.vector.tensor_scalar(dst, cent[:], beta, None, ALU.add).then_inc(sig.sem, 1)
                dve.wait_ge(sig.sem, sig.at(j))

            def pre_conv(j, par, s):
                if s == 0:
                    dve.wait_ge(p_xin.sem, p_xin.at(j))
                    for i in range(2):
                        a = nc.vector.tensor_scalar(xc[:, par, i, :], bank(L0 + i), pw("conv_w", 4 * i + 3, 1),
                                                    pw("conv_b", i, 1), ALU.mult, ALU.add)
                else:
                    dve.wait_ge(p_conv.sem, p_conv.at(j, s))
                    for i in range(2):
                        dst = xc[:, par, i, :].rearrange("p (b t) -> p b t", b=GB)[:, :, s:T]
                        a = nc.vector.scalar_tensor_tensor(dst, bank4(L0 + i)[:, :, 0:T - s],
                                                           pw("conv_w", 4 * i + 3 - s, 1), dst, ALU.mult, ALU.add)
                a.then_inc(p_conv.sem, 1)

            def pre_floor(j, par):
                dve.wait_ge(p_conv.sem, p_conv.at(j, 4))
                nc.vector.tensor_scalar(xc[:, par, :, :], xc[:, par, :, :], -40.0, None, ALU.max)\
                    .then_inc(p_conv.sem, 1)

            def pre_xc(j, par):
                dve.wait_ge(p_sx.sem, p_sx.at(j))
                nc.vector.tensor_tensor(xc[:, par, :, :], xc[:, par, :, :], sig_x[:], ALU.mult).then_inc(p_xc.sem, 1)

            def pre_zclip(j, par):
                dve.wait_ge(p_z.sem, p_z.at(j))
                nc.vector.tensor_scalar(sz[:, par, :, :], ps[:, L0:L0 + 2, 0:N], -40.0, None, ALU.max)\
                    .then_inc(p_zc.sem, 1)

            def pre_split(j, par):
                dve.wait_ge(p_drow.sem, p_drow.at(j))
                nc.vector.tensor_tensor(spx[64:P, 0, :], ps[64:P, L0, 0:N], bc[64:P, par, :], ALU.subtract)\
                    .then_inc(p_bc.sem, 1)
                dve.wait_ge(p_bc.sem, p_bc.at(j, 1))
                nc.vector.tensor_copy(bc[64:P, par, :], spx[64:P, 0, :]).then_inc(p_bc.sem, 1)
                dve.wait_ge(p_bc.sem, p_bc.at(j, 2))
                nc.vector.tensor_tensor(bc[96:P, par, :], spx[96:P, 0, :], bc[96:P, par, :], ALU.subtract)\
                    .then_inc(p_bc.sem, 1)

            def pre_clip(j, par):
                dve.wait_ge(p_dtm.sem, p_dtm.at(j))
                nc.vector.tensor_scalar(spx[:], ps[:, L0:L0 + 2, 0:N], 20.0, None, ALU.min).then_inc(p_clip.sem, 1)
                nc.vector.tensor_scalar(dt[:, par, :, :], ps[:, L0:L0 + 2, 0:N], -20.0, 0.0, ALU.add, ALU.max)\
                    .then_inc(p_clip.sem, 1)

            def pre_dt(j, par):
                dve.wait_ge(p_clip.sem, p_clip.at(j))
                dve.wait_ge(p_sp.sem, p_sp.at(j))
                nc.vector.tensor_tensor(dt[:, par, :, :], dt[:, par, :, :], spx[:], ALU.add).then_inc(p_dt.sem, 1)

            def pre_u(j, par):
                dve.wait_ge(p_dt.sem, p_dt.at(j))
                nc.vector.tensor_tensor(u[:, par, :, :], dt[:, par, :, :], xc[:, par, :, :], ALU.mult)\
                    .then_inc(p_u.sem, 1)

            def scan_db(j, par, n):
                if n == 0:
                    dve.wait_ge(p_u.sem, p_u.at(j))
                dve.wait_ge(s_h.sem, s_h.at(j, n - 1))
                dve.wait_ge(s_b.sem, s_b.at(j, n + 1))
                nc.vector.tensor_tensor(db[:, n % 2, :, :], u[:, par, :, :],
                                        ps[:, BB + n % 2:BB + n % 2 + 1, 0:N].to_broadcast([P, 2, N]), ALU.mult)\
                    .then_inc(s_db.sem, 1)

            def scan_h(j, n):
                dve.wait_ge(s_db.sem, s_db.at(j, n + 1))
                dve.wait_ge(s_da.sem, s_da.at(j, n + 1))
                dve.wait_ge(s_gq.sem, s_gq.at(j, n + 1 - DB))
                nc.vector.tensor_tensor_scan(hs[:, n % DB, :, :].rearrange("p i t -> p (i t)"),
                                             dA[:, n % DB, :, :].rearrange("p i t -> p (i t)"),
                                             db[:, n % 2, :, :].rearrange("p i t -> p (i t)"),
                                             0.0, ALU.mult, ALU.add).then_inc(s_h.sem, 1)

            def post_y(j, par):
                dve.wait_ge(wo_in.sem, wo_in.at(j // G))
                dve.wait_ge(s_sum.sem, s_sum.at(j))
                for i in range(2):
                    a = nc.vector.scalar_tensor_tensor(yv[:, i, :], xc[:, par, i, :], ow("D_skip", i, 1),
                                                       bank(Y + i), ALU.mult, ALU.add)
                a.then_inc(o_y.sem, 1)
                dve.wait_ge(o_y.sem, o_y.at(j))
                dve.wait_ge(p_silz.sem, p_silz.at(j))
                nc.vector.tensor_tensor(yv[:], yv[:], sz[:, par, :, :], ALU.mult).then_inc(o_yg.sem, 1)

            def post_x(j):
                dve.wait_ge(o_out.sem, o_out.at(j))
                nc.vector.tensor_tensor(resid[:], xgroup(j), bank(LP), ALU.add).then_inc(o_x.sem, 1)

            def post_x2(j):
                dve.wait_ge(o_m2.sem, o_m2.at(j))
                nc.vector.scalar_tensor_tensor(xgroup(j), bank(LP), ow("b2"), resid[:], ALU.add, ALU.add)\
                    .then_inc(o_x2.sem, 1)

            def dve_round(j, par, u_pre, u_post):
                for n in range(STATES):
                    if n == 0:
                        scan_db(j, par, 0)
                    if n + 1 < STATES:
                        scan_db(j, par, n + 1)
                    scan_h(j, n)
                    if u_post is not None and n == SLOT["y"]:
                        post_y(j - 1, 1 - par)
                    if u_pre is not None:
                        if n == SLOT["pre_cent"]:
                            dve_norm_center(u_pre, xgroup(j + 1))
                        if n == SLOT["pre_xn"]:
                            dve_norm_out(u_pre, xn[:], pw("ln1_g"), pw("ln1_b"), p_xn, j + 1, wp_in)
                        for s in range(4):
                            if n == SLOT["conv"][s]:
                                pre_conv(j + 1, 1 - par, s)
                        if n == SLOT["floor"]:
                            pre_floor(j + 1, 1 - par)
                        if n == SLOT["zclip"]:
                            pre_zclip(j + 1, 1 - par)
                        if n == SLOT["xc"]:
                            pre_xc(j + 1, 1 - par)
                        if n == SLOT["split"]:
                            pre_split(j + 1, 1 - par)
                        if n == SLOT["clip"]:
                            pre_clip(j + 1, 1 - par)
                        if n == SLOT["dt"]:
                            pre_dt(j + 1, 1 - par)
                        if n == SLOT["u"]:
                            pre_u(j + 1, 1 - par)
                    if u_post is not None:
                        if n == SLOT["x"]:
                            post_x(j - 1)
                        if n == SLOT["post_cent"]:
                            dve_norm_center(u_post, resid[:])
                        if n == SLOT["post_xn"]:
                            dve_norm_out(u_post, xn2[:], ow("ln2_g"), ow("ln2_b"), o_xn, j - 1, wo_in)
                        if n == SLOT["x2"]:
                            post_x2(j - 1)

            def dve_post(j, par, uu):
                post_y(j, par)
                post_x(j)
                dve_norm_center(uu, resid[:])
                dve_norm_out(uu, xn2[:], ow("ln2_g"), ow("ln2_b"), o_xn, j, wo_in)
                post_x2(j)

            dve_norm_center(LN0, xgroup(0))
            dve_norm_out(LN0, xn[:], pw("ln1_g"), pw("ln1_b"), p_xn, 0, wp_in)
            for s in range(4):
                pre_conv(0, 0, s)
            pre_floor(0, 0)
            pre_zclip(0, 0)
            pre_xc(0, 0)
            pre_split(0, 0)
            pre_clip(0, 0)
            pre_dt(0, 0)
            pre_u(0, 0)
            mamba_rounds(dve, dve_round, dve_post)
            dve.wait_ge(o_x2.sem, o_x2.at(ROUNDS - 1))
            with dve.Fori(0, G) as g:
                nc.vector.tensor_tensor(h[:, g, :], h[:, g, :], xs[:, g, :], ALU.add).then_inc(h_mamba.sem, 1)
            dve.wait_ge(h_mamba.sem, h_mamba.at(G - 1))
            nc.vector.memset(ohb[:], 0.0)
            nc.vector.tensor_copy(esel[:], selcol[:, 2 * STATES + HEADS:2 * STATES + HEADS + EXPERTS].unsqueeze(2)
                                  .to_broadcast([P, EXPERTS, P])).then_inc(m_const.sem, 1)
            dve.wait_ge(m_const.sem, 1)

            def group_of(g):
                return h[:, g, :] if isinstance(g, int) else h[:, bass.ds(g, 1), :].squeeze(1)

            def dve_attention(g, s, u):
                if s == AT["mean"]:
                    dve_norm_center(u, group_of(g))
                if s == AT["var"]:
                    dve.wait_ge(ln_rstd.sem, ln_rstd.at(u))
                    nc.vector.tensor_tensor(xe[:], cent[:], rstd[:], ALU.mult).then_inc(m_xe.sem, 1)
                if s == AT["qkv"]:
                    dve.wait_ge(m_qk_out.sem, m_qk_out.at(g, 1))
                    for hd in range(HEADS):
                        a = nc.vector.tensor_scalar(qm[:, hd, :], qh[:],
                                                    selcol[:, 2 * STATES + hd:2 * STATES + hd + 1], None, ALU.mult)
                    a.then_inc(m_qm.sem, 1)
                k = unit_at(s, "scores")
                if k is not None:
                    dve.wait_ge(m_sc.sem, m_sc.at(g, k + 1))
                    nc.vector.tensor_reduce(mmax[:, k % 2, :], ps[0:T, QB + k % 2, 0:N].rearrange("p (i s) -> p i s", i=UH),
                                            AX.X, ALU.max, negate=True).then_inc(m_mx.sem, 1)
                    dve.wait_ge(m_mx.sem, m_mx.at(g, 2 * k + 1))
                    nc.vector.tensor_scalar(mmax[:, k % 2, :], mmax[:, k % 2, :], DH ** -0.5, None, ALU.mult)\
                        .then_inc(m_mx.sem, 1)
                k = unit_at(s, "probs")
                if k is not None:
                    dve.wait_ge(m_pt.sem, m_pt.at(g, k + 1))
                    nc.vector.tensor_copy(mpT[:, k % 2, :, :].rearrange("p i t -> p (i t)"), ps[0:T, QB + k % 2, 0:N])\
                        .then_inc(m_pt_out.sem, 1)
                if unit_at(s, "context") == UNITS - 1:
                    dve.wait_ge(m_exp.sem, m_exp.at(g))
                    nc.vector.reciprocal(msum[:], msum[:]).then_inc(m_ri.sem, 1)
                    dve.wait_ge(m_ctx.sem, m_ctx.at(g))
                    dve.wait_ge(m_ri.sem, m_ri.at(g))
                    nc.vector.tensor_tensor(mctx[:].rearrange("p b (h d) -> p (b h) d", h=HEADS),
                                            ps[0:T, CTX, 0:GB * P].rearrange("p (q d) -> p q d", d=DH),
                                            msum[:].rearrange("p b h -> p (b h)").unsqueeze(2)
                                            .to_broadcast([T, GB * HEADS, DH]), ALU.mult).then_inc(m_ctx_n.sem, 1)
                if s == AT["sa"]:
                    dve.wait_ge(m_sa.sem, m_sa.at(g))
                    nc.vector.scalar_tensor_tensor(r1[:], bank(QB + 1), col("bo"), xe[:], ALU.add, ALU.add)\
                        .then_inc(m_r1.sem, 1)
                if s == AT["post_mean"]:
                    dve_norm_center(u + 1, r1[:])
                if s == AT["post_var"]:
                    dve.wait_ge(ln_rstd.sem, ln_rstd.at(u + 1))
                    nc.vector.scalar_tensor_tensor(cent[:], cent[:], col("g1"), rstd[:], ALU.mult, ALU.mult)\
                        .then_inc(m_x1.sem, 1)
                    dve.wait_ge(m_x1.sem, m_x1.at(g, 1))
                    nc.vector.tensor_scalar(x1[:], cent[:], col("beta1"), None, ALU.add).then_inc(m_x1.sem, 1)
                if s == AT["logits"]:
                    dve.wait_ge(m_lg.sem, m_lg.at(g))
                    nc.vector.tensor_tensor(lg[:], ps[0:T, QB, 0:GB * EXPERTS].rearrange("p (b e) -> p b e", b=GB),
                                            row("bg", T).unsqueeze(1).to_broadcast([T, GB, EXPERTS]), ALU.add)\
                        .then_inc(m_top.sem, 1)
                    dve.wait_ge(m_top.sem, m_top.at(g, 1))
                    nc.vector.tensor_reduce(lmx[:], lg[:], AX.X, ALU.max).then_inc(m_top.sem, 1)
                    dve.wait_ge(m_top.sem, m_top.at(g, 2))
                    nc.vector.tensor_tensor(eq[:], lg[:], lmx[:].unsqueeze(2).to_broadcast([T, GB, EXPERTS]),
                                            ALU.is_equal).then_inc(m_top.sem, 1)
                    dve.wait_ge(m_top.sem, m_top.at(g, 3))
                    nc.vector.tensor_tensor(lg[:], eq[:], row("places", T).unsqueeze(1)
                                            .to_broadcast([T, GB, EXPERTS]), ALU.mult).then_inc(m_top.sem, 1)
                    dve.wait_ge(m_top.sem, m_top.at(g, 4))
                    nc.vector.tensor_reduce(lmx[:], lg[:], AX.X, ALU.max).then_inc(m_top.sem, 1)
                    dve.wait_ge(m_top.sem, m_top.at(g, 5))
                    nc.vector.tensor_tensor(eq[:], lg[:], lmx[:].unsqueeze(2).to_broadcast([T, GB, EXPERTS]),
                                            ALU.is_equal).then_inc(m_top.sem, 1)
                if s == AT["onehot"]:
                    dve.wait_ge(m_oh_out.sem, m_oh_out.at(g, 1))
                    nc.vector.tensor_copy(ohb[0:EXPERTS, :], ohT[:]).then_inc(m_oh_out.sem, 1)

            def expert_input(g, e):
                dve.wait_ge(m_mask_out.sem, m_mask_out.at(g, e + 1))
                if e >= 2:
                    dve.wait_ge(m_hid_e.sem, m_hid_e.at(g, e - 1))
                nc.vector.tensor_tensor(xm[:, e % 2, :], x1[:], mask[:, e, :], ALU.mult).then_inc(m_xm.sem, 1)

            def dve_experts(g, s):
                if s % 2 and s < HALF - 4:
                    expert_input(g, s // 2 + 2)
                if s == HALF:
                    dve.wait_ge(m_b2.sem, m_b2.at(g))
                    nc.vector.tensor_tensor(acc[:], x1[:], bank(MK), ALU.add).then_inc(m_acc.sem, 1)
                if s > HALF and s % 2:
                    e = (s - HALF) // 2
                    dve.wait_ge(m_y.sem, m_y.at(g, e + 1))
                    nc.vector.tensor_tensor(yt[:, e % 2, :], mask[:, e, :], bank(HB + e % 2), ALU.mult)\
                        .then_inc(m_yt.sem, 1)
                    dve.wait_ge(m_yt.sem, m_yt.at(g, e + 1))
                    dve.wait_ge(m_acc.sem, m_acc.at(g, e + 1))
                    nc.vector.tensor_tensor(acc[:], acc[:], yt[:, e % 2, :], ALU.add).then_inc(m_acc.sem, 1)

            def dve_end(ge, ga, u):
                for s in range(SLOTS):
                    if ge is not None:
                        dve_experts(ge, s)
                    if ga is not None:
                        dve_attention(ga, s, u)
                uf = u if ga is None else u + 2
                if ge is not None:
                    dve_norm_center(uf, acc[:])
                if ga is not None:
                    expert_input(ga, 0)
                    expert_input(ga, 1)
                if ge is not None:
                    dve.wait_ge(ln_rstd.sem, ln_rstd.at(uf))
                    nc.vector.scalar_tensor_tensor(cent[:], cent[:], col("g2"), rstd[:], ALU.mult, ALU.mult)\
                        .then_inc(m_g2.sem, 1)
                    dve.wait_ge(m_g2.sem, m_g2.at(ge))
                    nc.vector.scalar_tensor_tensor(group_of(ge), cent[:], col("beta2"), group_of(ge),
                                                   ALU.add, ALU.add).then_inc(h_out.sem, 1)
                    dve.wait_ge(h_out.sem, h_out.at(ge))

            tower_end(dve, dve_end)


ORDER = ["x_t", "tok_w", "cols", "mats", "rows", "layers", "w1", "w2", "moe_rows", "wg", "ident", "selcol"]


def kernel(**inputs):
    import numpy as np
    import concourse.bacc as bacc
    from concourse.bass_utils import run_bass_kernel_spmd

    i = {k: np.asarray(v) for k, v in inputs.items()}
    a0, l1, f1 = (lambda n: i["L0_attn_" + n]), (lambda n: i["L1_attn_" + n]), (lambda n: i["L1_ffn_" + n])

    cols = {"tok_b": i["L0_tok_b"], "tok_gamma": i["L0_tok_gamma"], "tok_beta": i["L0_tok_beta"]}
    for n in ("db", "bq_cr", "bk_cr", "bq_d", "bk_d", "bq_c", "bk_c"):
        cols[n] = a0(n)
    for n in ("bq", "bk", "bv", "bo", "g1", "beta1", "g2", "beta2"):
        cols[n] = f1(n)
    gate = a0("gw").reshape(3, 3, P).transpose(1, 0, 2).reshape(9, P)
    for k in range(9):
        cols[f"gw{k}"] = gate[k]
    mats = {f"dw{k}": a0("dw")[:, :, k].T for k in range(3)}
    for n in ("wq_cr", "wk_cr", "wv_cr", "wq_d", "wk_d", "wv_d", "wq_c", "wk_c", "wv_c"):
        mats[n] = a0(n).T
    mats["ffn"] = i["L0_ffn_weight"]
    for n in ("Wq", "Wk", "Wv", "Wo"):
        mats[n] = f1(n)
    f32 = np.float32
    rows = {"bv": np.concatenate([a0("bv_" + n) for n in ("cr", "d", "c")]),
            "ln_g": np.concatenate([a0(f"ln_{n}_g") for n in ("cr", "d", "c")]),
            "ln_b": np.concatenate([a0(f"ln_{n}_b") for n in ("cr", "d", "c")]),
            "gb": a0("gb"), "temp": a0("temp").reshape(1), "bg": f1("bg"),
            "places": np.arange(EXPERTS, 0, -1).astype(f32),
            "scales": np.array([P ** -0.5, P ** -0.5, 1.0], f32)}
    xw = l1("xproj_w").transpose(0, 2, 1).reshape(LAYERS, 2, P, RANK + 2 * STATES)
    xproj = np.zeros((LAYERS, 2, P, P), f32)
    xproj[..., 0:RANK] = xw[..., 0:RANK]
    for q in range(1, 4):
        xproj[..., 32 * q:32 * q + 32] = xw[..., RANK:]
    dtproj = np.zeros((LAYERS, P, 2 * P), f32)
    dtproj[:, 0:RANK] = l1("dtproj_w").transpose(0, 2, 1)
    dtproj[:, RANK] = l1("dtproj_b")

    def halves(w):
        return w.reshape(LAYERS, 2, P, -1).transpose(0, 2, 1, 3).reshape(LAYERS, P, -1)

    lw = {"ln1_g": l1("ln1_g")[:, :, None], "ln1_b": l1("ln1_b")[:, :, None], "in_w": l1("in_w").transpose(0, 2, 1),
          "conv_w": halves(l1("conv_w")), "conv_b": halves(l1("conv_b")), "xproj": halves(xproj.reshape(LAYERS, 2 * P, P)),
          "dtproj": dtproj, "A_log": halves(l1("A_log")), "D_skip": halves(l1("D_skip")),
          "out_w": halves(l1("out_w").transpose(0, 2, 1)), "ln2_g": l1("ln2_g")[:, :, None],
          "ln2_b": l1("ln2_b")[:, :, None], "w1": l1("mlp_w1").transpose(0, 2, 1), "b1": halves(l1("mlp_b1")),
          "w2": halves(l1("mlp_w2").transpose(0, 2, 1)), "b2": l1("mlp_b2")[:, :, None]}
    layers = np.concatenate([lw[n] for n in LW], axis=2)
    selcol = np.zeros((P, 2 * STATES + HEADS + EXPERTS + 1), f32)
    for n in range(2 * STATES):
        selcol[[32 + n, 64 + n, 96 + n], n] = 1.0
    for n in range(HEADS):
        selcol[DH * n:DH * n + DH, 2 * STATES + n] = 1.0
    for n in range(EXPERTS):
        selcol[n, 2 * STATES + HEADS + n] = 1.0
    selcol[RANK, -1] = 1.0
    arrays = {
        "x_t": i["x"].transpose(2, 0, 1), "tok_w": i["L0_tok_W"].T,
        "cols": np.stack([cols[n] for n in COLS], axis=1), "mats": np.stack([mats[n] for n in MATS], axis=1),
        "rows": np.concatenate([rows[n] for n, _ in ROWS]), "layers": layers,
        "w1": f1("W1").transpose(1, 0, 2), "w2": f1("W2").reshape(EXPERTS, HID // P, P, P).transpose(2, 0, 1, 3),
        "moe_rows": np.concatenate([f1("b1"), f1("b2")], axis=1), "wg": f1("Wg"),
        "ident": np.eye(P, dtype=f32), "selcol": selcol,
    }
    arrays = {k + "_dram": np.ascontiguousarray(v) for k, v in arrays.items()}
    nc = bacc.Bacc("TRN2", target_bir_lowering=False, num_devices=1)
    aps = {k[:-5]: nc.dram_tensor(k, v.shape, mybir.dt.float32, kind="ExternalInput").ap() for k, v in arrays.items()}
    out = nc.dram_tensor("out_dram", (P, G, N), mybir.dt.float32, kind="ExternalOutput").ap()
    audio_tower(nc, *[aps[n] for n in ORDER], out)
    r = run_bass_kernel_spmd(nc, [arrays], core_ids=[0])
    return np.ascontiguousarray(r.results[0]["out_dram"].reshape(P, B, T).transpose(1, 2, 0))
```

```python
from contextlib import ExitStack

import concourse.bass as bass
from concourse import mybir

F32 = mybir.dt.float32
BF16 = mybir.dt.bfloat16
U32 = mybir.dt.uint32
ALU = mybir.AluOpType
ACT = mybir.ActivationFunctionType
AX = mybir.AxisListType

P = 128
B, T_IN, D_IN = 32, 125, 23
CONTEXT = 5
T = T_IN - CONTEXT + 1
GB = 4
G = B // GB
N = GB * T
BANK = 512
TD = (T + 2 - 3) // 2 + 1
FK = CONTEXT * D_IN
EPS = 1e-5
LAYERS = 5
STATES = 16
RANK = 8
HEADS, DH = 8, 16
EXPERTS, HID = 8, 512
FP8_MAX = 448.0

COLS = ["tok_b", "tok_gamma", "tok_beta", "db", "bq_cr", "bk_cr", "bq_d", "bk_d", "bq_c", "bk_c",
        "bq", "bk", "bv", "bo", "g1", "beta1", "g2", "beta2"] + [f"gw{k}" for k in range(9)]
COL = {n: i for i, n in enumerate(COLS)}
MATS = ["dw0", "dw1", "dw2", "wq_cr", "wk_cr", "wv_cr", "wq_d", "wk_d", "wq_c", "wk_c", "wv_d", "wv_c", "ffn",
        "Wq", "Wk", "Wv", "Wo"]
MAT = {n: i for i, n in enumerate(MATS)}
ROWS = [("bv", 384), ("ln_g", 384), ("ln_b", 384), ("gb", 3), ("temp", 1), ("bg", EXPERTS),
        ("places", EXPERTS), ("scales", 3)]
ROW = {}
for _n, _k in ROWS:
    ROW[_n] = (sum(v[1] - v[0] for v in ROW.values()), sum(v[1] - v[0] for v in ROW.values()) + _k)
ROW_ALL = sum(k for _, k in ROWS)
LW = {}
for _n, _k in [("ln1_g", 1), ("ln1_b", 1), ("in_w", 512), ("conv_w", 8), ("conv_b", 2), ("xproj", 256),
               ("dtproj", 256), ("A_log", 32), ("D_skip", 256), ("out_w", 256), ("ln2_g", 1), ("ln2_b", 1),
               ("w1", 256), ("b1", 2), ("w2", 256), ("b2", 1)]:
    LW[_n] = (sum(v[1] - v[0] for v in LW.values()), sum(v[1] - v[0] for v in LW.values()) + _k)
LW_ALL = max(v[1] for v in LW.values())


ARENA = 31500


class Count:

    def __init__(self, sem, per=1, credit=0):
        self.sem, self.per, self.credit = sem, per, credit

    def at(self, r, k=None):
        return self.credit + self.per * r + (self.per if k is None else k)


def audio_tower(nc, x_t, tok_w, cols_d, mats_d, rows_d, layers_d, w1_d, w2_d, moe_rows_d, wg_d, ident_d, selcol_d, out):
    with ExitStack() as ctx:
        def sb(name, shape, dt=F32):
            return ctx.enter_context(nc.sbuf_tensor(name, shape, dt))

        def count(name, per=1, credit=0):
            c = Count(ctx.enter_context(nc.semaphore(name)), per, credit)
            if credit:
                credits.append(c)
            return c

        arena = sb("arena", [P, ARENA])

        def stage():
            used = [0]

            def place(_, shape, dtype=F32):
                n = 1
                for k in shape[1:]:
                    n *= k
                words = n if dtype == F32 else (n + 1) // 2
                flat = arena[0:shape[0], used[0]:used[0] + words]
                used[0] += words
                assert used[0] <= ARENA
                if dtype != F32:
                    flat = flat.bitcast(dtype)
                if len(shape) == 2:
                    return flat
                names = "abcd"[:len(shape) - 1]
                return flat.rearrange("p (%s) -> p %s" % (" ".join(names), " ".join(names)),
                                      **dict(zip(names[1:], shape[2:])))
            return place

        credits = []
        ps = ctx.enter_context(nc.psum_tensor("ps", [P, 8, BANK], F32))

        def bank(k):
            return ps[:, k, 0:N]

        def bank4(k):
            return ps[:, k, 0:N].rearrange("p (b t) -> p b t", b=GB)

        cols = sb("cols", [P, len(COLS)])
        mats = sb("mats", [P, len(MATS), P])
        rows = sb("rows", [P, ROW_ALL])
        ident = sb("ident", [P, P])
        mean_w = sb("mean_w", [P, P])
        ones_w = sb("ones_w", [P, P])
        eps_c = sb("eps_c", [P, 1])

        def col(name):
            return cols[:, COL[name]:COL[name] + 1]

        def mat(name, k=1):
            return mats[:, MAT[name]:MAT[name] + k, :].rearrange("p a b -> p (a b)")

        def row(name, n=P):
            return rows[0:n, ROW[name][0]:ROW[name][1]]

        h = sb("h", [P, G, N])
        xs = sb("xs", [P, G, N])

        param = count("param")
        consts = count("consts")

        ln_mean = count("ln_mean")
        ln_cent = count("ln_cent")
        ln_square = count("ln_square")
        ln_var = count("ln_var")
        ln_log = count("ln_log", credit=1)
        ln_rstd = count("ln_rstd")
        cent = sb("cent", [P, N])
        rstd = sb("rstd", [P, N])
        LNB = 0

        ALN = 4

        def attention_norm_pe(pe, g, step):
            if step == 0:
                pe.wait_ge(h_tok.sem, h_tok.at(g))
                nc.tensor.matmul(bank(ALN), mean_w[:], hgroup(g), start=True, stop=True).then_inc(ln_mean.sem, 1)
            else:
                pe.wait_ge(ln_square.sem, ln_square.at(g))
                nc.tensor.matmul(bank(ALN), mean_w[:], rstd[:], start=True, stop=True).then_inc(ln_var.sem, 1)

        def attention_norm_act(act, g, step):
            if step == 0:
                act.wait_ge(ln_cent.sem, ln_cent.at(g))
                nc.scalar.activation(rstd[:], cent[:], ACT.Square).then_inc(ln_square.sem, 1)
            else:
                act.wait_ge(ln_var.sem, ln_var.at(g))
                nc.scalar.activation(rstd[:], bank(ALN), ACT.Ln, bias=eps_c[:]).then_inc(ln_log.sem, 1)
                act.wait_ge(ln_log.sem, ln_log.at(g))
                nc.scalar.activation(rstd[:], rstd[:], ACT.Exp, scale=-0.5).then_inc(ln_rstd.sem, 1)

        NS = 4
        ns_mean = count("ns_mean")
        ns_cent = count("ns_cent")
        ns_square = count("ns_square")
        ns_var = count("ns_var")
        ns_log = count("ns_log", credit=NS)
        ns_rstd = count("ns_rstd")
        ns_out = count("ns_out", credit=NS)

        def norms_pe(pe, r):
            with pe.Fori(0, G // NS) as s:
                for i in range(NS):
                    nc.tensor.matmul(bank(i), mean_w[:], h[:, bass.ds(s * NS + i, 1), :].squeeze(1),
                                     start=True, stop=True).then_inc(ns_mean.sem, 1)
                for i in range(NS):
                    v = s * NS + (r * G + i)
                    pe.wait_ge(ns_square.sem, ns_square.at(v))
                    pe.wait_ge(ns_log.sem, ns_log.at(v - NS))
                    nc.tensor.matmul(bank(NS + i), mean_w[:], rstd4[:, i, :], start=True, stop=True)\
                        .then_inc(ns_var.sem, 1)

        def norms_act(act, r):
            with act.Fori(0, G // NS) as s:
                for i in range(NS):
                    act.wait_ge(ns_cent.sem, ns_cent.at(s * NS + (r * G + i)))
                    nc.scalar.activation(rstd4[:, i, :], cent4[:, i, :], ACT.Square).then_inc(ns_square.sem, 1)
                for i in range(NS):
                    v = s * NS + (r * G + i)
                    act.wait_ge(ns_var.sem, ns_var.at(v))
                    nc.scalar.activation(rstd4[:, i, :], bank(NS + i), ACT.Ln, bias=eps_c[:]).then_inc(ns_log.sem, 1)
                    act.wait_ge(ns_log.sem, ns_log.at(v))
                    nc.scalar.activation(rstd4[:, i, :], rstd4[:, i, :], ACT.Exp, scale=-0.5).then_inc(ns_rstd.sem, 1)

        def norms_dve(dve, r):
            with dve.Fori(0, G // NS) as s:
                for i in range(NS):
                    v = s * NS + (r * G + i)
                    dve.wait_ge(ns_mean.sem, ns_mean.at(v))
                    dve.wait_ge(ns_out.sem, ns_out.at(v - NS))
                    nc.vector.tensor_tensor(cent4[:, i, :], h[:, bass.ds(s * NS + i, 1), :].squeeze(1), bank(i),
                                            ALU.subtract).then_inc(ns_cent.sem, 1)
                for i in range(NS):
                    dve.wait_ge(ns_rstd.sem, ns_rstd.at(s * NS + (r * G + i)))
                    nc.vector.tensor_tensor(xs[:, bass.ds(s * NS + i, 1), :].squeeze(1), cent4[:, i, :],
                                            rstd4[:, i, :], ALU.mult).then_inc(ns_out.sem, 1)

        tok_ws = sb("tok_ws", [FK, P])
        tok_mm = count("tok_mm")
        tok_y = count("tok_y")
        tok_stats = count("tok_stats", G)
        bn = sb("bn", [P, G, 6])
        bn_mv = sb("bn_mv", [P, 2])
        bn_sc = sb("bn_sc", [P, 4])
        bn_step = count("bn_step")
        frames_in = count("frames_in")
        h_tok = count("h_tok")

        att = stage()
        xp = att("xp", [P, GB, T + 2])
        xd = att("xd", [P, GB, TD])
        q_cr, q_d, q_c, k_d, k_c = (att(n, [P, GB, T]) for n in ("q_cr", "q_d", "q_c", "k_d", "k_c"))
        k_cr = att("k_cr", [P, GB, TD])
        v_dc = att("v_dc", [T, GB, 2 * P])
        v_cr = att("v_cr", [TD, GB, P])
        nq = att("nq", [P, 2, N])
        SC = TD + 2 * T
        prob = att("prob", [T, GB, SC])
        probT = att("probT", [T, GB, 3 * T])
        nmax = att("nmax", [T, GB, 3])
        nbias = att("nbias", [T, GB, 3])
        rsum = att("rsum", [T, GB, 3])
        rinv = att("rinv", [T, GB, 3])
        ao = att("ao", [T, GB, 3, P])
        ast = att("ast", [T, GB, 3, 6])
        amv = att("amv", [T, GB * 3, 2])
        ad = att("ad", [T, GB * 3])
        ars = att("ars", [T, GB * 3])
        aoT = att("aoT", [P, 2, 3, T])
        glog = att("glog", [T, GB, 3])
        gmx = att("gmx", [T, GB])
        z = att("z", [T, GB, P])
        rtemp = sb("rtemp", [P, 1])
        BR = [(0, TD), (TD, TD + T), (TD + T, SC)]
        KEYS = [TD, T, T]

        xn_ready = count("xn_ready")
        at_conv = count("at_conv")
        at_xd = count("at_xd")
        at_proj = count("at_proj", 5)
        at_kcr = count("at_kcr")
        at_q_act = count("at_q_act", 5)
        at_kcr_out = count("at_kcr_out")
        at_v = count("at_v", 3)
        at_v_out = count("at_v_out", 3)
        at_sq = count("at_sq", 2)
        at_ss = count("at_ss", 2)
        at_nrm = count("at_nrm", 8)
        at_qkn = count("at_qkn", 2)
        at_score = count("at_score", GB)
        at_max = count("at_max", 4)
        at_bias = count("at_bias", 2)
        at_exp = count("at_exp", GB)
        at_rinv = count("at_rinv")
        at_pt = count("at_pt", GB)
        at_pt_out = count("at_pt_out", GB)
        at_o = count("at_o", GB)
        at_on = count("at_on")
        at_st = count("at_st", 4)
        at_log = count("at_log")
        at_rstd = count("at_rstd")
        at_aff = count("at_aff", 3)
        at_aot = count("at_aot", GB)
        at_aot_out = count("at_aot_out", GB)
        at_logit = count("at_logit", GB)
        at_gate = count("at_gate", 3)
        at_gexp = count("at_gexp")
        at_gn = count("at_gn", 3)
        at_z = count("at_z", 3)
        at_zt = count("at_zt")
        h_attn = count("h_attn", credit=1)
        norm_c = sb("norm_c", [P, 2])
        GATE_B = 6

        def attention_groups(eng, body):
            body(0, None, 1)
            with eng.Fori(1, G - 1) as g:
                body(g, g - 1, g + 1)
            body(G - 1, G - 2, None)
            body(None, G - 1, None)

        def hgroup(g):
            return h[:, g, :] if isinstance(g, int) else h[:, bass.ds(g, 1), :].squeeze(1)

        f_max = count("f_max")
        f_gmax = count("f_gmax")
        f_step = count("f_step")
        f_q = count("f_q", 6)
        f_wq = count("f_wq")
        f_mm = count("f_mm")
        h_ffn = count("h_ffn")
        ffn = stage()
        famax = ffn("famax", [P, G + 1])
        f_wstep = count("f_wstep", 6)
        fpair = ffn("fpair", [P, 2])
        fall = ffn("fall", [P, 2])
        fsc = ffn("fsc", [P, 4])
        wq8 = ffn("wq8", [P, P], BF16)
        wtmp = ffn("wtmp", [P, 3, P])
        ftmp = ffn("ftmp", [P, 2, N])
        xq8 = ffn("xq8", [P, N], BF16)
        cent4 = ffn("cent4", [P, NS, N])
        rstd4 = ffn("rstd4", [P, NS, N])
        C2 = 2 * N
        PRE = ["ln1_g", "ln1_b", "in_w", "conv_w", "conv_b", "xproj", "dtproj"]
        POST = ["D_skip", "out_w", "ln2_g", "ln2_b", "w1", "b1", "w2", "b2"]
        PRE_N = LW["dtproj"][1]
        POST_0 = LW["D_skip"][0]
        wp = sb("wp", [P, PRE_N])
        wo = sb("wo", [P, LW_ALL - POST_0])

        def pw(name, lo=0, n=None):
            a, b = LW[name]
            return wp[:, a + lo:(b if n is None else a + lo + n)]

        def ow(name, lo=0, n=None):
            a, b = LW[name]
            return wo[:, a + lo - POST_0:(b if n is None else a + lo + n) - POST_0]

        nega = sb("nega", [P, LAYERS, 2 * STATES])
        selcol = sb("selcol", [P, 2 * STATES + HEADS + EXPERTS + 1])
        sel = sb("sel", [P, 2 * STATES, P], BF16)
        ssm = stage()
        LAG = 3
        AHEAD = 2
        DB = 4
        dt = ssm("dt", [P, 2, 2, N])
        u = ssm("u", [P, 2, 2, N])
        xc = ssm("xc", [P, 2, 2, N])
        sz = ssm("sz", [P, 2, 2, N])
        bc = ssm("bc", [P, 2, N], BF16)
        dA = ssm("dA", [P, DB, 2, N])
        db = ssm("db", [P, 2, 2, N])
        hs = ssm("hs", [P, DB, 2, N])
        cb = ssm("cb", [P, DB, N])
        gq = ssm("gq", [P, DB, 2, N])
        xn = ssm("xn", [P, N])
        sig_x = ssm("sig_x", [P, 2, N])
        sig_z = ssm("sig_z", [P, 2, N])
        spx = ssm("spx", [P, 2, N])
        drow = ssm("drow", [P, N])
        resid = ssm("resid", [P, N])
        yv = ssm("yv", [P, 2, N])
        xn2 = ssm("xn2", [P, N])
        gl = ssm("gl", [P, 2, N])
        LP, Y, BB, CC, L0 = LNB, 1, 3, 5, 6

        wp_in, wo_in = count("wp_in", 16), count("wo_in", 16)
        a_in = count("a_in", 16)
        sel_in = count("sel_in", 16)
        sel_made = count("sel_made")
        a_neg = count("a_neg", 2)
        p_xn = count("p_xn", 2)
        p_xin = count("p_xin")
        p_conv = count("p_conv", 5)
        p_sx = count("p_sx", 3)
        p_xc = count("p_xc")
        p_z = count("p_z")
        p_zc = count("p_zc")
        p_sz = count("p_sz", 3)
        p_silz = count("p_silz")
        p_xp = count("p_xp")
        p_bc = count("p_bc", 3)
        p_drow = count("p_drow")
        p_dtm = count("p_dtm")
        p_dt_in = count("p_dt_in", 2)
        p_sp = count("p_sp", 2)
        p_dt = count("p_dt")
        p_u = count("p_u")
        s_b = count("s_b", STATES)
        s_c = count("s_c", STATES)
        s_da = count("s_da", STATES)
        s_cb = count("s_cb", STATES, credit=2)
        s_db = count("s_db", STATES, credit=2)
        s_h = count("s_h", STATES, credit=DB)
        s_gq = count("s_gq", STATES, credit=DB)
        s_sum = count("s_sum", STATES, credit=DB)
        s_skip = count("s_skip")
        o_y = count("o_y", 1, credit=1)
        o_out = count("o_out")
        o_x = count("o_x")
        o_xn = count("o_xn", 2)
        o_m1 = count("o_m1")
        o_gl = count("o_gl")
        o_m2 = count("o_m2")
        o_x2 = count("o_x2", 1, credit=1)
        h_mamba = count("h_mamba")
        ROUNDS = LAYERS * G
        LN0 = G

        SLOT = dict(pre_mean=0, pre_cent=0.5, pre_square=1.5, pre_var=1.5, pre_rstd=2.5, pre_xn=2.5, in_x=2.5,
                    conv=(3.5, 4.0, 4.0, 4.5), floor=5.5, sig_x=(6.5, 6.5, 7.5), in_z=5.5, xc=7.0, zclip=6.5,
                    xproj=7.5, drow=8.5, sig_z=(14.5, 14.5, 14.5), split=8.5, dtproj=9.5,
                    softplus=(10.5, 11.5, 11.5), silz=15, dt=12.5, u=13.5, y=3.5, out=4.5, x=4.5, post_mean=5.5,
                    post_cent=5.5, post_square=6.5, post_var=6.5, post_rstd=7.5, post_xn=8.5, mlp1=11.5, gelu=12.5,
                    mlp2=12.5, x2=13.5)

        def mamba_rounds(eng, body, post):
            body(0, 0, LN0 + 1, None)
            with eng.Fori(0, (ROUNDS - 2) // 2) as q:
                j = q * 2 + 1
                body(j, 1, j * 2 + LN0, j * 2 + (LN0 + 1))
                body(j + 1, 0, j * 2 + (LN0 + 2), j * 2 + (LN0 + 3))
            last = ROUNDS - 1
            body(last, last % 2, None, LN0 + 2 * last)
            post(last, last % 2, LN0 + 2 * last + 1)

        wg = sb("wg", [P, EXPERTS])
        OH = 96
        moe_b = sb("moe_b", [OH, HID + P])
        UH = HEADS // 2
        UNITS = 2 * GB
        last = stage()
        w1 = last("w1", [P, EXPERTS, HID])
        w2 = last("w2", [P, EXPERTS, HID // P, P])
        esel = last("esel", [P, EXPERTS, P], BF16)
        xe = last("xe", [P, N])
        qh = last("qh", [P, N])
        qm = last("qm", [P, HEADS, N])
        kh = last("kh", [P, N])
        vh = last("vh", [T, GB, P])
        mp_ = last("mp_", [T, 2, UH, T])
        mpT = last("mpT", [T, 2, UH, T])
        mmax = last("mmax", [T, 2, UH])
        msum = last("msum", [T, GB, HEADS])
        mctx = last("mctx", [T, GB, P])
        ctxT = last("ctxT", [P, N])
        r1 = last("r1", [P, N])
        x1 = last("x1", [P, N])
        lg = last("lg", [T, GB, EXPERTS])
        eq = last("eq", [T, GB, EXPERTS])
        lmx = last("lmx", [T, GB])
        moe_d = last("moe_d", [OH, HID + P])
        moe_b3 = last("moe_b3", [OH, HID + P], BF16)
        eq3 = last("eq3", [T, GB, 3, OH // 3])
        ohb = last("ohb", [P, N], BF16)
        mask = last("mask", [P, EXPERTS, N])
        xm = last("xm", [P, 2, N])
        gh = last("gh", [P, HID // P, N])
        yt = last("yt", [P, 2, N])
        acc = last("acc", [P, N])
        moe_in = count("moe_in", 16)
        moe_w_in = count("moe_w_in", 16)
        m_split = count("m_split", 7)
        m_const = count("m_const")
        m_xe = count("m_xe")
        m_qk = count("m_qk", 3)
        m_qk_out = count("m_qk_out", 3)
        m_qm = count("m_qm")
        m_sc = count("m_sc", UNITS)
        m_mx = count("m_mx", 2 * UNITS)
        m_exp = count("m_exp", UNITS)
        m_ri = count("m_ri")
        m_pt = count("m_pt", UNITS)
        m_pt_out = count("m_pt_out", UNITS)
        m_ctx = count("m_ctx", UNITS)
        m_ctx_n = count("m_ctx_n")
        m_ct = count("m_ct")
        m_ct_out = count("m_ct_out")
        m_sa = count("m_sa")
        m_r1 = count("m_r1")
        m_x1 = count("m_x1", 2)
        m_lg = count("m_lg")
        m_top = count("m_top", 6)
        m_oh = count("m_oh")
        m_oh_out = count("m_oh_out")
        m_mask = count("m_mask", EXPERTS)
        m_mask_out = count("m_mask_out", EXPERTS)
        m_xm = count("m_xm", EXPERTS)
        m_hid_e = count("m_hid_e", EXPERTS - 1)
        m_hid = count("m_hid", HID // P)
        m_gelu = count("m_gelu", HID // P)
        m_b2 = count("m_b2")
        m_y = count("m_y", EXPERTS)
        m_yt = count("m_yt", EXPERTS)
        m_acc = count("m_acc", EXPERTS + 1)
        m_g2 = count("m_g2")
        h_out = count("h_out")
        LE = LN0 + 2 * ROUNDS
        HALF = 2 * EXPERTS
        SLOTS = 2 * HALF
        CTX, HB, MK, QB = LNB, 1, 5, 6
        AT = dict(mean=0, var=1, qkv=3, scores=5, probs=7, context=9, ctx_t=25, sa=26, post_mean=27, post_var=28,
                  logits=29, onehot=31)

        def unit_at(s, what):
            k, rest = divmod(s - AT[what], 2)
            return k if rest == 0 and 0 <= k < UNITS else None

        def tower_end(eng, body):
            body(None, 0, LE)
            with eng.Fori(0, G - 1) as g:
                body(g, g + 1, g * 3 + (LE + 2))
            body(G - 1, None, LE + 3 * G - 1)

        out_done = count("out_done")

        block = ctx.enter_context(nc.Block())

        @block.sync
        def _(sp):
            for c in credits:
                sp.sem_inc(c.sem, c.credit)
            frames = xs[0:FK, :, :].rearrange("p g (b t) -> p (g b) t", b=GB)
            for k in range(CONTEXT):
                sp.dma_start(frames[k * D_IN:(k + 1) * D_IN, :, :], x_t[:, :, k:k + T]).then_inc(frames_in.sem, 16)
            sp.dma_start(tok_ws[:], tok_w).then_inc(frames_in.sem, 16)
            sp.dma_start(cols[:], cols_d).then_inc(frames_in.sem, 16)
            sp.dma_start(mats[:], mats_d).then_inc(param.sem, 16)
            sp.dma_start(ident[:], ident_d).then_inc(param.sem, 16)
            sp.dma_start(rows[:], rows_d.partition_broadcast(P)).then_inc(param.sem, 16)
            sp.dma_start(nega[:], layers_d[:, :, LW["A_log"][0]:LW["A_log"][1]].rearrange("l p c -> p l c"))\
                .then_inc(a_in.sem, 16)
            sp.dma_start(selcol[:], selcol_d).then_inc(sel_in.sem, 16)
            sp.dma_start(wp[:], layers_d[0, :, 0:PRE_N]).then_inc(wp_in.sem, 16)
            sp.dma_start(wo[:], layers_d[0, :, POST_0:LW_ALL]).then_inc(wo_in.sem, 16)
            with sp.Fori(1, LAYERS) as l:
                sp.wait_ge(p_dtm.sem, p_dtm.at(l * G - 1))
                sp.dma_start(wp[:], layers_d[bass.ds(l, 1), :, 0:PRE_N].squeeze(0)).then_inc(wp_in.sem, 16)
                sp.wait_ge(o_x2.sem, o_x2.at(l * G - 1))
                sp.dma_start(wo[:], layers_d[bass.ds(l, 1), :, POST_0:LW_ALL].squeeze(0)).then_inc(wo_in.sem, 16)
            sp.dma_start(wg[:], wg_d).then_inc(moe_in.sem, 16)
            for k in range(0, OH, OH // 3):
                sp.dma_start(moe_b[k:k + EXPERTS, :], moe_rows_d).then_inc(moe_in.sem, 16)
            sp.wait_ge(h_mamba.sem, h_mamba.at(G - 1))
            sp.dma_start(w1[:], w1_d).then_inc(moe_w_in.sem, 16)
            sp.dma_start(w2[:], w2_d).then_inc(moe_w_in.sem, 16)
            with sp.Fori(0, G) as g:
                sp.wait_ge(h_out.sem, h_out.at(g))
                sp.dma_start(out[:, bass.ds(g, 1), :], h[:, bass.ds(g, 1), :]).then_inc(out_done.sem, 16)
            sp.wait_ge(out_done.sem, 16 * G)

        PARAM_ALL = 16 * 3
        FRAMES_ALL = 16 * (CONTEXT + 2)

        @block.tensor
        def _(pe):
            pe.wait_ge(frames_in.sem, FRAMES_ALL)
            with pe.Fori(0, G) as g:
                nc.tensor.matmul(ps[:, g, 0:N], tok_ws[:], xs[0:FK, g, :], start=True, stop=True)\
                    .then_inc(tok_mm.sem, 1)
            pe.wait_ge(consts.sem, 1)
            pe.wait_ge(param.sem, PARAM_ALL)
            pe.wait_ge(tok_y.sem, tok_y.at(G - 1))

            def pe_project(g):
                pe.wait_ge(xn_ready.sem, xn_ready.at(g))
                for k in range(3):
                    mm = nc.tensor.matmul(ps[:, 1, 0:GB * TD], mat(f"dw{k}"), xp[:, :, k:k + 2 * TD - 1:2],
                                          start=(k == 0), stop=(k == 2))
                mm.then_inc(at_conv.sem, 1)
                for bk, w in ((6, "wk_c"), (4, "wq_c"), (2, "wq_cr"), (3, "wq_d"), (5, "wk_d")):
                    nc.tensor.matmul(bank(bk), mat(w), xp[:, :, 1:T + 1], start=True, stop=True)\
                        .then_inc(at_proj.sem, 1)
                for k, i in enumerate((1, 0)):
                    pe.wait_ge(at_sq.sem, at_sq.at(g, k + 1))
                    nc.tensor.matmul(bank((4, 6)[i]), ones_w[:], nq[:, i, :], start=True, stop=True)\
                        .then_inc(at_ss.sem, 1)
                for b in range(GB):
                    mm = nc.tensor.matmul(ps[0:T, (7, 0)[b // 2], 256 * (b % 2):256 * (b % 2) + 256],
                                          xp[:, b, 1:T + 1], mat("wv_d", 2), start=True, stop=True)
                    if b % 2:
                        mm.then_inc(at_v.sem, 1)
                pe.wait_ge(at_xd.sem, at_xd.at(g))
                nc.tensor.matmul(ps[:, 1, 0:GB * TD], mat("wk_cr"), xd[:], start=True, stop=True)\
                    .then_inc(at_kcr.sem, 1)
                pe.wait_ge(at_q_act.sem, at_q_act.at(g))
                for b in range(GB):
                    mm = nc.tensor.matmul(ps[0:TD, 5, P * b:P * b + P], xd[:, b, :], mat("wv_cr"),
                                          start=True, stop=True)
                mm.then_inc(at_v.sem, 1)

            def pe_gate_transposed(g, b):
                if b >= 2:
                    pe.wait_ge(at_aot_out.sem, at_aot_out.at(g, b - 1))
                for i in range(3):
                    mm = nc.tensor.transpose(ps[:, (5, 7)[b % 2], T * i:T * i + T], ao[:, b, i, :],
                                             ident[0:T, 0:T])
                mm.then_inc(at_aot.sem, 1)

            def pe_gate_logits(g, b):
                pe.wait_ge(at_aot_out.sem, at_aot_out.at(g, b + 1))
                for i in range(3):
                    gw = cols[:, COL["gw0"] + 3 * i:COL["gw0"] + 3 * i + 3]
                    mm = nc.tensor.matmul(ps[0:T, GATE_B, 3 * b:3 * b + 3], aoT[:, b % 2, i, :], gw,
                                          start=(i == 0), stop=(i == 2))
                mm.then_inc(at_logit.sem, 1)

            def pe_scores(g):
                pe.wait_ge(at_kcr_out.sem, at_kcr_out.at(g))
                pe.wait_ge(at_qkn.sem, at_qkn.at(g))
                pe.wait_ge(at_v_out.sem, at_v_out.at(g))
                for b in range(GB):
                    for (lo, hi), q, k in zip(BR, (q_cr, q_d, q_c), (k_cr, k_d, k_c)):
                        mm = nc.tensor.matmul(ps[0:T, b, lo:hi], q[:, b, :], k[:, b, :], start=True, stop=True)
                    mm.then_inc(at_score.sem, 1)

            def pe_outputs(g, gn):
                def outputs(b):
                    pe.wait_ge(at_pt_out.sem, at_pt_out.at(g, b + 1))
                    for i in range(3):
                        v = v_cr[:, b, :] if i == 0 else v_dc[:, b, P * (i - 1):P * i]
                        mm = nc.tensor.matmul(ps[0:T, b, P * i:P * i + P], probT[0:KEYS[i], b, T * i:T * i + T], v,
                                              start=True, stop=True)
                    mm.then_inc(at_o.sem, 1)

                for b in range(GB):
                    pe.wait_ge(at_exp.sem, at_exp.at(g, b + 1))
                    for i in (1, 2, 0):
                        lo, hi = BR[i]
                        mm = nc.tensor.transpose(ps[0:KEYS[i], b, T * i:T * i + T], prob[:, b, lo:hi],
                                                 ident[0:T, 0:T])
                    mm.then_inc(at_pt.sem, 1)
                    if b:
                        outputs(b - 1)
                    if b == 1 and gn is not None:
                        attention_norm_pe(pe, gn, 1)
                outputs(GB - 1)

            def pe_mix(g):
                pe.wait_ge(at_z.sem, at_z.at(g))
                for b in range(GB):
                    mm = nc.tensor.transpose(ps[:, GATE_B, T * b:T * b + T], z[:, b, :], ident[0:T, 0:T])
                mm.then_inc(at_zt.sem, 1)

            def pe_attention_groups(ga, gb, gn):
                if ga is not None:
                    if gb is not None:
                        pe.wait_ge(at_on.sem, at_on.at(gb))
                        pe.wait_ge(h_attn.sem, h_attn.at(gb - 1))
                    pe_project(ga)
                if gb is not None:
                    if ga is not None:
                        pe.wait_ge(at_v_out.sem, at_v_out.at(ga))
                        pe.wait_ge(at_nrm.sem, at_nrm.at(ga, 2))
                    pe.wait_ge(at_aff.sem, at_aff.at(gb))
                    pe_gate_transposed(gb, 0)
                    pe_gate_transposed(gb, 1)
                    for b in range(GB):
                        pe_gate_logits(gb, b)
                        if b + 2 < GB:
                            pe_gate_transposed(gb, b + 2)
                if ga is not None:
                    pe_scores(ga)
                    if gn is not None:
                        attention_norm_pe(pe, gn, 0)
                    pe_outputs(ga, gn)
                if gb is not None:
                    pe_mix(gb)

            attention_norm_pe(pe, 0, 0)
            attention_norm_pe(pe, 0, 1)
            attention_groups(pe, pe_attention_groups)

            pe.wait_ge(h_attn.sem, h_attn.at(G - 1))
            norms_pe(pe, 0)
            pe.wait_ge(f_wq.sem, 1)
            with pe.Fori(0, G) as g:
                pe.wait_ge(f_q.sem, f_q.at(g))
                nc.tensor.matmul(ps[:, g, 0:N], wq8[:], xq8[:], start=True, stop=True).then_inc(f_mm.sem, 1)
            pe.wait_ge(h_ffn.sem, h_ffn.at(G - 1))
            norms_pe(pe, 1)

            def pe_norm_mean(uu, src):
                pe.wait_ge(ln_log.sem, ln_log.at(uu - 1))
                nc.tensor.matmul(bank(LNB), mean_w[:], src, start=True, stop=True).then_inc(ln_mean.sem, 1)

            def pe_norm_var(uu):
                pe.wait_ge(ln_square.sem, ln_square.at(uu))
                nc.tensor.matmul(bank(LNB), mean_w[:], rstd[:], start=True, stop=True).then_inc(ln_var.sem, 1)

            def pre_in_x(j, par):
                pe.wait_ge(p_xn.sem, p_xn.at(j))
                pe.wait_ge(wp_in.sem, wp_in.at(j // G))
                for i in range(2):
                    mm = nc.tensor.matmul(bank(L0 + i), pw("in_w", P * i, P), xn[:], start=True, stop=True)
                mm.then_inc(p_xin.sem, 1)

            def pre_in_z(j, par):
                pe.wait_ge(p_conv.sem, p_conv.at(j, 4))
                for i in range(2):
                    mm = nc.tensor.matmul(bank(L0 + i), pw("in_w", P * (2 + i), P), xn[:], start=True, stop=True)
                mm.then_inc(p_z.sem, 1)

            def pre_xproj(j, par):
                pe.wait_ge(p_xc.sem, p_xc.at(j))
                pe.wait_ge(p_zc.sem, p_zc.at(j))
                for i in range(2):
                    mm = nc.tensor.matmul(bank(L0), pw("xproj", P * i, P), xc[:, par, i, :],
                                          start=(i == 0), stop=(i == 1))
                mm.then_inc(p_xp.sem, 1)

            def pre_dtproj(j, par):
                pe.wait_ge(p_drow.sem, p_drow.at(j))
                pe.wait_ge(p_bc.sem, p_bc.at(j))
                for i in range(2):
                    mm = nc.tensor.matmul(bank(L0 + i), pw("dtproj", P * i, P), drow[:], start=True, stop=True)
                mm.then_inc(p_dtm.sem, 1)

            def scan_c(j, par, n):
                par, row = (par, n) if n < STATES else (1 - par, n - STATES)
                pe.wait_ge(s_cb.sem, s_cb.at(j, n))
                nc.tensor.matmul(bank(CC), sel[:, STATES + row, :], bc[:, par, :], start=True, stop=True)\
                    .then_inc(s_c.sem, 1)

            def scan_b(j, par, n):
                if n % STATES == 0:
                    pe.wait_ge(p_bc.sem, p_bc.at(j + n // STATES))
                par, row = (par, n) if n < STATES else (1 - par, n - STATES)
                pe.wait_ge(s_db.sem, s_db.at(j, n - 1))
                nc.tensor.matmul(bank(BB + n % 2), sel[:, row, :], bc[:, par, :], start=True, stop=True)\
                    .then_inc(s_b.sem, 1)

            def scan_sum(j, n):
                pe.wait_ge(s_gq.sem, s_gq.at(j, n + 1))
                if n == 0:
                    pe.wait_ge(o_y.sem, o_y.at(j - 1))
                for i in range(2):
                    mm = nc.tensor.matmul(bank(Y + i), ident[:], gq[:, n % DB, i, :], start=(n == 0), stop=False)
                mm.then_inc(s_sum.sem, 1)

            def scan_skip(j, par):
                pe.wait_ge(wo_in.sem, wo_in.at(j // G))
                for i in range(2):
                    mm = nc.tensor.matmul(bank(Y + i), ow("D_skip", P * i, P), xc[:, par, i, :], start=False, stop=True)
                mm.then_inc(s_skip.sem, 1)

            def post_out(j, uu):
                pe.wait_ge(ln_log.sem, ln_log.at(uu - 1))
                pe.wait_ge(o_y.sem, o_y.at(j))
                for i in range(2):
                    mm = nc.tensor.matmul(bank(LP), ow("out_w", P * i, P), yv[:, i, :], start=(i == 0), stop=(i == 1))
                mm.then_inc(o_out.sem, 1)

            def post_mlp1(j):
                pe.wait_ge(o_xn.sem, o_xn.at(j))
                for i in range(2):
                    mm = nc.tensor.matmul(bank(L0 + i), ow("w1", P * i, P), xn2[:], start=True, stop=True)
                mm.then_inc(o_m1.sem, 1)

            def post_mlp2(j):
                pe.wait_ge(o_gl.sem, o_gl.at(j))
                for i in range(2):
                    mm = nc.tensor.matmul(bank(L0), ow("w2", P * i, P), gl[:, i, :], start=(i == 0), stop=(i == 1))
                mm.then_inc(o_m2.sem, 1)

            def xgroup(j):
                return xs[:, j % G, :] if isinstance(j, int) else xs[:, bass.ds(j % G, 1), :].squeeze(1)

            def pe_round(j, par, u_pre, u_post):
                def beside(at):
                    if u_pre is not None:
                        if at == SLOT["pre_mean"]:
                            pe_norm_mean(u_pre, xgroup(j + 1))
                        if at == SLOT["pre_var"]:
                            pe_norm_var(u_pre)
                        if at == SLOT["in_x"]:
                            if u_post is not None:
                                pe.wait_ge(o_x2.sem, o_x2.at(j - 2))
                            pre_in_x(j + 1, 1 - par)
                        if at == SLOT["in_z"]:
                            pre_in_z(j + 1, 1 - par)
                        if at == SLOT["xproj"]:
                            pre_xproj(j + 1, 1 - par)
                        if at == SLOT["dtproj"]:
                            pre_dtproj(j + 1, 1 - par)
                    if u_post is not None:
                        if at == SLOT["out"]:
                            post_out(j - 1, u_post)
                        if at == SLOT["post_mean"]:
                            pe.wait_ge(o_x.sem, o_x.at(j - 1))
                            pe_norm_mean(u_post, resid[:])
                        if at == SLOT["post_var"]:
                            pe_norm_var(u_post)
                        if at == SLOT["mlp1"]:
                            if u_pre is not None:
                                pe.wait_ge(p_dt_in.sem, p_dt_in.at(j + 1))
                            post_mlp1(j - 1)
                        if at == SLOT["mlp2"]:
                            post_mlp2(j - 1)

                for n in range(STATES):
                    beside(n)
                    if n + 2 < STATES or u_pre is not None:
                        scan_b(j, par, n + 2)
                    if n + 1 < STATES or u_pre is not None:
                        scan_c(j, par, n + 1)
                    if n >= LAG or u_post is not None:
                        scan_sum(j, n - LAG)
                    if n == LAG - 1 and u_post is not None:
                        scan_skip(j - 1, 1 - par)
                    beside(n + 0.5)
                if u_pre is None:
                    for n in range(STATES - LAG, STATES):
                        scan_sum(j, n)
                    scan_skip(j, par)

            def pe_post(j, par, uu):
                post_out(j, uu)
                pe.wait_ge(o_x.sem, o_x.at(j))
                pe_norm_mean(uu, resid[:])
                pe_norm_var(uu)
                post_mlp1(j)
                post_mlp2(j)

            pe.wait_ge(sel_made.sem, 1)
            pe.wait_ge(ns_out.sem, ns_out.at(2 * G - 1))
            pe_norm_mean(LN0, xgroup(0))
            pe_norm_var(LN0)
            pre_in_x(0, 0)
            pre_in_z(0, 0)
            pre_xproj(0, 0)
            pre_dtproj(0, 0)
            scan_b(0, 0, 0)
            scan_c(0, 0, 0)
            scan_b(0, 0, 1)
            mamba_rounds(pe, pe_round, pe_post)
            pe.wait_ge(moe_in.sem, 64)
            pe.wait_ge(m_const.sem, 1)
            pe.wait_ge(h_mamba.sem, h_mamba.at(G - 1))

            def group_of(g):
                return h[:, g, :] if isinstance(g, int) else h[:, bass.ds(g, 1), :].squeeze(1)

            def pe_attention(g, s, u):
                if s == AT["mean"]:
                    pe_norm_mean(u, group_of(g))
                if s == AT["var"]:
                    pe_norm_var(u)
                if s == AT["qkv"]:
                    pe.wait_ge(m_xe.sem, m_xe.at(g))
                    nc.tensor.matmul(bank(QB), mat("Wq"), xe[:], start=True, stop=True).then_inc(m_qk.sem, 1)
                    nc.tensor.matmul(bank(QB + 1), mat("Wk"), xe[:], start=True, stop=True).then_inc(m_qk.sem, 1)
                    for b in range(GB):
                        mm = nc.tensor.matmul(ps[0:T, CTX, P * b:P * b + P], xe[:, T * b:T * b + T], mat("Wv"),
                                              start=True, stop=True)
                    mm.then_inc(m_qk.sem, 1)
                k = unit_at(s, "context")
                if k is not None:
                    b = k // 2
                    pe.wait_ge(m_pt_out.sem, m_pt_out.at(g, k + 1))
                    for i in range(UH):
                        lo = DH * (UH * (k % 2) + i)
                        mm = nc.tensor.matmul(ps[0:T, CTX, P * b + lo:P * b + lo + DH], mpT[:, k % 2, i, :],
                                              vh[:, b, lo:lo + DH], start=True, stop=True)
                    mm.then_inc(m_ctx.sem, 1)
                k = unit_at(s, "scores")
                if k is not None:
                    b = k // 2
                    if k == 0:
                        pe.wait_ge(m_qk_out.sem, m_qk_out.at(g))
                        pe.wait_ge(m_qm.sem, m_qm.at(g))
                    if k >= 2:
                        pe.wait_ge(m_pt_out.sem, m_pt_out.at(g, k - 1))
                    for i in range(UH):
                        mm = nc.tensor.matmul(ps[0:T, QB + k % 2, T * i:T * i + T],
                                              qm[:, UH * (k % 2) + i, T * b:T * b + T], kh[:, T * b:T * b + T],
                                              start=True, stop=True)
                    mm.then_inc(m_sc.sem, 1)
                k = unit_at(s, "probs")
                if k is not None:
                    pe.wait_ge(m_exp.sem, m_exp.at(g, k + 1))
                    for i in range(UH):
                        mm = nc.tensor.transpose(ps[0:T, QB + k % 2, T * i:T * i + T], mp_[:, k % 2, i, :],
                                                 ident[0:T, 0:T])
                    mm.then_inc(m_pt.sem, 1)
                if s == AT["ctx_t"]:
                    pe.wait_ge(m_ctx_n.sem, m_ctx_n.at(g))
                    for b in range(GB):
                        mm = nc.tensor.transpose(ps[:, QB, T * b:T * b + T], mctx[:, b, :], ident[0:T, 0:T])
                    mm.then_inc(m_ct.sem, 1)
                if s == AT["sa"]:
                    pe.wait_ge(m_ct_out.sem, m_ct_out.at(g))
                    nc.tensor.matmul(bank(QB + 1), mat("Wo"), ctxT[:], start=True, stop=True).then_inc(m_sa.sem, 1)
                if s == AT["post_mean"]:
                    pe.wait_ge(m_r1.sem, m_r1.at(g))
                    pe_norm_mean(u + 1, r1[:])
                if s == AT["post_var"]:
                    pe_norm_var(u + 1)
                if s == AT["logits"]:
                    pe.wait_ge(m_x1.sem, m_x1.at(g))
                    for b in range(GB):
                        mm = nc.tensor.matmul(ps[0:T, QB, EXPERTS * b:EXPERTS * b + EXPERTS], x1[:, T * b:T * b + T],
                                              wg[:], start=True, stop=True)
                    mm.then_inc(m_lg.sem, 1)
                if s == AT["onehot"]:
                    pe.wait_ge(m_top.sem, m_top.at(g))
                    for b in range(GB):
                        mm = nc.tensor.matmul(ps[0:OH, QB + 1, T * b:T * b + T],
                                              eq3[:, b, :, :].rearrange("p k e -> p (k e)"), ident[0:T, 0:T],
                                              start=True, stop=True)
                    mm.then_inc(m_oh.sem, 1)

            def expert_mask(g, e):
                if e == 0:
                    pe.wait_ge(m_oh_out.sem, m_oh_out.at(g))
                else:
                    pe.wait_ge(m_mask_out.sem, m_mask_out.at(g, e))
                nc.tensor.matmul(bank(MK), esel[:, e, :], ohb[:], start=True, stop=True).then_inc(m_mask.sem, 1)

            def pe_experts(g, s):
                e, half = (s % HALF) // 2, s % 2
                cs = range(half * HID // P // 2, (half + 1) * HID // P // 2)
                if s < HALF:
                    if half == 0:
                        pe.wait_ge(m_xm.sem, m_xm.at(g, e + 1))
                    for c in cs:
                        mm = nc.tensor.matmul(bank(HB + c), w1[:, e, P * c:P * c + P], xm[:, e % 2, :], start=False,
                                              stop=(e == EXPERTS - 1))
                        if e == EXPERTS - 1:
                            mm.then_inc(m_hid.sem, 1)
                    if half == 1 and e < EXPERTS - 1:
                        mm.then_inc(m_hid_e.sem, 1)
                        if e + 2 < EXPERTS:
                            expert_mask(g, e + 2)
                    if s == HALF - 1:
                        pe.wait_ge(m_mask_out.sem, m_mask_out.at(g))
                        nc.tensor.matmul(bank(MK), moe_b3[:, HID:HID + P], ohb[0:OH, :], start=True, stop=True)\
                            .then_inc(m_b2.sem, 1)
                else:
                    if half == 0 and e >= 2:
                        pe.wait_ge(m_yt.sem, m_yt.at(g, e - 1))
                    for c in cs:
                        if e == 0:
                            pe.wait_ge(m_gelu.sem, m_gelu.at(g, c + 1))
                        mm = nc.tensor.matmul(bank(HB + e % 2), w2[:, e, c, :], gh[:, c, :],
                                              start=(c == 0), stop=(c == HID // P - 1))
                    if half == 1:
                        mm.then_inc(m_y.sem, 1)

            def pe_end(ge, ga, u):
                for s in range(SLOTS):
                    if ge is not None:
                        pe_experts(ge, s)
                    if ga is not None:
                        pe_attention(ga, s, u)
                uf = u if ga is None else u + 2
                if ga is not None:
                    expert_mask(ga, 0)
                if ge is not None:
                    pe.wait_ge(m_acc.sem, m_acc.at(ge))
                    pe_norm_mean(uf, acc[:])
                if ge is None:
                    pe.wait_ge(moe_w_in.sem, 32)
                    pe.wait_ge(m_split.sem, m_split.at(0))
                if ga is not None:
                    for c in range(HID // P):
                        nc.tensor.matmul(bank(HB + c), moe_b3[:, P * c:P * c + P], ohb[0:OH, :], start=True, stop=False)
                    expert_mask(ga, 1)
                if ge is not None:
                    pe_norm_var(uf)

            tower_end(pe, pe_end)

        @block.scalar
        def _(act):
            act.wait_ge(consts.sem, 1)
            nc.scalar.preload_act_table_set("natural_log_exp_and_others")
            act.wait_ge(bn_step.sem, 1)
            nc.scalar.activation(bn_sc[:, 0:1], bn_mv[:, 1:2], ACT.Ln, bias=eps_c[:]).then_inc(bn_step.sem, 1)
            act.wait_ge(bn_step.sem, 2)
            nc.scalar.activation(bn_sc[:, 1:2], bn_sc[:, 0:1], ACT.Exp, scale=-0.5).then_inc(bn_step.sem, 1)

            act.wait_ge(param.sem, PARAM_ALL)
            def act_project(g):
                for k, (dst, bk, b) in enumerate(((k_c, 6, "bk_c"), (q_c, 4, "bq_c"), (q_cr, 2, "bq_cr"),
                                                  (q_d, 3, "bq_d"), (k_d, 5, "bk_d"))):
                    act.wait_ge(at_proj.sem, at_proj.at(g, k + 1))
                    nc.scalar.activation(dst[:], bank4(bk), ACT.Identity, bias=col(b)).then_inc(at_q_act.sem, 1)
                    if k < 2:
                        act.wait_ge(at_q_act.sem, at_q_act.at(g, k + 1))
                        nc.scalar.activation(nq[:, 1 - k, :], dst[:].rearrange("p b t -> p (b t)"), ACT.Square)\
                            .then_inc(at_sq.sem, 1)

            def act_values(g):
                for i in range(2):
                    act.wait_ge(at_v.sem, at_v.at(g, i + 1))
                    nc.scalar.copy(v_dc[:, 2 * i:2 * i + 2, :].rearrange("p b c -> p (b c)"), ps[0:T, (7, 0)[i], :])\
                        .then_inc(at_v_out.sem, 1)
                act.wait_ge(at_v.sem, at_v.at(g, 3))
                nc.scalar.copy(v_cr[:].rearrange("p b c -> p (b c)"), ps[0:TD, 5, :]).then_inc(at_v_out.sem, 1)

            def act_norms(g, steps):
                for step in steps:
                    for k, i in enumerate((1, 0)):
                        if step == 0:
                            act.wait_ge(at_ss.sem, at_ss.at(g, k + 1))
                        else:
                            act.wait_ge(at_nrm.sem, at_nrm.at(g, 2 * step - 1 + k))
                        src = bank((4, 6)[i]) if step == 0 else nq[:, i, :]
                        if step % 2 == 0:
                            a = nc.scalar.activation(nq[:, i, :], src, ACT.Ln, bias=norm_c[:, step // 2:step // 2 + 1])
                        else:
                            a = nc.scalar.activation(nq[:, i, :], src, ACT.Exp, scale=(0.5, -1.0)[step // 2])
                        a.then_inc(at_nrm.sem, 1)

            def act_exponents(g, gn):
                for b in range(GB):
                    act.wait_ge(at_bias.sem, at_bias.at(g, b // 2 + 1))
                    for i, (lo, hi) in enumerate(BR):
                        a = nc.scalar.activation(prob[:, b, lo:hi], ps[0:T, b, lo:hi], ACT.Exp,
                                                 bias=nbias[:, b, i:i + 1], scale=(P ** -0.5, P ** -0.5, 1.0)[i],
                                                 accum_out=rsum[:, b, i:i + 1])
                    a.then_inc(at_exp.sem, 1)
                if gn is not None:
                    attention_norm_act(act, gn, 0)
                for b in range(GB):
                    if b == 2 and gn is not None:
                        attention_norm_act(act, gn, 1)
                    act.wait_ge(at_pt.sem, at_pt.at(g, b + 1))
                    nc.scalar.copy(probT[0:TD, b, 0:T], ps[0:TD, b, 0:T])
                    nc.scalar.copy(probT[:, b, T:3 * T], ps[0:T, b, T:3 * T]).then_inc(at_pt_out.sem, 1)

            def act_branch_rstd(g):
                act.wait_ge(at_st.sem, at_st.at(g))
                nc.scalar.activation(ars[:], amv[:, :, 1], ACT.Ln, bias=eps_c[0:T, :]).then_inc(at_log.sem, 1)
                act.wait_ge(at_log.sem, at_log.at(g))
                nc.scalar.activation(ars[:], ars[:], ACT.Exp, scale=-0.5).then_inc(at_rstd.sem, 1)

            def act_gate_inputs(g, bs):
                for b in bs:
                    act.wait_ge(at_aot.sem, at_aot.at(g, b + 1))
                    if b >= 2:
                        act.wait_ge(at_logit.sem, at_logit.at(g, b - 1))
                    nc.scalar.copy(aoT[:, b % 2, :, :].rearrange("p i t -> p (i t)"), ps[:, (5, 7)[b % 2], 0:3 * T])\
                        .then_inc(at_aot_out.sem, 1)

            def act_gates(g):
                act.wait_ge(at_gate.sem, at_gate.at(g))
                nc.scalar.activation(glog[:], glog[:], ACT.Exp).then_inc(at_gexp.sem, 1)

            attention_norm_act(act, 0, 0)
            attention_norm_act(act, 0, 1)

            def act_attention_groups(ga, gb, gn):
                if gb is not None:
                    act_branch_rstd(gb)
                if ga is not None:
                    act_project(ga)
                    act_norms(ga, (0, 1))
                    act_values(ga)
                if gb is not None:
                    act_gate_inputs(gb, (0, 1))
                if ga is not None:
                    act_norms(ga, (2,))
                if gb is not None:
                    act_gate_inputs(gb, (2, 3))
                if ga is not None:
                    act_norms(ga, (3,))
                if gb is not None:
                    act_gates(gb)
                if ga is not None:
                    act_exponents(ga, gn)

            attention_groups(act, act_attention_groups)

            norms_act(act, 0)
            act.wait_ge(a_in.sem, 16)
            nc.scalar.activation(nega[:], nega[:], ACT.Exp).then_inc(a_neg.sem, 1)
            norms_act(act, 1)

            def act_norm_square(uu):
                act.wait_ge(ln_cent.sem, ln_cent.at(uu))
                nc.scalar.activation(rstd[:], cent[:], ACT.Square).then_inc(ln_square.sem, 1)

            def act_norm_rstd(uu):
                act.wait_ge(ln_var.sem, ln_var.at(uu))
                nc.scalar.activation(rstd[:], bank(LNB), ACT.Ln, bias=eps_c[:]).then_inc(ln_log.sem, 1)
                act.wait_ge(ln_log.sem, ln_log.at(uu))
                nc.scalar.activation(rstd[:], rstd[:], ACT.Exp, scale=-0.5).then_inc(ln_rstd.sem, 1)

            def pre_conv_start(j, par):
                act.wait_ge(p_xin.sem, p_xin.at(j))
                for i in range(2):
                    a = nc.scalar.activation(xc[:, par, i, :], bank(L0 + i), ACT.Identity,
                                             bias=pw("conv_b", i, 1), scale=pw("conv_w", 4 * i + 3, 1))
                a.then_inc(p_conv.sem, 1)

            def sigmoid(k, src, dst, ready, sig, j):
                if k == 0:
                    act.wait_ge(ready.sem, ready.at(j))
                    nc.scalar.activation(dst, src, ACT.Exp, scale=-1.0).then_inc(sig.sem, 1)
                elif k == 1:
                    act.wait_ge(sig.sem, sig.at(j, 1))
                    nc.scalar.activation(dst, dst, ACT.Ln, bias=1.0).then_inc(sig.sem, 1)
                else:
                    act.wait_ge(sig.sem, sig.at(j, 2))
                    nc.scalar.activation(dst, dst, ACT.Exp, scale=-1.0).then_inc(sig.sem, 1)

            def pre_drow(j, par):
                act.wait_ge(p_xp.sem, p_xp.at(j))
                for lo, hi in ((32, 64), (64, P)):
                    nc.scalar.copy(bc[lo:hi, par, :], ps[lo:hi, L0, 0:N])
                nc.scalar.activation(drow[0:32, :], ps[0:32, L0, 0:N], ACT.Identity,
                                     bias=selcol[0:32, -1:]).then_inc(p_drow.sem, 1)

            def pre_softplus(j, par, k):
                if k == 0:
                    act.wait_ge(p_dtm.sem, p_dtm.at(j))
                    nc.scalar.activation(spx[:], ps[:, L0:L0 + 2, 0:N], ACT.Abs).then_inc(p_dt_in.sem, 1)
                    nc.scalar.activation(dt[:, par, :, :], ps[:, L0:L0 + 2, 0:N], ACT.Relu).then_inc(p_dt_in.sem, 1)
                elif k == 1:
                    act.wait_ge(p_dt_in.sem, p_dt_in.at(j, 1))
                    nc.scalar.activation(spx[:], spx[:], ACT.Exp, scale=-1.0).then_inc(p_sp.sem, 1)
                else:
                    act.wait_ge(p_sp.sem, p_sp.at(j, 1))
                    nc.scalar.activation(spx[:], spx[:], ACT.Ln, bias=1.0).then_inc(p_sp.sem, 1)

            def scan_cb(j, n):
                act.wait_ge(s_c.sem, s_c.at(j, n + 1))
                act.wait_ge(s_gq.sem, s_gq.at(j, n + 1 - DB))
                nc.scalar.copy(cb[:, n % DB, :], bank(CC)).then_inc(s_cb.sem, 1)

            def scan_da(j, par, n):
                if n >= STATES:
                    j, par = j + 1, 1 - par
                if n % STATES == 0:
                    act.wait_ge(p_dt.sem, p_dt.at(j))
                n %= STATES
                act.wait_ge(s_h.sem, s_h.at(j, n + 1 - DB))
                for i in range(2):
                    at = (j // G) * (2 * STATES) + (STATES * i + n)
                    scale = nega[:].rearrange("p l s -> p (l s)")[:, bass.ds(at, 1)]
                    a = nc.scalar.activation(
                        dA[:, n % DB, i, :].rearrange("p (b t) -> p b t", b=GB)[:, :, 1:T],
                        dt[:, par, i, :].rearrange("p (b t) -> p b t", b=GB)[:, :, 1:T], ACT.Exp, scale=scale)
                a.then_inc(s_da.sem, 1)

            def post_gelu(j):
                act.wait_ge(o_m1.sem, o_m1.at(j))
                for i in range(2):
                    a = nc.scalar.activation(gl[:, i, :], bank(L0 + i), ACT.Gelu, bias=ow("b1", i, 1))
                a.then_inc(o_gl.sem, 1)
                nc.scalar.preload_act_table_set("natural_log_exp_and_others")

            def act_round(j, par, u_pre, u_post):
                def beside(at):
                    if u_pre is not None:
                        if at == SLOT["pre_square"]:
                            act_norm_square(u_pre)
                        if at == SLOT["pre_rstd"]:
                            act_norm_rstd(u_pre)
                        if at == SLOT["conv"][0]:
                            if u_post is not None:
                                act.wait_ge(o_y.sem, o_y.at(j - 1))
                            pre_conv_start(j + 1, 1 - par)
                        if at == SLOT["drow"]:
                            pre_drow(j + 1, 1 - par)
                        for k in range(3):
                            if at == SLOT["sig_x"][k]:
                                sigmoid(k, xc[:, 1 - par, :, :], sig_x[:], p_conv, p_sx, j + 1)
                            if at == SLOT["sig_z"][k]:
                                sigmoid(k, sz[:, 1 - par, :, :], sig_z[:], p_zc, p_sz, j + 1)
                            if at == SLOT["softplus"][k]:
                                pre_softplus(j + 1, 1 - par, k)
                    if u_post is not None:
                        if at == SLOT["post_square"]:
                            act_norm_square(u_post)
                        if at == SLOT["post_rstd"]:
                            act_norm_rstd(u_post)
                        if at == SLOT["gelu"]:
                            post_gelu(j - 1)

                for n in range(STATES):
                    beside(n)
                    scan_cb(j, n)
                    if n + AHEAD < STATES or u_pre is not None:
                        scan_da(j, par, n + AHEAD)
                    beside(n + 0.5)

            def act_post(j, par, uu):
                act_norm_square(uu)
                act_norm_rstd(uu)
                post_gelu(j)

            act.wait_ge(a_neg.sem, 2)
            act.wait_ge(sel_in.sem, 16)
            act_norm_square(LN0)
            act_norm_rstd(LN0)
            pre_conv_start(0, 0)
            for k in range(3):
                sigmoid(k, xc[:, 0, :, :], sig_x[:], p_conv, p_sx, 0)
            for k in range(3):
                sigmoid(k, sz[:, 0, :, :], sig_z[:], p_zc, p_sz, 0)
            pre_drow(0, 0)
            for k in range(3):
                pre_softplus(0, 0, k)
            for n in range(AHEAD):
                scan_da(0, 0, n)
            mamba_rounds(act, act_round, act_post)
            act.wait_ge(h_mamba.sem, h_mamba.at(G - 1))

            def act_attention(g, s, u):
                if s == AT["mean"]:
                    act_norm_square(u)
                if s == AT["var"]:
                    act_norm_rstd(u)
                if s == AT["qkv"]:
                    for i, (dst, bias) in enumerate(((qh, "bq"), (kh, "bk"))):
                        act.wait_ge(m_qk.sem, m_qk.at(g, i + 1))
                        nc.scalar.activation(dst[:], bank(QB + i), ACT.Identity, bias=col(bias))\
                            .then_inc(m_qk_out.sem, 1)
                    act.wait_ge(m_qk.sem, m_qk.at(g))
                    nc.scalar.copy(vh[:].rearrange("p b c -> p (b c)"), ps[0:T, CTX, :]).then_inc(m_qk_out.sem, 1)
                k = unit_at(s, "scores")
                if k is not None:
                    act.wait_ge(m_mx.sem, m_mx.at(g, 2 * k + 2))
                    for i in range(UH):
                        hd = UH * (k % 2) + i
                        a = nc.scalar.activation(mp_[:, k % 2, i, :], ps[0:T, QB + k % 2, T * i:T * i + T],
                                                 ACT.Exp, bias=mmax[:, k % 2, i:i + 1], scale=DH ** -0.5,
                                                 accum_out=msum[:, k // 2, hd:hd + 1])
                    a.then_inc(m_exp.sem, 1)
                if s == AT["ctx_t"]:
                    act.wait_ge(m_ct.sem, m_ct.at(g))
                    nc.scalar.activation(ctxT[:], bank(QB), ACT.Identity, bias=col("bv")).then_inc(m_ct_out.sem, 1)
                if s == AT["post_mean"]:
                    act_norm_square(u + 1)
                if s == AT["post_var"]:
                    act_norm_rstd(u + 1)
                if s == AT["onehot"]:
                    act.wait_ge(m_oh.sem, m_oh.at(g))
                    nc.scalar.copy(ohb[0:OH, :], ps[0:OH, QB + 1, 0:N]).then_inc(m_oh_out.sem, 1)

            def mask_copy(g, e):
                act.wait_ge(m_mask.sem, m_mask.at(g, e + 1))
                nc.scalar.copy(mask[:, e, :], bank(MK)).then_inc(m_mask_out.sem, 1)

            def act_experts(g, s):
                if s % 2 and s < HALF - 4:
                    mask_copy(g, s // 2 + 2)
                if s == HALF - 1:
                    for c in range(HID // P):
                        act.wait_ge(m_hid.sem, m_hid.at(g, c + 1))
                        nc.scalar.activation(gh[:, c, :], bank(HB + c), ACT.Gelu).then_inc(m_gelu.sem, 1)
                    nc.scalar.preload_act_table_set("natural_log_exp_and_others")

            def act_end(ge, ga, u):
                for s in range(SLOTS):
                    if ge is not None:
                        act_experts(ge, s)
                    if ga is not None:
                        act_attention(ga, s, u)
                uf = u if ga is None else u + 2
                if ga is not None:
                    mask_copy(ga, 0)
                if ge is not None:
                    act_norm_square(uf)
                if ga is not None:
                    mask_copy(ga, 1)
                if ge is not None:
                    act_norm_rstd(uf)

            tower_end(act, act_end)

        @block.gpsimd
        def _(pool):
            pool.wait_ge(f_max.sem, G + 2)
            nc.gpsimd.partition_all_reduce(fall[:], fpair[:], P, bass.bass_isa.ReduceOp.max)\
                .then_inc(f_gmax.sem, 1)
            def pre_silz(j, par):
                pool.wait_ge(p_sz.sem, p_sz.at(j))
                nc.gpsimd.tensor_tensor(sz[:, par, :, :], sz[:, par, :, :], sig_z[:], ALU.mult).then_inc(p_silz.sem, 1)

            pre_silz(0, 0)

            def pool_round(j, par, u_pre, u_post):
                for n in range(STATES):
                    pool.wait_ge(s_h.sem, s_h.at(j, n + 1))
                    pool.wait_ge(s_cb.sem, s_cb.at(j, n + 1))
                    pool.wait_ge(s_sum.sem, s_sum.at(j, n + 1 - DB))
                    nc.gpsimd.tensor_tensor(gq[:, n % DB, :, :], hs[:, n % DB, :, :],
                                            cb[:, n % DB:n % DB + 1, :].to_broadcast([P, 2, N]), ALU.mult)\
                        .then_inc(s_gq.sem, 1)
                    if u_pre is not None and n == SLOT["silz"]:
                        pre_silz(j + 1, 1 - par)

            mamba_rounds(pool, pool_round, lambda j, par, uu: None)

        @block.vector
        def _(dve):
            nc.vector.memset(mean_w[:], 1.0 / P)
            nc.vector.memset(ones_w[:], 1.0)
            nc.vector.memset(norm_c[:, 0:1], 1e-36)
            nc.vector.memset(norm_c[:, 1:2], 1e-8)
            nc.vector.memset(xp[:], 0.0)
            nc.vector.memset(moe_b[:], 0.0)
            nc.vector.memset(eps_c[:], EPS).then_inc(consts.sem, 1)
            dve.wait_ge(frames_in.sem, FRAMES_ALL)
            with dve.Fori(0, G) as g:
                dve.wait_ge(tok_mm.sem, tok_mm.at(g))
                nc.vector.tensor_scalar(h[:, g, :], ps[:, g, 0:N], col("tok_b"), 0.0, ALU.add, ALU.max)\
                    .then_inc(tok_y.sem, 1)
                dve.wait_ge(tok_y.sem, tok_y.at(g))
                nc.vector.bn_stats(bn[:, g, :], h[:, g, :]).then_inc(tok_stats.sem, 1)
            dve.wait_ge(tok_stats.sem, G)
            nc.vector.bn_aggr(bn_mv[:], bn[:].rearrange("p g s -> p (g s)")).then_inc(bn_step.sem, 1)
            dve.wait_ge(bn_step.sem, 3)
            nc.vector.tensor_tensor(bn_sc[:, 2:3], bn_sc[:, 1:2], col("tok_gamma"), ALU.mult).then_inc(bn_step.sem, 1)
            dve.wait_ge(bn_step.sem, 4)
            nc.vector.tensor_scalar(bn_sc[:, 3:4], bn_mv[:, 0:1], bn_sc[:, 2:3], None, ALU.mult)\
                .then_inc(bn_step.sem, 1)
            dve.wait_ge(bn_step.sem, 5)
            nc.vector.tensor_tensor(bn_sc[:, 0:1], col("tok_beta"), bn_sc[:, 3:4], ALU.subtract)\
                .then_inc(bn_step.sem, 1)
            dve.wait_ge(bn_step.sem, 6)
            with dve.Fori(0, G) as g:
                nc.vector.tensor_scalar(h[:, g, :], h[:, g, :], bn_sc[:, 2:3], bn_sc[:, 0:1], ALU.mult, ALU.add)\
                    .then_inc(h_tok.sem, 1)

            dve.wait_ge(param.sem, PARAM_ALL)
            nc.vector.tensor_scalar(rtemp[:], row("temp"), 0.01, None, ALU.max).then_inc(bn_step.sem, 1)
            dve.wait_ge(bn_step.sem, 7)
            nc.vector.reciprocal(rtemp[:], rtemp[:]).then_inc(bn_step.sem, 1)
            dve.wait_ge(bn_step.sem, 8)
            def dve_center(g):
                dve.wait_ge(h_tok.sem, h_tok.at(g))
                dve.wait_ge(ln_mean.sem, ln_mean.at(g))
                nc.vector.tensor_tensor(cent[:], hgroup(g), bank(ALN), ALU.subtract).then_inc(ln_cent.sem, 1)

            def dve_normalised(g):
                dve.wait_ge(ln_rstd.sem, ln_rstd.at(g))
                nc.vector.tensor_tensor(xp[:, :, 1:T + 1], cent[:].rearrange("p (b t) -> p b t", b=GB),
                                        rstd[:].rearrange("p (b t) -> p b t", b=GB), ALU.mult)\
                    .then_inc(xn_ready.sem, 1)
                dve.wait_ge(xn_ready.sem, xn_ready.at(g))

            def dve_branch_stats(g):
                for b in range(GB):
                    for i in range(3):
                        a = nc.vector.bn_stats(ast[:, b, i, :], ao[:, b, i, :])
                a.then_inc(at_st.sem, 1)
                dve.wait_ge(at_st.sem, at_st.at(g, 1))
                st = ast[:].rearrange("p b i s -> p (b i) s")
                nc.vector.tensor_tensor(amv[:, :, 0], st[:, :, 1], st[:, :, 4], ALU.add)
                nc.vector.tensor_tensor(amv[:, :, 1], st[:, :, 2], st[:, :, 5], ALU.add)
                nc.vector.tensor_tensor(ad[:], st[:, :, 1], st[:, :, 4], ALU.subtract).then_inc(at_st.sem, 1)
                dve.wait_ge(at_st.sem, at_st.at(g, 2))
                nc.vector.tensor_scalar(amv[:, :, 0], amv[:, :, 0], 0.5, None, ALU.mult)
                nc.vector.scalar_tensor_tensor(ad[:], ad[:], 0.25, ad[:], ALU.mult, ALU.mult).then_inc(at_st.sem, 1)
                dve.wait_ge(at_st.sem, at_st.at(g, 3))
                nc.vector.scalar_tensor_tensor(amv[:, :, 1], amv[:, :, 1], 1.0 / P, ad[:], ALU.mult, ALU.add)\
                    .then_inc(at_st.sem, 1)

            def dve_conv_out(g):
                dve.wait_ge(at_conv.sem, at_conv.at(g))
                nc.vector.tensor_scalar(xd[:], ps[:, 1, 0:GB * TD].rearrange("p (b t) -> p b t", b=GB), col("db"),
                                        None, ALU.add).then_inc(at_xd.sem, 1)

            def dve_project_out(g):
                dve.wait_ge(at_kcr.sem, at_kcr.at(g))
                nc.vector.tensor_scalar(k_cr[:], ps[:, 1, 0:GB * TD].rearrange("p (b t) -> p b t", b=GB),
                                        col("bk_cr"), None, ALU.add).then_inc(at_kcr_out.sem, 1)

            def dve_branch_norm(g):
                dve.wait_ge(at_rstd.sem, at_rstd.at(g))
                for b in range(GB):
                    for i in range(3):
                        k = 3 * b + i
                        a = nc.vector.tensor_scalar(ao[:, b, i, :], ao[:, b, i, :], amv[:, k, 0:1], ars[:, k:k + 1],
                                                    ALU.subtract, ALU.mult)
                a.then_inc(at_aff.sem, 1)
                ao3 = ao[:].rearrange("p b i c -> p b (i c)")
                dve.wait_ge(at_aff.sem, at_aff.at(g, 1))
                nc.vector.tensor_tensor(ao3, ao3, row("ln_g", T).unsqueeze(1).to_broadcast([T, GB, 3 * P]), ALU.mult)\
                    .then_inc(at_aff.sem, 1)
                dve.wait_ge(at_aff.sem, at_aff.at(g, 2))
                nc.vector.tensor_tensor(ao3, ao3, row("ln_b", T).unsqueeze(1).to_broadcast([T, GB, 3 * P]), ALU.add)\
                    .then_inc(at_aff.sem, 1)

            def dve_normalise_qk(g):
                dve.wait_ge(at_nrm.sem, at_nrm.at(g))
                nc.vector.scalar_tensor_tensor(q_c[:].rearrange("p b t -> p (b t)"),
                                               q_c[:].rearrange("p b t -> p (b t)"), rtemp[:], nq[:, 0, :],
                                               ALU.mult, ALU.mult).then_inc(at_qkn.sem, 1)
                nc.vector.tensor_tensor(k_c[:].rearrange("p b t -> p (b t)"), k_c[:].rearrange("p b t -> p (b t)"),
                                        nq[:, 1, :], ALU.mult).then_inc(at_qkn.sem, 1)

            def dve_maxima(g):
                for p in range(2):
                    b0, b1 = 2 * p, 2 * p + 2
                    dve.wait_ge(at_score.sem, at_score.at(g, b1))
                    nc.vector.tensor_reduce(nmax[:, b0:b1, 0:1].squeeze(2), ps[0:T, b0:b1, 0:TD], AX.X, ALU.max,
                                            negate=True).then_inc(at_max.sem, 1)
                    nc.vector.tensor_reduce(nmax[:, b0:b1, 1:3],
                                            ps[0:T, b0:b1, TD:SC].rearrange("p b (i s) -> p b i s", i=2),
                                            AX.X, ALU.max, negate=True).then_inc(at_max.sem, 1)
                    dve.wait_ge(at_max.sem, at_max.at(g, b1))
                    nc.vector.tensor_tensor(nbias[:, b0:b1, :], nmax[:, b0:b1, :],
                                            row("scales", T).unsqueeze(1).to_broadcast([T, 2, 3]), ALU.mult)\
                        .then_inc(at_bias.sem, 1)

            def dve_gates(g):
                dve.wait_ge(at_logit.sem, at_logit.at(g))
                nc.vector.tensor_tensor(glog[:], ps[0:T, GATE_B, 0:3 * GB].rearrange("p (b i) -> p b i", b=GB),
                                        row("gb", T).unsqueeze(1).to_broadcast([T, GB, 3]), ALU.add)\
                    .then_inc(at_gate.sem, 1)
                dve.wait_ge(at_gate.sem, at_gate.at(g, 1))
                nc.vector.tensor_reduce(gmx[:], glog[:], AX.X, ALU.max).then_inc(at_gate.sem, 1)
                dve.wait_ge(at_gate.sem, at_gate.at(g, 2))
                nc.vector.tensor_tensor(glog[:], glog[:], gmx[:].unsqueeze(2).to_broadcast([T, GB, 3]), ALU.subtract)\
                    .then_inc(at_gate.sem, 1)

            def dve_mix(g):
                dve.wait_ge(at_gexp.sem, at_gexp.at(g))
                nc.vector.tensor_reduce(gmx[:], glog[:], AX.X, ALU.add).then_inc(at_gn.sem, 1)
                dve.wait_ge(at_gn.sem, at_gn.at(g, 1))
                nc.vector.reciprocal(gmx[:], gmx[:]).then_inc(at_gn.sem, 1)
                dve.wait_ge(at_gn.sem, at_gn.at(g, 2))
                nc.vector.tensor_tensor(glog[:], glog[:], gmx[:].unsqueeze(2).to_broadcast([T, GB, 3]), ALU.mult)\
                    .then_inc(at_gn.sem, 1)
                dve.wait_ge(at_gn.sem, at_gn.at(g))
                for b in range(GB):
                    a = nc.vector.tensor_scalar(z[:, b, :], ao[:, b, 0, :], glog[:, b, 0:1], None, ALU.mult)
                a.then_inc(at_z.sem, 1)
                for i in range(1, 3):
                    dve.wait_ge(at_z.sem, at_z.at(g, i))
                    for b in range(GB):
                        a = nc.vector.scalar_tensor_tensor(z[:, b, :], ao[:, b, i, :], glog[:, b, i:i + 1], z[:, b, :],
                                                           ALU.mult, ALU.add)
                    a.then_inc(at_z.sem, 1)

            def dve_outputs(g):
                dve.wait_ge(at_exp.sem, at_exp.at(g))
                nc.vector.reciprocal(rinv[:], rsum[:]).then_inc(at_rinv.sem, 1)
                dve.wait_ge(at_rinv.sem, at_rinv.at(g))
                for b in range(GB):
                    dve.wait_ge(at_o.sem, at_o.at(g, b + 1))
                    for i in range(3):
                        a = nc.vector.scalar_tensor_tensor(ao[:, b, i, :], ps[0:T, b, P * i:P * i + P],
                                                           rinv[:, b, i:i + 1], row("bv", T)[:, P * i:P * i + P],
                                                           ALU.mult, ALU.add)
                a.then_inc(at_on.sem, 1)
                dve.wait_ge(at_on.sem, at_on.at(g))

            def dve_add_mix(g):
                dve.wait_ge(at_zt.sem, at_zt.at(g))
                nc.vector.tensor_tensor(hgroup(g), hgroup(g), bank(GATE_B), ALU.add).then_inc(h_attn.sem, 1)

            def dve_attention_groups(ga, gb, gn):
                if gb is not None:
                    dve_branch_stats(gb)
                if ga is not None:
                    dve_conv_out(ga)
                if gb is not None:
                    dve_branch_norm(gb)
                if ga is not None:
                    dve_project_out(ga)
                    dve_normalise_qk(ga)
                if gb is not None:
                    dve_gates(gb)
                if ga is not None:
                    dve_maxima(ga)
                if gn is not None:
                    dve_center(gn)
                if gb is not None:
                    dve_mix(gb)
                    dve.wait_ge(at_z.sem, at_z.at(gb))
                if gn is not None:
                    dve_normalised(gn)
                if ga is not None:
                    dve_outputs(ga)
                if gb is not None:
                    dve_add_mix(gb)

            dve_center(0)
            dve_normalised(0)
            attention_groups(dve, dve_attention_groups)

            dve.wait_ge(h_attn.sem, h_attn.at(G - 1))
            norms_dve(dve, 0)
            with dve.Fori(0, G) as g:
                dve.wait_ge(ns_out.sem, ns_out.at(g))
                nc.vector.tensor_reduce(famax[:, bass.ds(g, 1)], xs[:, g, :], AX.X, ALU.max, apply_absolute_value=True)\
                    .then_inc(f_max.sem, 1)
            dve.wait_ge(f_max.sem, G)
            nc.vector.tensor_reduce(fpair[:, 0:1], famax[:, 0:G], AX.X, ALU.max).then_inc(f_max.sem, 1)
            nc.vector.tensor_reduce(fpair[:, 1:2], mat("ffn"), AX.X, ALU.max, apply_absolute_value=True)\
                .then_inc(f_max.sem, 1)
            dve.wait_ge(f_gmax.sem, 1)
            nc.vector.tensor_scalar(fall[:], fall[:], 1e-12, None, ALU.max).then_inc(f_step.sem, 1)
            dve.wait_ge(f_step.sem, 1)
            nc.vector.reciprocal(fpair[:], fall[:]).then_inc(f_step.sem, 1)
            dve.wait_ge(f_step.sem, 2)
            nc.vector.tensor_scalar(fsc[:, 0:2], fpair[:], FP8_MAX, None, ALU.mult).then_inc(f_step.sem, 1)
            dve.wait_ge(f_step.sem, 3)
            nc.vector.reciprocal(fpair[:], fsc[:, 0:2]).then_inc(f_step.sem, 1)
            dve.wait_ge(f_step.sem, 4)
            nc.vector.tensor_tensor(fsc[:, 2:3], fpair[:, 0:1], fpair[:, 1:2], ALU.mult).then_inc(f_step.sem, 1)
            dve.wait_ge(f_step.sem, 5)

            def quantise(dst, src, scale, a, m, sig, r):
                nc.vector.tensor_scalar(a, src, scale, FP8_MAX, ALU.mult, ALU.min).then_inc(sig.sem, 1)
                dve.wait_ge(sig.sem, sig.at(r, 1))
                nc.vector.tensor_scalar(a, a, -FP8_MAX, None, ALU.max).then_inc(sig.sem, 1)
                dve.wait_ge(sig.sem, sig.at(r, 2))
                nc.vector.tensor_scalar(m.bitcast(U32), a.bitcast(U32), 0x7F800000, None, ALU.bitwise_and)\
                    .then_inc(sig.sem, 1)
                dve.wait_ge(sig.sem, sig.at(r, 3))
                nc.vector.tensor_scalar(m, m, 2.0 ** -6, 1.5 * 2.0 ** 20, ALU.max, ALU.mult).then_inc(sig.sem, 1)
                dve.wait_ge(sig.sem, sig.at(r, 4))
                nc.vector.tensor_tensor(a, a, m, ALU.add).then_inc(sig.sem, 1)
                dve.wait_ge(sig.sem, sig.at(r, 5))
                nc.vector.tensor_tensor(dst, a, m, ALU.subtract).then_inc(sig.sem, 1)

            quantise(wq8[:], mat("ffn"), fsc[:, 1:2], wtmp[:, 0, :], wtmp[:, 1, :], f_wstep, 0)
            dve.wait_ge(f_wstep.sem, f_wstep.at(0))
            nc.vector.memset(wtmp[:, 2, :], 0.0).then_inc(f_wq.sem, 1)

            def dequantise(g):
                dve.wait_ge(f_mm.sem, f_mm.at(g))
                nc.vector.scalar_tensor_tensor(h[:, g, :], ps[:, g, 0:N], fsc[:, 2:3], h[:, g, :],
                                               ALU.mult, ALU.add).then_inc(h_ffn.sem, 1)

            with dve.Fori(0, G) as g:
                quantise(xq8[:], xs[:, g, :], fsc[:, 0:1], ftmp[:, 0, :], ftmp[:, 1, :], f_q, g)
                dequantise(g)
            norms_dve(dve, 1)
            dve.wait_ge(ns_out.sem, ns_out.at(2 * G - 1))
            dve.wait_ge(sel_in.sem, 16)
            nc.vector.memset(dA[:], 0.0)
            nc.vector.memset(drow[:], 0.0)
            nc.vector.memset(bc[:], 0.0)
            nc.vector.tensor_copy(sel[:], selcol[:, 0:2 * STATES].unsqueeze(2).to_broadcast([P, 2 * STATES, P]))\
                .then_inc(sel_made.sem, 1)
            dve.wait_ge(a_neg.sem, 1)
            nc.vector.tensor_scalar(nega[:], nega[:], -1.0, None, ALU.mult).then_inc(a_neg.sem, 1)

            def xgroup(j):
                return xs[:, j % G, :] if isinstance(j, int) else xs[:, bass.ds(j % G, 1), :].squeeze(1)

            def dve_norm_center(uu, src):
                dve.wait_ge(ln_mean.sem, ln_mean.at(uu))
                nc.vector.tensor_tensor(cent[:], src, bank(LNB), ALU.subtract).then_inc(ln_cent.sem, 1)

            def dve_norm_out(uu, dst, gamma, beta, sig, j, w_in):
                dve.wait_ge(w_in.sem, w_in.at(j // G))
                dve.wait_ge(ln_rstd.sem, ln_rstd.at(uu))
                nc.vector.scalar_tensor_tensor(cent[:], cent[:], gamma, rstd[:], ALU.mult, ALU.mult)\
                    .then_inc(sig.sem, 1)
                dve.wait_ge(sig.sem, sig.at(j, 1))
                nc.vector.tensor_scalar(dst, cent[:], beta, None, ALU.add).then_inc(sig.sem, 1)
                dve.wait_ge(sig.sem, sig.at(j))

            def pre_conv(j, par, s):
                dve.wait_ge(p_conv.sem, p_conv.at(j, s))
                for i in range(2):
                    dst = xc[:, par, i, :].rearrange("p (b t) -> p b t", b=GB)[:, :, s:T]
                    a = nc.vector.scalar_tensor_tensor(dst, bank4(L0 + i)[:, :, 0:T - s],
                                                       pw("conv_w", 4 * i + 3 - s, 1), dst, ALU.mult, ALU.add)
                a.then_inc(p_conv.sem, 1)

            def pre_floor(j, par):
                dve.wait_ge(p_conv.sem, p_conv.at(j, 4))
                nc.vector.tensor_scalar(xc[:, par, :, :], xc[:, par, :, :], -40.0, None, ALU.max)\
                    .then_inc(p_conv.sem, 1)

            def pre_xc(j, par):
                dve.wait_ge(p_sx.sem, p_sx.at(j))
                nc.vector.tensor_tensor(xc[:, par, :, :], xc[:, par, :, :], sig_x[:], ALU.mult).then_inc(p_xc.sem, 1)

            def pre_zclip(j, par):
                dve.wait_ge(p_z.sem, p_z.at(j))
                nc.vector.tensor_scalar(sz[:, par, :, :], ps[:, L0:L0 + 2, 0:N], -40.0, None, ALU.max)\
                    .then_inc(p_zc.sem, 1)

            def pre_split(j, par):
                dve.wait_ge(p_drow.sem, p_drow.at(j))
                nc.vector.tensor_tensor(spx[64:P, 0, :], ps[64:P, L0, 0:N], bc[64:P, par, :], ALU.subtract)\
                    .then_inc(p_bc.sem, 1)
                dve.wait_ge(p_bc.sem, p_bc.at(j, 1))
                nc.vector.tensor_copy(bc[64:P, par, :], spx[64:P, 0, :]).then_inc(p_bc.sem, 1)
                dve.wait_ge(p_bc.sem, p_bc.at(j, 2))
                nc.vector.tensor_tensor(bc[96:P, par, :], spx[96:P, 0, :], bc[96:P, par, :], ALU.subtract)\
                    .then_inc(p_bc.sem, 1)

            def pre_dt(j, par):
                dve.wait_ge(p_sp.sem, p_sp.at(j))
                nc.vector.tensor_tensor(dt[:, par, :, :], dt[:, par, :, :], spx[:], ALU.add).then_inc(p_dt.sem, 1)

            def pre_u(j, par):
                dve.wait_ge(p_dt.sem, p_dt.at(j))
                nc.vector.tensor_tensor(u[:, par, :, :], dt[:, par, :, :], xc[:, par, :, :], ALU.mult)\
                    .then_inc(p_u.sem, 1)

            def scan_db(j, par, n):
                if n == 0:
                    dve.wait_ge(p_u.sem, p_u.at(j))
                dve.wait_ge(s_h.sem, s_h.at(j, n - 1))
                dve.wait_ge(s_b.sem, s_b.at(j, n + 1))
                nc.vector.tensor_tensor(db[:, n % 2, :, :], u[:, par, :, :],
                                        ps[:, BB + n % 2:BB + n % 2 + 1, 0:N].to_broadcast([P, 2, N]), ALU.mult)\
                    .then_inc(s_db.sem, 1)

            def scan_h(j, n):
                dve.wait_ge(s_db.sem, s_db.at(j, n + 1))
                dve.wait_ge(s_da.sem, s_da.at(j, n + 1))
                dve.wait_ge(s_gq.sem, s_gq.at(j, n + 1 - DB))
                nc.vector.tensor_tensor_scan(hs[:, n % DB, :, :].rearrange("p i t -> p (i t)"),
                                             dA[:, n % DB, :, :].rearrange("p i t -> p (i t)"),
                                             db[:, n % 2, :, :].rearrange("p i t -> p (i t)"),
                                             0.0, ALU.mult, ALU.add).then_inc(s_h.sem, 1)

            def post_y(j, par):
                dve.wait_ge(p_silz.sem, p_silz.at(j))
                dve.wait_ge(s_skip.sem, s_skip.at(j))
                nc.vector.tensor_tensor(yv[:], sz[:, par, :, :], ps[:, Y:Y + 2, 0:N], ALU.mult).then_inc(o_y.sem, 1)

            def post_x(j):
                dve.wait_ge(o_out.sem, o_out.at(j))
                nc.vector.tensor_tensor(resid[:], xgroup(j), bank(LP), ALU.add).then_inc(o_x.sem, 1)

            def post_x2(j):
                dve.wait_ge(o_m2.sem, o_m2.at(j))
                nc.vector.scalar_tensor_tensor(xgroup(j), bank(L0), ow("b2"), resid[:], ALU.add, ALU.add)\
                    .then_inc(o_x2.sem, 1)

            def dve_round(j, par, u_pre, u_post):
                def beside(at):
                    if u_post is not None and at == SLOT["y"]:
                        post_y(j - 1, 1 - par)
                    if u_pre is not None:
                        if at == SLOT["pre_cent"]:
                            dve_norm_center(u_pre, xgroup(j + 1))
                        if at == SLOT["pre_xn"]:
                            dve_norm_out(u_pre, xn[:], pw("ln1_g"), pw("ln1_b"), p_xn, j + 1, wp_in)
                        for s in range(1, 4):
                            if at == SLOT["conv"][s]:
                                pre_conv(j + 1, 1 - par, s)
                        if at == SLOT["floor"]:
                            pre_floor(j + 1, 1 - par)
                        if at == SLOT["zclip"]:
                            pre_zclip(j + 1, 1 - par)
                        if at == SLOT["xc"]:
                            pre_xc(j + 1, 1 - par)
                        if at == SLOT["split"]:
                            pre_split(j + 1, 1 - par)
                        if at == SLOT["dt"]:
                            pre_dt(j + 1, 1 - par)
                        if at == SLOT["u"]:
                            pre_u(j + 1, 1 - par)
                    if u_post is not None:
                        if at == SLOT["x"]:
                            post_x(j - 1)
                        if at == SLOT["post_cent"]:
                            dve_norm_center(u_post, resid[:])
                        if at == SLOT["post_xn"]:
                            dve_norm_out(u_post, xn2[:], ow("ln2_g"), ow("ln2_b"), o_xn, j - 1, wo_in)
                        if at == SLOT["x2"]:
                            post_x2(j - 1)

                for n in range(STATES):
                    if n == 0:
                        scan_db(j, par, 0)
                    if n + 1 < STATES:
                        scan_db(j, par, n + 1)
                    beside(n)
                    scan_h(j, n)
                    beside(n + 0.5)

            def dve_post(j, par, uu):
                post_y(j, par)
                post_x(j)
                dve_norm_center(uu, resid[:])
                dve_norm_out(uu, xn2[:], ow("ln2_g"), ow("ln2_b"), o_xn, j, wo_in)
                post_x2(j)

            dve_norm_center(LN0, xgroup(0))
            dve_norm_out(LN0, xn[:], pw("ln1_g"), pw("ln1_b"), p_xn, 0, wp_in)
            for s in range(1, 4):
                pre_conv(0, 0, s)
            pre_floor(0, 0)
            pre_zclip(0, 0)
            pre_xc(0, 0)
            pre_split(0, 0)
            pre_dt(0, 0)
            pre_u(0, 0)
            mamba_rounds(dve, dve_round, dve_post)
            dve.wait_ge(o_x2.sem, o_x2.at(ROUNDS - 1))
            with dve.Fori(0, G) as g:
                nc.vector.tensor_tensor(h[:, g, :], h[:, g, :], xs[:, g, :], ALU.add).then_inc(h_mamba.sem, 1)
            dve.wait_ge(h_mamba.sem, h_mamba.at(G - 1))
            nc.vector.memset(ohb[:], 0.0)
            nc.vector.memset(eq3[:], 0.0)
            nc.vector.tensor_copy(esel[:], selcol[:, 2 * STATES + HEADS:2 * STATES + HEADS + EXPERTS].unsqueeze(2)
                                  .to_broadcast([P, EXPERTS, P])).then_inc(m_const.sem, 1)
            dve.wait_ge(m_const.sem, 1)
            dve.wait_ge(moe_in.sem, 64)
            nc.vector.tensor_copy(moe_b3[:], moe_b[:]).then_inc(m_split.sem, 1)
            dve.wait_ge(m_split.sem, 1)
            for k in (32, 64):
                nc.vector.tensor_tensor(moe_d[k:k + 32, :], moe_b[k:k + 32, :], moe_b3[k:k + 32, :], ALU.subtract)\
                    .then_inc(m_split.sem, 1)
            dve.wait_ge(m_split.sem, 3)
            for k in (32, 64):
                nc.vector.tensor_copy(moe_b3[k:k + 32, :], moe_d[k:k + 32, :]).then_inc(m_split.sem, 1)
            dve.wait_ge(m_split.sem, 5)
            nc.vector.tensor_tensor(moe_d[64:OH, :], moe_d[64:OH, :], moe_b3[64:OH, :], ALU.subtract)\
                .then_inc(m_split.sem, 1)
            dve.wait_ge(m_split.sem, 6)
            nc.vector.tensor_copy(moe_b3[64:OH, :], moe_d[64:OH, :]).then_inc(m_split.sem, 1)

            def group_of(g):
                return h[:, g, :] if isinstance(g, int) else h[:, bass.ds(g, 1), :].squeeze(1)

            def dve_attention(g, s, u):
                if s == AT["mean"]:
                    dve_norm_center(u, group_of(g))
                if s == AT["var"]:
                    dve.wait_ge(ln_rstd.sem, ln_rstd.at(u))
                    nc.vector.tensor_tensor(xe[:], cent[:], rstd[:], ALU.mult).then_inc(m_xe.sem, 1)
                if s == AT["qkv"]:
                    dve.wait_ge(m_qk_out.sem, m_qk_out.at(g, 1))
                    for hd in range(HEADS):
                        a = nc.vector.tensor_scalar(qm[:, hd, :], qh[:],
                                                    selcol[:, 2 * STATES + hd:2 * STATES + hd + 1], None, ALU.mult)
                    a.then_inc(m_qm.sem, 1)
                k = unit_at(s, "scores")
                if k is not None:
                    dve.wait_ge(m_sc.sem, m_sc.at(g, k + 1))
                    nc.vector.tensor_reduce(mmax[:, k % 2, :],
                                            ps[0:T, QB + k % 2, 0:N].rearrange("p (i s) -> p i s", i=UH),
                                            AX.X, ALU.max, negate=True).then_inc(m_mx.sem, 1)
                    dve.wait_ge(m_mx.sem, m_mx.at(g, 2 * k + 1))
                    nc.vector.tensor_scalar(mmax[:, k % 2, :], mmax[:, k % 2, :], DH ** -0.5, None, ALU.mult)\
                        .then_inc(m_mx.sem, 1)
                k = unit_at(s, "probs")
                if k is not None:
                    dve.wait_ge(m_pt.sem, m_pt.at(g, k + 1))
                    nc.vector.tensor_copy(mpT[:, k % 2, :, :].rearrange("p i t -> p (i t)"), ps[0:T, QB + k % 2, 0:N])\
                        .then_inc(m_pt_out.sem, 1)
                if unit_at(s, "context") == UNITS - 1:
                    dve.wait_ge(m_exp.sem, m_exp.at(g))
                    nc.vector.reciprocal(msum[:], msum[:]).then_inc(m_ri.sem, 1)
                    dve.wait_ge(m_ctx.sem, m_ctx.at(g))
                    dve.wait_ge(m_ri.sem, m_ri.at(g))
                    nc.vector.tensor_tensor(mctx[:].rearrange("p b (h d) -> p (b h) d", h=HEADS),
                                            ps[0:T, CTX, 0:GB * P].rearrange("p (q d) -> p q d", d=DH),
                                            msum[:].rearrange("p b h -> p (b h)").unsqueeze(2)
                                            .to_broadcast([T, GB * HEADS, DH]), ALU.mult).then_inc(m_ctx_n.sem, 1)
                if s == AT["sa"]:
                    dve.wait_ge(m_sa.sem, m_sa.at(g))
                    nc.vector.scalar_tensor_tensor(r1[:], bank(QB + 1), col("bo"), xe[:], ALU.add, ALU.add)\
                        .then_inc(m_r1.sem, 1)
                if s == AT["post_mean"]:
                    dve_norm_center(u + 1, r1[:])
                if s == AT["post_var"]:
                    dve.wait_ge(ln_rstd.sem, ln_rstd.at(u + 1))
                    nc.vector.scalar_tensor_tensor(cent[:], cent[:], col("g1"), rstd[:], ALU.mult, ALU.mult)\
                        .then_inc(m_x1.sem, 1)
                    dve.wait_ge(m_x1.sem, m_x1.at(g, 1))
                    nc.vector.tensor_scalar(x1[:], cent[:], col("beta1"), None, ALU.add).then_inc(m_x1.sem, 1)
                if s == AT["logits"]:
                    dve.wait_ge(m_lg.sem, m_lg.at(g))
                    nc.vector.tensor_tensor(lg[:], ps[0:T, QB, 0:GB * EXPERTS].rearrange("p (b e) -> p b e", b=GB),
                                            row("bg", T).unsqueeze(1).to_broadcast([T, GB, EXPERTS]), ALU.add)\
                        .then_inc(m_top.sem, 1)
                    dve.wait_ge(m_top.sem, m_top.at(g, 1))
                    nc.vector.tensor_reduce(lmx[:], lg[:], AX.X, ALU.max).then_inc(m_top.sem, 1)
                    dve.wait_ge(m_top.sem, m_top.at(g, 2))
                    nc.vector.tensor_tensor(eq[:], lg[:], lmx[:].unsqueeze(2).to_broadcast([T, GB, EXPERTS]),
                                            ALU.is_equal).then_inc(m_top.sem, 1)
                    dve.wait_ge(m_top.sem, m_top.at(g, 3))
                    nc.vector.tensor_tensor(lg[:], eq[:], row("places", T).unsqueeze(1)
                                            .to_broadcast([T, GB, EXPERTS]), ALU.mult).then_inc(m_top.sem, 1)
                    dve.wait_ge(m_top.sem, m_top.at(g, 4))
                    nc.vector.tensor_reduce(lmx[:], lg[:], AX.X, ALU.max).then_inc(m_top.sem, 1)
                    dve.wait_ge(m_top.sem, m_top.at(g, 5))
                    nc.vector.tensor_tensor(eq3[:, :, :, 0:EXPERTS],
                                            lg[:].unsqueeze(2).to_broadcast([T, GB, 3, EXPERTS]),
                                            lmx[:].unsqueeze(2).unsqueeze(3).to_broadcast([T, GB, 3, EXPERTS]),
                                            ALU.is_equal).then_inc(m_top.sem, 1)

            def expert_input(g, e):
                dve.wait_ge(m_mask_out.sem, m_mask_out.at(g, e + 1))
                if e >= 2:
                    dve.wait_ge(m_hid_e.sem, m_hid_e.at(g, e - 1))
                nc.vector.tensor_tensor(xm[:, e % 2, :], x1[:], mask[:, e, :], ALU.mult).then_inc(m_xm.sem, 1)

            def dve_experts(g, s):
                if s % 2 and s < HALF - 4:
                    expert_input(g, s // 2 + 2)
                if s == HALF:
                    dve.wait_ge(m_b2.sem, m_b2.at(g))
                    nc.vector.tensor_tensor(acc[:], x1[:], bank(MK), ALU.add).then_inc(m_acc.sem, 1)
                if s > HALF and s % 2:
                    e = (s - HALF) // 2
                    dve.wait_ge(m_y.sem, m_y.at(g, e + 1))
                    nc.vector.tensor_tensor(yt[:, e % 2, :], mask[:, e, :], bank(HB + e % 2), ALU.mult)\
                        .then_inc(m_yt.sem, 1)
                    dve.wait_ge(m_yt.sem, m_yt.at(g, e + 1))
                    dve.wait_ge(m_acc.sem, m_acc.at(g, e + 1))
                    nc.vector.tensor_tensor(acc[:], acc[:], yt[:, e % 2, :], ALU.add).then_inc(m_acc.sem, 1)

            def dve_end(ge, ga, u):
                for s in range(SLOTS):
                    if ge is not None:
                        dve_experts(ge, s)
                    if ga is not None:
                        dve_attention(ga, s, u)
                uf = u if ga is None else u + 2
                if ge is not None:
                    dve_norm_center(uf, acc[:])
                if ga is not None:
                    expert_input(ga, 0)
                    expert_input(ga, 1)
                if ge is not None:
                    dve.wait_ge(ln_rstd.sem, ln_rstd.at(uf))
                    nc.vector.scalar_tensor_tensor(cent[:], cent[:], col("g2"), rstd[:], ALU.mult, ALU.mult)\
                        .then_inc(m_g2.sem, 1)
                    dve.wait_ge(m_g2.sem, m_g2.at(ge))
                    nc.vector.scalar_tensor_tensor(group_of(ge), cent[:], col("beta2"), group_of(ge),
                                                   ALU.add, ALU.add).then_inc(h_out.sem, 1)
                    dve.wait_ge(h_out.sem, h_out.at(ge))

            tower_end(dve, dve_end)


ORDER = ["x_t", "tok_w", "cols", "mats", "rows", "layers", "w1", "w2", "moe_rows", "wg", "ident", "selcol"]


def kernel(**inputs):
    import numpy as np
    import concourse.bacc as bacc
    from concourse.bass_utils import run_bass_kernel_spmd

    i = {k: np.asarray(v) for k, v in inputs.items()}
    a0, l1, f1 = (lambda n: i["L0_attn_" + n]), (lambda n: i["L1_attn_" + n]), (lambda n: i["L1_ffn_" + n])

    cols = {"tok_b": i["L0_tok_b"], "tok_gamma": i["L0_tok_gamma"], "tok_beta": i["L0_tok_beta"]}
    for n in ("db", "bq_cr", "bk_cr", "bq_d", "bk_d", "bq_c", "bk_c"):
        cols[n] = a0(n)
    for n in ("bq", "bk", "bv", "bo", "g1", "beta1", "g2", "beta2"):
        cols[n] = f1(n)
    gate = a0("gw").reshape(3, 3, P).transpose(1, 0, 2).reshape(9, P)
    for k in range(9):
        cols[f"gw{k}"] = gate[k]
    mats = {f"dw{k}": a0("dw")[:, :, k].T for k in range(3)}
    for n in ("wq_cr", "wk_cr", "wv_cr", "wq_d", "wk_d", "wv_d", "wq_c", "wk_c", "wv_c"):
        mats[n] = a0(n).T
    mats["ffn"] = i["L0_ffn_weight"]
    for n in ("Wq", "Wk", "Wv", "Wo"):
        mats[n] = f1(n)
    f32 = np.float32
    rows = {"bv": np.concatenate([a0("bv_" + n) for n in ("cr", "d", "c")]),
            "ln_g": np.concatenate([a0(f"ln_{n}_g") for n in ("cr", "d", "c")]),
            "ln_b": np.concatenate([a0(f"ln_{n}_b") for n in ("cr", "d", "c")]),
            "gb": a0("gb"), "temp": a0("temp").reshape(1), "bg": f1("bg"),
            "places": np.arange(EXPERTS, 0, -1).astype(f32),
            "scales": np.array([P ** -0.5, P ** -0.5, 1.0], f32)}
    xw = l1("xproj_w").transpose(0, 2, 1).reshape(LAYERS, 2, P, RANK + 2 * STATES)
    xproj = np.zeros((LAYERS, 2, P, P), f32)
    xproj[..., 0:RANK] = xw[..., 0:RANK]
    for q in range(1, 4):
        xproj[..., 32 * q:32 * q + 32] = xw[..., RANK:]
    dtproj = np.zeros((LAYERS, P, 2 * P), f32)
    dtproj[:, 0:RANK] = l1("dtproj_w").transpose(0, 2, 1)
    dtproj[:, RANK] = l1("dtproj_b")

    def halves(w):
        return w.reshape(LAYERS, 2, P, -1).transpose(0, 2, 1, 3).reshape(LAYERS, P, -1)

    skip = np.zeros((LAYERS, 2, P, P), f32)
    skip[:, :, np.arange(P), np.arange(P)] = l1("D_skip").reshape(LAYERS, 2, P)
    skip = skip.reshape(LAYERS, 2 * P, P)
    lw = {"ln1_g": l1("ln1_g")[:, :, None], "ln1_b": l1("ln1_b")[:, :, None], "in_w": l1("in_w").transpose(0, 2, 1),
          "conv_w": halves(l1("conv_w")), "conv_b": halves(l1("conv_b")), "xproj": halves(xproj.reshape(LAYERS, 2 * P, P)),
          "dtproj": dtproj, "A_log": halves(l1("A_log")), "D_skip": halves(skip),
          "out_w": halves(l1("out_w").transpose(0, 2, 1)), "ln2_g": l1("ln2_g")[:, :, None],
          "ln2_b": l1("ln2_b")[:, :, None], "w1": l1("mlp_w1").transpose(0, 2, 1), "b1": halves(l1("mlp_b1")),
          "w2": halves(l1("mlp_w2").transpose(0, 2, 1)), "b2": l1("mlp_b2")[:, :, None]}
    layers = np.concatenate([lw[n] for n in LW], axis=2)
    selcol = np.zeros((P, 2 * STATES + HEADS + EXPERTS + 1), f32)
    for n in range(2 * STATES):
        selcol[[32 + n, 64 + n, 96 + n], n] = 1.0
    for n in range(HEADS):
        selcol[DH * n:DH * n + DH, 2 * STATES + n] = 1.0
    for n in range(EXPERTS):
        selcol[n, 2 * STATES + HEADS + n] = 1.0
    selcol[RANK, -1] = 1.0
    arrays = {
        "x_t": i["x"].transpose(2, 0, 1), "tok_w": i["L0_tok_W"].T,
        "cols": np.stack([cols[n] for n in COLS], axis=1), "mats": np.stack([mats[n] for n in MATS], axis=1),
        "rows": np.concatenate([rows[n] for n, _ in ROWS]), "layers": layers,
        "w1": f1("W1").transpose(1, 0, 2), "w2": f1("W2").reshape(EXPERTS, HID // P, P, P).transpose(2, 0, 1, 3),
        "moe_rows": np.concatenate([f1("b1"), f1("b2")], axis=1), "wg": f1("Wg"),
        "ident": np.eye(P, dtype=f32), "selcol": selcol,
    }
    arrays = {k + "_dram": np.ascontiguousarray(v) for k, v in arrays.items()}
    nc = bacc.Bacc("TRN2", target_bir_lowering=False, num_devices=1)
    aps = {k[:-5]: nc.dram_tensor(k, v.shape, mybir.dt.float32, kind="ExternalInput").ap() for k, v in arrays.items()}
    out = nc.dram_tensor("out_dram", (P, G, N), mybir.dt.float32, kind="ExternalOutput").ap()
    audio_tower(nc, *[aps[n] for n in ORDER], out)
    r = run_bass_kernel_spmd(nc, [arrays], core_ids=[0])
    return np.ascontiguousarray(r.results[0]["out_dram"].reshape(P, B, T).transpose(1, 2, 0))
```
